# Optimizing a Trainium2 kernel written in Bass

```python
import numpy as np
import jax
import jax.numpy as jnp

def _softmax(x, axis=-1):
    return jax.nn.softmax(x, axis=axis)

def _gelu(x):
    return jax.nn.gelu(x, approximate=True)

def _silu(x):
    return jax.nn.silu(x)

def _sigmoid(x):
    return jax.nn.sigmoid(x)

def _layernorm(x, axis=-1, eps=1e-05):
    m = jnp.mean(x, axis=axis, keepdims=True)
    v = jnp.var(x, axis=axis, keepdims=True)
    return (x - m) / jnp.sqrt(v + eps)

def _scatter_add(tgt, idx, src, axis=0):
    return tgt.at[idx].add(src)

def _segment_sum(src, seg, n):
    return jax.ops.segment_sum(src, seg, n)
kernel_name = 'mk_decoder_preln_d2_seqx_r4_c152aa'

def setup_inputs(seed: int=0):
    np.random.seed(seed)
    _w = jnp.asarray

    def _rec_inputs():
        import jax
        import jax.numpy as jnp
        _rk = jax.random.key(seed)
        x = 7.22e-05 + 1 * jax.random.normal(jax.random.fold_in(_rk, 1), (4, 512, 256), jnp.float32)
        _lenS = 512 - jax.random.randint(jax.random.fold_in(_rk, 7), (4,), 0, max(1, 512 // 4) + 1, jnp.int32)
        _lenS2 = 512 - jax.random.randint(jax.random.fold_in(_rk, 8), (4,), 0, max(1, 512 // 4) + 1, jnp.int32)
        _ctx_768P = jax.random.normal(jax.random.fold_in(_rk, 11), (4, 16, 192), jnp.float32)
        _ctx_768c = jax.random.dirichlet(jax.random.fold_in(_rk, 511), 0.3 * jnp.ones((16,), jnp.float32), (4, 512))
        _ctx_768t = jnp.einsum('bsk,bkd->bsd', _ctx_768c, _ctx_768P)
        _ctx_768t = _ctx_768t * jax.lax.rsqrt(jnp.mean(jnp.square(_ctx_768t)) + 1e-12) * 0.953939
        ctx_768 = -0.000191848 + 0.999787 * (_ctx_768t + 0.3 * jax.random.normal(jax.random.fold_in(_rk, 611), (4, 512, 192), jnp.float32))
        return (x, ctx_768)
    x, ctx_768 = _rec_inputs()

    def _L0_attn_setup():
        import jax, jax.numpy as jnp
        import numpy as np
        D_MODEL, HD_DIM, NUM_HEADS = (256, 512, 16)
        HEAD_DIM = HD_DIM // NUM_HEADS
        B, T = (4, 512)
        key = jax.random.key(seed)
        ks = jax.random.split(key, 10)
        s = 0.02
        x = jax.random.normal(ks[0], (B, T, D_MODEL), dtype=jnp.float32)
        conv_w = jax.random.normal(ks[1], (D_MODEL, 1, 4), dtype=jnp.float32) * s
        conv_b = jax.random.normal(ks[2], (D_MODEL,), dtype=jnp.float32) * s
        qk_w = jax.random.normal(ks[3], (HD_DIM, D_MODEL), dtype=jnp.float32) * s
        v_w = jnp.eye(HD_DIM, D_MODEL, dtype=jnp.float32)
        g_w = jax.random.normal(ks[4], (HD_DIM, D_MODEL), dtype=jnp.float32) * s
        g_b = jnp.full((HD_DIM,), 2.0, dtype=jnp.float32)
        o_w = jax.random.normal(ks[5], (D_MODEL, HD_DIM), dtype=jnp.float32) * s
        ln_g = jnp.ones((D_MODEL,), dtype=jnp.float32)
        ln_b = jnp.zeros((D_MODEL,), dtype=jnp.float32)
        idx = jnp.linspace(0.0, 1.0, HEAD_DIM)
        h = jnp.arange(NUM_HEADS, dtype=jnp.float32)[:, None]
        freqs = jnp.where(h > 0, (10.0 ** idx)[None, :] * h, 0.0).astype(jnp.float32)
        gamma = jnp.full((NUM_HEADS, 1, 1), 0.999, dtype=jnp.float32).at[0].set(1.0)
        return {'x': x, 'conv_w': conv_w, 'conv_b': conv_b, 'qk_w': qk_w, 'v_w': v_w, 'g_w': g_w, 'g_b': g_b, 'o_w': o_w, 'ln_g': ln_g, 'ln_b': ln_b, 'freqs': freqs, 'gamma': gamma}
    _L0_attn_all = _L0_attn_setup()
    _L0_attn_in = {k: v for k, v in _L0_attn_all.items() if k in ('conv_w', 'conv_b', 'qk_w', 'v_w', 'g_w', 'g_b', 'o_w', 'ln_g', 'ln_b', 'freqs', 'gamma')}
    del _L0_attn_all

    def _L0_xattn_setup():
        import jax, jax.numpy as jnp
        import numpy as np
        NUM_HEADS = 16
        CLAMP = 10000.0
        key = jax.random.key(seed)
        ks = jax.random.split(key, 8)
        B, Nq, Nkv, Cq, Ckv = (4, 512, 512, 256, 192)
        s_q = 1.0 / np.sqrt(Cq)
        s_kv = 1.0 / np.sqrt(Ckv)
        return {'query': jax.random.normal(ks[0], (B, Nq, Cq), jnp.float32), 'key_value': jax.random.normal(ks[1], (B, Nkv, Ckv), jnp.float32), 'Wq': jax.random.normal(ks[2], (Cq, Cq), jnp.float32) * s_q, 'bq': jnp.zeros((Cq,), jnp.float32), 'Wk': jax.random.normal(ks[3], (Ckv, Cq), jnp.float32) * s_kv, 'bk': jnp.zeros((Cq,), jnp.float32), 'Wv': jax.random.normal(ks[4], (Ckv, Cq), jnp.float32) * s_kv, 'bv': jnp.zeros((Cq,), jnp.float32), 'Wo': jax.random.normal(ks[5], (Cq, Cq), jnp.float32) * s_q, 'bo': jnp.zeros((Cq,), jnp.float32)}
    _L0_xattn_all = _L0_xattn_setup()
    _L0_xattn_in = {k: v for k, v in _L0_xattn_all.items() if k in ('Wq', 'bq', 'Wk', 'bk', 'Wv', 'bv', 'Wo', 'bo')}
    del _L0_xattn_all

    def _L0_ffn_setup():
        import jax, jax.numpy as jnp
        import numpy as np
        B, S, D = (2, 512, 256)
        DFF = 512
        E_FFN = 8
        E_ZERO = 4
        E_TOT = E_FFN + E_ZERO
        TOP_K = 2
        key = jax.random.key(seed)
        k1, k2, k3, k4 = jax.random.split(key, 4)
        x = jax.random.normal(k1, (B, S, D), dtype=jnp.float32)
        gate_w = jax.random.normal(k2, (E_TOT, D), dtype=jnp.float32) * (1.0 / np.sqrt(D))
        expert_bias = jnp.zeros((E_TOT,), dtype=jnp.float32)
        w1 = jax.random.normal(k3, (E_FFN, DFF, D), dtype=jnp.float32) * (1.0 / np.sqrt(D))
        w2 = jax.random.normal(k4, (E_FFN, D, DFF), dtype=jnp.float32) * (1.0 / np.sqrt(DFF))
        return {'x': x, 'gate_w': gate_w, 'expert_bias': expert_bias, 'w1': w1, 'w2': w2}
    _L0_ffn_all = _L0_ffn_setup()
    _L0_ffn_in = {k: v for k, v in _L0_ffn_all.items() if k in ('gate_w', 'expert_bias', 'w1', 'w2')}
    del _L0_ffn_all

    def _L1_attn_setup():
        import jax, jax.numpy as jnp
        import numpy as np
        LOG_HALF = float(np.log(0.5))

        def log_g(x):
            return jnp.where(x >= 0.0, jnp.log(jnp.maximum(x, 0.0) + 0.5), -jax.nn.softplus(-x))
        key = jax.random.key(seed)
        k1, k2, k3, k4 = jax.random.split(key, 4)
        B, T, D, E = (4, 1024, 256, 384)
        x = jax.random.normal(k1, (B, T, D), dtype=jnp.float32)
        W_f = jax.random.normal(k2, (2 * E, D), dtype=jnp.float32) * 0.02
        b_f = jax.random.normal(k3, (2 * E,), dtype=jnp.float32) * 0.02
        W_down = jax.random.normal(k4, (D, E), dtype=jnp.float32) * 0.02
        return {'x': x, 'W_f': W_f, 'b_f': b_f, 'W_down': W_down}
    _L1_attn_all = _L1_attn_setup()
    _L1_attn_in = {k: v for k, v in _L1_attn_all.items() if k in ('W_f', 'b_f', 'W_down')}
    del _L1_attn_all

    def _L1_xattn_setup():
        import jax, jax.numpy as jnp
        import numpy as np
        import math
        E = 256
        EV = 256
        FFN = 1024
        DINO = 192
        B, S, P = (64, 128, 64)

        def bitnet_linear(x, W, b):
            w_scale = jnp.maximum(jnp.mean(jnp.abs(W)), 1e-05)
            qW = jnp.sign(W) * (jnp.abs(W) > 0.5 * w_scale).astype(W.dtype)
            i_scale = jnp.maximum(jnp.max(jnp.abs(x)), 1e-08) / 127.0
            qx = jnp.clip(jnp.round(x / i_scale), -128.0, 127.0)
            out = jnp.einsum('...i,oi->...o', qx, qW) * (w_scale * i_scale)
            return out + b
        key = jax.random.key(seed)
        ks = iter(jax.random.split(key, 32))

        def lin_w(fin, fout):
            return jax.random.normal(next(ks), (fout, fin), jnp.float32) * math.sqrt(2.0 / fin)
        return {'text_embeddings': jax.random.normal(next(ks), (B, S, E), jnp.float32), 'dinov2_features': jax.random.normal(next(ks), (B, P, DINO), jnp.float32), 'W_d2v': lin_w(DINO, EV), 'b_d2v': jnp.zeros((EV,), jnp.float32), 'W_img': lin_w(EV, E), 'b_img': jnp.zeros((E,), jnp.float32), 'W_txt': lin_w(E, E), 'b_txt': jnp.zeros((E,), jnp.float32), 'W_att0': lin_w(E, E // 2), 'b_att0': jnp.zeros((E // 2,), jnp.float32), 'W_att1': lin_w(E, E // 2), 'b_att1': jnp.zeros((E // 2,), jnp.float32), 'W_f1': lin_w(2 * E, FFN), 'b_f1': jnp.zeros((FFN,), jnp.float32), 'W_f2': lin_w(FFN, E), 'b_f2': jnp.zeros((E,), jnp.float32)}
    _L1_xattn_all = _L1_xattn_setup()
    _L1_xattn_in = {k: v for k, v in _L1_xattn_all.items() if k in ('W_d2v', 'b_d2v', 'W_img', 'b_img', 'W_txt', 'b_txt', 'W_att0', 'b_att0', 'W_att1', 'b_att1', 'W_f1', 'b_f1', 'W_f2', 'b_f2')}
    del _L1_xattn_all

    def _L1_ffn_setup():
        import jax, jax.numpy as jnp
        import numpy as np
        D_MODEL = 256
        HIDDEN = 1024
        NUM_EXPERTS = 8
        TOP_K = 2
        key = jax.random.key(seed)
        k_x, k_g, k_in, k_out = jax.random.split(key, 4)
        bound_in = 1.0 / HIDDEN
        bound_out = 1.0 / D_MODEL
        x = jax.random.normal(k_x, (2, 512, D_MODEL), dtype=jnp.float32)
        w_gate = jax.random.uniform(k_g, (NUM_EXPERTS, D_MODEL), dtype=jnp.float32, minval=-D_MODEL ** (-0.5), maxval=D_MODEL ** (-0.5))
        w_in = jax.random.uniform(k_in, (NUM_EXPERTS, HIDDEN, D_MODEL), dtype=jnp.float32, minval=-bound_in, maxval=bound_in)
        w_out = jax.random.uniform(k_out, (NUM_EXPERTS, D_MODEL, HIDDEN), dtype=jnp.float32, minval=-bound_out, maxval=bound_out)
        return {'x': x, 'w_gate': w_gate, 'w_in': w_in, 'w_out': w_out}
    _L1_ffn_all = _L1_ffn_setup()
    _L1_ffn_in = {k: v for k, v in _L1_ffn_all.items() if k in ('w_gate', 'w_in', 'w_out')}
    del _L1_ffn_all
    return {'x': x, 'ctx_768': ctx_768, 'L0_attn_conv_w': _L0_attn_in['conv_w'], 'L0_attn_conv_b': _L0_attn_in['conv_b'], 'L0_attn_qk_w': _L0_attn_in['qk_w'], 'L0_attn_v_w': _L0_attn_in['v_w'], 'L0_attn_g_w': _L0_attn_in['g_w'], 'L0_attn_g_b': _L0_attn_in['g_b'], 'L0_attn_o_w': _L0_attn_in['o_w'], 'L0_attn_ln_g': _L0_attn_in['ln_g'], 'L0_attn_ln_b': _L0_attn_in['ln_b'], 'L0_attn_freqs': _L0_attn_in['freqs'], 'L0_attn_gamma': _L0_attn_in['gamma'], 'L0_xattn_Wq': _L0_xattn_in['Wq'], 'L0_xattn_bq': _L0_xattn_in['bq'], 'L0_xattn_Wk': _L0_xattn_in['Wk'], 'L0_xattn_bk': _L0_xattn_in['bk'], 'L0_xattn_Wv': _L0_xattn_in['Wv'], 'L0_xattn_bv': _L0_xattn_in['bv'], 'L0_xattn_Wo': _L0_xattn_in['Wo'], 'L0_xattn_bo': _L0_xattn_in['bo'], 'L0_ffn_gate_w': _L0_ffn_in['gate_w'], 'L0_ffn_expert_bias': _L0_ffn_in['expert_bias'], 'L0_ffn_w1': _L0_ffn_in['w1'], 'L0_ffn_w2': _L0_ffn_in['w2'], 'L1_attn_W_f': _L1_attn_in['W_f'], 'L1_attn_b_f': _L1_attn_in['b_f'], 'L1_attn_W_down': _L1_attn_in['W_down'], 'L1_xattn_W_d2v': _L1_xattn_in['W_d2v'], 'L1_xattn_b_d2v': _L1_xattn_in['b_d2v'], 'L1_xattn_W_img': _L1_xattn_in['W_img'], 'L1_xattn_b_img': _L1_xattn_in['b_img'], 'L1_xattn_W_txt': _L1_xattn_in['W_txt'], 'L1_xattn_b_txt': _L1_xattn_in['b_txt'], 'L1_xattn_W_att0': _L1_xattn_in['W_att0'], 'L1_xattn_b_att0': _L1_xattn_in['b_att0'], 'L1_xattn_W_att1': _L1_xattn_in['W_att1'], 'L1_xattn_b_att1': _L1_xattn_in['b_att1'], 'L1_xattn_W_f1': _L1_xattn_in['W_f1'], 'L1_xattn_b_f1': _L1_xattn_in['b_f1'], 'L1_xattn_W_f2': _L1_xattn_in['W_f2'], 'L1_xattn_b_f2': _L1_xattn_in['b_f2'], 'L1_ffn_w_gate': _L1_ffn_in['w_gate'], 'L1_ffn_w_in': _L1_ffn_in['w_in'], 'L1_ffn_w_out': _L1_ffn_in['w_out']}

def reference(x, ctx_768, L0_attn_conv_w, L0_attn_conv_b, L0_attn_qk_w, L0_attn_v_w, L0_attn_g_w, L0_attn_g_b, L0_attn_o_w, L0_attn_ln_g, L0_attn_ln_b, L0_attn_freqs, L0_attn_gamma, L0_xattn_Wq, L0_xattn_bq, L0_xattn_Wk, L0_xattn_bk, L0_xattn_Wv, L0_xattn_bv, L0_xattn_Wo, L0_xattn_bo, L0_ffn_gate_w, L0_ffn_expert_bias, L0_ffn_w1, L0_ffn_w2, L1_attn_W_f, L1_attn_b_f, L1_attn_W_down, L1_xattn_W_d2v, L1_xattn_b_d2v, L1_xattn_W_img, L1_xattn_b_img, L1_xattn_W_txt, L1_xattn_b_txt, L1_xattn_W_att0, L1_xattn_b_att0, L1_xattn_W_att1, L1_xattn_b_att1, L1_xattn_W_f1, L1_xattn_b_f1, L1_xattn_W_f2, L1_xattn_b_f2, L1_ffn_w_gate, L1_ffn_w_in, L1_ffn_w_out):
    import jax
    import jax.numpy as jnp

    def _L0_attn_ref(x, conv_w, conv_b, qk_w, v_w, g_w, g_b, o_w, ln_g, ln_b, freqs, gamma):
        import jax, jax.numpy as jnp
        import numpy as np
        D_MODEL, HD_DIM, NUM_HEADS = (256, 512, 16)
        HEAD_DIM = HD_DIM // NUM_HEADS
        B, T = (4, 512)
        Bsz, Tlen, C = x.shape
        H, D = freqs.shape
        xc = jax.lax.conv_general_dilated(x.transpose(0, 2, 1), conv_w, window_strides=(1,), padding=[(3, 0)], feature_group_count=C, dimension_numbers=('NCH', 'OIH', 'NCH'))
        xc = (xc + conv_b[None, :, None]).transpose(0, 2, 1)
        qk = jnp.einsum('btc,ec->bte', xc, qk_w).reshape(Bsz, Tlen, H, D)
        nrm = jnp.maximum(jnp.sqrt(jnp.sum(qk * qk, axis=-1, keepdims=True)), 1e-12)
        q = qk / nrm
        k = q
        v = jnp.einsum('btc,ec->bte', xc, v_w).reshape(Bsz, Tlen, H, D)
        g = jax.nn.sigmoid(jnp.einsum('btc,ec->bte', xc, g_w) + g_b).reshape(Bsz, Tlen, H, D)
        t = jnp.arange(Tlen, dtype=x.dtype)[None, :, None, None]
        angles = t * freqs[None, None]
        k_sh = jnp.concatenate([jnp.zeros_like(k[:, :1]), k[:, :-1]], axis=1)
        state_r = (v * jnp.cos(angles) + v * k_sh) * g
        decay = jnp.power(gamma.reshape(1, 1, H, 1), t)
        mem_r = jnp.cumsum(state_r * decay, axis=1) / (decay + 1e-06)
        out = (mem_r * q).reshape(Bsz, Tlen, H * D)
        out = jnp.einsum('bte,ce->btc', out, o_w)
        mu = jnp.mean(out, axis=-1, keepdims=True)
        var = jnp.mean((out - mu) ** 2, axis=-1, keepdims=True)
        return (out - mu) / jnp.sqrt(var + 1e-05) * ln_g + ln_b

    def _L0_xattn_ref(query, key_value, Wq, bq, Wk, bk, Wv, bv, Wo, bo):
        import jax, jax.numpy as jnp
        import numpy as np
        NUM_HEADS = 16
        CLAMP = 10000.0
        B, Nq, Cq = query.shape
        Nkv = key_value.shape[1]
        H = NUM_HEADS
        D = Cq // H
        scale = D ** (-0.5)
        q = (query @ Wq + bq).reshape(B, Nq, H, D).transpose(0, 2, 1, 3)
        k = (key_value @ Wk + bk).reshape(B, Nkv, H, D).transpose(0, 2, 1, 3)
        v = (key_value @ Wv + bv).reshape(B, Nkv, H, D).transpose(0, 2, 1, 3)
        attn = jnp.einsum('bhqd,bhkd->bhqk', q, k) * scale
        attn = jnp.clip(attn, -CLAMP, CLAMP)
        attn = jax.nn.softmax(attn, axis=-1)
        attn = jnp.where(jnp.any(jnp.isnan(attn)), jnp.asarray(1.0 / Nkv, attn.dtype), attn)
        x = jnp.einsum('bhqk,bhkd->bqhd', attn, v).reshape(B, Nq, Cq)
        return x @ Wo + bo

    def _L0_ffn_ref(x, gate_w, expert_bias, w1, w2):
        import jax, jax.numpy as jnp
        import numpy as np
        B, S, D = (2, 512, 256)
        DFF = 512
        E_FFN = 8
        E_ZERO = 4
        E_TOT = E_FFN + E_ZERO
        TOP_K = 2
        logits = jnp.einsum('btd,ed->bte', x, gate_w) + expert_bias
        topk_logits, topk_idx = jax.lax.top_k(logits, TOP_K)
        topk_w = jax.nn.softmax(topk_logits, axis=-1)
        onehot = jax.nn.one_hot(topk_idx, E_TOT, dtype=x.dtype)
        w = jnp.einsum('btk,btke->bte', topk_w, onehot)
        w_ffn = w[..., :E_FFN]
        w_zero = jnp.sum(w[..., E_FFN:], axis=-1)
        h = jax.nn.silu(jnp.einsum('btd,efd->btef', x, w1))
        y = jnp.einsum('btef,edf->bted', h, w2)
        out = jnp.einsum('bte,bted->btd', w_ffn, y) + w_zero[..., None] * x
        return out

    def _L1_attn_ref(x, W_f, b_f, W_down):
        import jax, jax.numpy as jnp
        import numpy as np
        LOG_HALF = float(np.log(0.5))

        def log_g(x):
            return jnp.where(x >= 0.0, jnp.log(jnp.maximum(x, 0.0) + 0.5), -jax.nn.softplus(-x))
        B, T, D = x.shape
        E = W_down.shape[1]
        kz, h_x = jnp.split(jnp.einsum('btd,ed->bte', x, W_f) + b_f, 2, axis=-1)
        log_z = -jax.nn.softplus(-kz)
        log_coeffs = -jax.nn.softplus(kz)
        log_tilde_h = log_g(h_x)
        log_h0 = jnp.full((B, 1, E), LOG_HALF, dtype=x.dtype)
        log_values = jnp.concatenate([log_h0, log_tilde_h + log_z], axis=1)
        a_star = jnp.concatenate([jnp.zeros((B, 1, E), dtype=x.dtype), jnp.cumsum(log_coeffs, axis=1)], axis=1)
        log_h = a_star + jax.lax.cumlogsumexp(log_values - a_star, axis=1)
        h = jnp.exp(log_h)[:, 1:]
        return jnp.einsum('bte,de->btd', h, W_down)

    def _L1_xattn_ref(text_embeddings, dinov2_features, W_d2v, b_d2v, W_img, b_img, W_txt, b_txt, W_att0, b_att0, W_att1, b_att1, W_f1, b_f1, W_f2, b_f2):
        import jax, jax.numpy as jnp
        import numpy as np
        import math
        E = 256
        EV = 256
        FFN = 1024
        DINO = 192
        B, S, P = (64, 128, 64)

        def bitnet_linear(x, W, b):
            w_scale = jnp.maximum(jnp.mean(jnp.abs(W)), 1e-05)
            qW = jnp.sign(W) * (jnp.abs(W) > 0.5 * w_scale).astype(W.dtype)
            i_scale = jnp.maximum(jnp.max(jnp.abs(x)), 1e-08) / 127.0
            qx = jnp.clip(jnp.round(x / i_scale), -128.0, 127.0)
            out = jnp.einsum('...i,oi->...o', qx, qW) * (w_scale * i_scale)
            return out + b
        b, s, e = text_embeddings.shape
        vis = bitnet_linear(dinov2_features, W_d2v, b_d2v)
        image_embeds = bitnet_linear(vis, W_img, b_img)
        fused = bitnet_linear(text_embeddings, W_txt, b_txt)
        inv_sqrt_e = 1.0 / math.sqrt(e)
        for Wa, ba in ((W_att0, b_att0), (W_att1, b_att1)):
            kv = bitnet_linear(image_embeds, Wa, ba)
            k = jnp.concatenate([kv, kv], axis=-1)
            scores = jnp.einsum('bse,bpe->bsp', fused, k) * inv_sqrt_e
            attn = jax.nn.softmax(scores, axis=-1)
            fused = fused + 0.1 * jnp.einsum('bsp,bpe->bse', attn, k)
        avg_img = jnp.mean(image_embeds, axis=1, keepdims=True)
        concatenated = jnp.concatenate([fused, jnp.broadcast_to(avg_img, (b, s, e))], axis=-1)
        h = jax.nn.relu(bitnet_linear(concatenated, W_f1, b_f1))
        return bitnet_linear(h, W_f2, b_f2)

    def _L1_ffn_ref(x, w_gate, w_in, w_out):
        import jax, jax.numpy as jnp
        import numpy as np
        D_MODEL = 256
        HIDDEN = 1024
        NUM_EXPERTS = 8
        TOP_K = 2
        B, S, D = x.shape
        E = w_in.shape[0]
        xt = x.reshape(-1, D)
        logits = (xt @ w_gate.T).astype(jnp.float32)
        top_logits, top_idx = jax.lax.top_k(logits, TOP_K)
        top_gates = jax.nn.softmax(top_logits, axis=-1).astype(x.dtype)
        gates = (jax.nn.one_hot(top_idx, E, dtype=x.dtype) * top_gates[..., None]).sum(axis=1)
        y = jnp.zeros_like(xt)
        for e in range(E):
            h = xt @ w_in[e].T
            y = y + gates[:, e:e + 1] * (h @ w_out[e].T)
        return y.reshape(B, S, D)
    x = x + _L0_attn_ref(_layernorm(x, axis=-1), L0_attn_conv_w, L0_attn_conv_b, L0_attn_qk_w, L0_attn_v_w, L0_attn_g_w, L0_attn_g_b, L0_attn_o_w, L0_attn_ln_g, L0_attn_ln_b, L0_attn_freqs, L0_attn_gamma)
    x = x + _L0_xattn_ref(_layernorm(x, axis=-1), ctx_768, L0_xattn_Wq, L0_xattn_bq, L0_xattn_Wk, L0_xattn_bk, L0_xattn_Wv, L0_xattn_bv, L0_xattn_Wo, L0_xattn_bo)
    x = x + _L0_ffn_ref(_layernorm(x, axis=-1), L0_ffn_gate_w, L0_ffn_expert_bias, L0_ffn_w1, L0_ffn_w2)
    x = x + _L1_attn_ref(_layernorm(x, axis=-1), L1_attn_W_f, L1_attn_b_f, L1_attn_W_down)
    x = x + _L1_xattn_ref(_layernorm(x, axis=-1), ctx_768, L1_xattn_W_d2v, L1_xattn_b_d2v, L1_xattn_W_img, L1_xattn_b_img, L1_xattn_W_txt, L1_xattn_b_txt, L1_xattn_W_att0, L1_xattn_b_att0, L1_xattn_W_att1, L1_xattn_b_att1, L1_xattn_W_f1, L1_xattn_b_f1, L1_xattn_W_f2, L1_xattn_b_f2)
    x = x + _L1_ffn_ref(_layernorm(x, axis=-1), L1_ffn_w_gate, L1_ffn_w_in, L1_ffn_w_out)
    return x

_drawn_inputs = setup_inputs


def setup_inputs(seed=0):
    import zlib

    import numpy as np

    out = dict(_drawn_inputs(seed))
    spreads = {'L0_attn_g_b': (2.0, 0.2),
     'L0_attn_ln_g': (1.0, 0.2),
     'L0_attn_ln_b': (0.0, 0.1),
     'L0_xattn_bq': (0.0, 0.1),
     'L0_xattn_bk': (0.0, 2.0),
     'L0_xattn_bv': (0.0, 0.1),
     'L0_xattn_bo': (0.0, 0.1),
     'L0_ffn_expert_bias': (0.0, 0.1),
     'L1_xattn_b_d2v': (0.0, 0.395),
     'L1_xattn_b_img': (0.0, 0.32),
     'L1_xattn_b_txt': (0.0, 0.35),
     'L1_xattn_b_att0': (0.0, 2.0),
     'L1_xattn_b_att1': (0.0, 2.0),
     'L1_xattn_b_f1': (0.0, 0.1),
     'L1_xattn_b_f2': (0.0, 0.1)}
    factors = {'L0_attn_g_w': 26.826,
     'L1_attn_b_f': 8.0,
     'L1_xattn_W_att0': 5.638,
     'L1_xattn_W_att1': 5.249,
     'L1_ffn_w_gate': 28.093,
     'L1_ffn_w_in': 24.743,
     'L1_ffn_w_out': 24.867}
    for name, (base, spread) in spreads.items():
        noise = np.random.default_rng([zlib.crc32(name.encode()), seed]).standard_normal(out[name].shape)
        drawn = base * np.exp(spread * noise) if base else spread * noise
        out[name] = jnp.asarray(drawn.astype(out[name].dtype))
    for name, factor in factors.items():
        out[name] = (out[name] * factor).astype(out[name].dtype)
    return out
```

```python
from contextlib import ExitStack

import numpy as np
import concourse.bass as bass
from concourse import mybir

F32 = mybir.dt.float32
BF16 = mybir.dt.bfloat16
ALU = mybir.AluOpType
ACT = mybir.ActivationFunctionType
AX = mybir.AxisListType
RED = bass.bass_isa.ReduceOp

P = 128
B = 4
T = 512
N = B * T
NT = N // P
TB = T // P
D = 256
KD = D // P
E0 = 512
ET = E0 // P
H0 = 16
HX = 16
DX = D // HX
CTX = 192
CK = CTX // 2
NE = 8
NE_ALL = 12
FF0 = 512
FF1 = 1024
EG = 384
GT = EG // P
FX = 1024
CLAMP = 10000.0
MAGIC = 12582912.0
TWO_PI_HI = 6.28125
TWO_PI_MID = 0.0019350051879882812
TWO_PI_LO = 2.0 * np.pi - TWO_PI_HI - TWO_PI_MID
EPS = 1e-5

COLS = {}
_at = 0
for _name, _n in (("conv_w", KD * 4), ("conv_b", KD), ("g_b", ET), ("freqs", ET), ("bq", KD), ("bk", KD),
                  ("bv", KD), ("b_f", 2 * GT), ("b_d2v", KD), ("b_img", KD), ("b_txt", KD), ("b_att0", 1),
                  ("b_att1", 1), ("b_f1", FX // P), ("gamma", 1)):
    COLS[_name] = (_at, _at + _n)
    _at += _n
N_COLS = _at
ROWS = {}
_at = 0
for _name, _n in (("ln_g", D), ("ln_b", D), ("bo", D), ("b_f2", D), ("expert_bias", NE_ALL),
                  ("steps", T), ("expert_index", NE_ALL)):
    ROWS[_name] = (_at, _at + _n)
    _at += _n
N_ROWS = _at


class Core:

    def __init__(self, nc, ctx, dram):
        self.nc, self.ctx, self.dram = nc, ctx, dram
        self.tallies = {}
        self.section_sems = []
        self.saved = nc.alloc_semaphore(name="saved")
        self.bank = ctx.enter_context(nc.psum_tensor("bank", [P, 8, 512], F32))
        self.X = self.sb(ctx, "X", [P, NT, D])
        self.xn = self.sb(ctx, "xn", [P, NT, D])
        self.xn_f = self.sb(ctx, "xn_f", [P, KD, N])
        self.ident = self.sb(ctx, "ident", [P, P])
        self.cols = self.sb(ctx, "cols", [P, N_COLS])
        self.rows = self.sb(ctx, "rows", [P, N_ROWS])
        self.eps = self.sb(ctx, "eps", [P, 1])

    def sb(self, ctx, name, shape, dt=F32):
        return ctx.enter_context(self.nc.sbuf_tensor(name, shape, dt))

    def sem(self, name):
        handle = self.nc.alloc_semaphore(name=name)
        self.section_sems.append(handle)
        return handle

    def end_section(self):
        self.nc.clear_and_free_semaphores(self.section_sems)
        self.section_sems = []
        self.nc.all_engine_barrier()

    def tally(self, name, total):
        if name not in self.tallies:
            self.tallies[name] = [self.nc.alloc_semaphore(name=name), 0]
        sem, before = self.tallies[name]
        self.tallies[name][1] += total
        return sem, before

    def col(self, name, i=0, n=1, p=P):
        a = COLS[name][0] + i
        return self.cols[0:p, a:a + n]

    def row(self, name):
        a, b = ROWS[name]
        return self.rows[:, a:b]


def load_block(c):
    nc = c.nc
    loaded = c.sem("loaded")
    eps_set = c.sem("eps_set")
    with nc.Block() as block:
        @block.sync
        def _(sp):
            sp.dma_start(c.X[:, :, :], c.dram["x"].rearrange("(t p) d -> p t d", p=P)).then_inc(loaded, 16)
            sp.dma_start(c.ident[:, :], c.dram["ident"]).then_inc(loaded, 16)
            sp.dma_start(c.cols[:, :], c.dram["columns"]).then_inc(loaded, 16)
            sp.dma_start(c.rows[:, :], c.dram["rows"]).then_inc(loaded, 16)
            sp.wait_ge(loaded, 64)

        @block.vector
        def _(dve):
            nc.vector.memset(c.eps[:, :], EPS).then_inc(eps_set, 1)


def norm_block(c, tag, put=None):
    nc = c.nc
    if put is None:
        def put(k, b):
            return c.xn_f[:, k, b * T:(b + 1) * T]
    moments_in, moments_in0 = c.tally("norm_moments_in", NT)
    moments, moments0 = c.tally("norm_moments", NT)
    std, std0 = c.tally("norm_std", B)
    rstd, rstd0 = c.tally("norm_rstd", B)
    normed, normed0 = c.tally("norm_normed", NT)
    turned, turned0 = c.tally("norm_turned", KD * B)
    stored, stored0 = c.tally("norm_stored", KD * B)
    with ExitStack() as ctx:
        parts = c.sb(ctx, tag + "_parts", [P, NT, 6])
        mom = c.sb(ctx, tag + "_mom", [P, NT, 2])
        sd = c.sb(ctx, tag + "_sd", [P, NT])
        rs = c.sb(ctx, tag + "_rs", [P, NT])
        with nc.Block() as block:
            @block.vector
            def _(dve):
                def stats(b):
                    for t in range(TB * b, TB * b + TB):
                        nc.vector.bn_stats(parts[:, t, :], c.X[:, t, :]).then_inc(moments_in, 1)
                    for t in range(TB * b, TB * b + TB):
                        dve.wait_ge(moments_in, moments_in0 + t + 1)
                        nc.vector.bn_aggr(mom[:, t, :], parts[:, t, :]).then_inc(moments, 1)

                def scale(b):
                    dve.wait_ge(std, std0 + b + 1)
                    nc.vector.reciprocal(rs[:, TB * b:TB * b + TB], sd[:, TB * b:TB * b + TB]).then_inc(rstd, 1)
                    dve.wait_ge(rstd, rstd0 + b + 1)
                    for t in range(TB * b, TB * b + TB):
                        nc.vector.tensor_scalar(c.xn[:, t, :], c.X[:, t, :], mom[:, t, 0:1], rs[:, t:t + 1],
                                                ALU.subtract, ALU.mult).then_inc(normed, 1)

                stats(0)
                for b in range(B):
                    if b + 1 < B:
                        stats(b + 1)
                    scale(b)

            @block.scalar
            def _(act):
                def root(b):
                    act.wait_ge(moments, moments0 + TB * (b + 1))
                    nc.scalar.activation(sd[:, TB * b:TB * b + TB], mom[:, TB * b:TB * b + TB, 1], ACT.Sqrt,
                                         bias=c.eps[:, 0:1]).then_inc(std, 1)

                root(0)
                for b in range(B):
                    if b + 1 < B:
                        root(b + 1)
                    for k in range(KD):
                        act.wait_ge(turned, turned0 + KD * b + k + 1)
                        src = c.bank[:, KD * b + k, :]
                        if len(put(k, b).shape) == 3:
                            src = src.rearrange("p (a t) -> p a t", a=1)
                        nc.scalar.activation(put(k, b), src, ACT.Copy).then_inc(stored, 1)

            @block.tensor
            def _(pe):
                for b in range(B):
                    pe.wait_ge(normed, normed0 + TB * (b + 1))
                    for k in range(KD):
                        for i in range(TB):
                            tr = nc.tensor.transpose(c.bank[:, KD * b + k, i * P:(i + 1) * P],
                                                     c.xn[:, TB * b + i, k * P:(k + 1) * P], c.ident[:, :])
                        tr.then_inc(turned, 1)


def attention_blocks(c):
    nc, dram = c.nc, c.dram
    with ExitStack() as ctx:
        wo = c.sb(ctx, "a0_wo", [P, ET, D])
        wq = c.sb(ctx, "a0_wq", [P, KD, E0])
        wv = c.sb(ctx, "a0_wv", [P, KD, E0])
        wg = c.sb(ctx, "a0_wg", [P, KD, E0])
        head_in = c.sb(ctx, "a0_head_in", [P, ET, 32])
        head_out = c.sb(ctx, "a0_head_out", [P, ET, P])
        xc = c.sb(ctx, "a0_xc", [P, KD, B, T])
        cos = c.sb(ctx, "a0_cos", [P, ET, T])
        decay = c.sb(ctx, "a0_decay", [P, ET, T])
        undecay = c.sb(ctx, "a0_undecay", [P, ET, T])
        gate = c.sb(ctx, "a0_gate", [P, ET, B, T])
        half_pi = c.sb(ctx, "a0_half_pi", [P, 1])
        with ExitStack() as ctx2:
            xpad = c.sb(ctx2, "a0_xpad", [P, KD, B, 3 + T])
            pad_set = c.sem("a0_pad_set")
            with nc.Block() as block:
                @block.gpsimd
                def _(pool):
                    nc.gpsimd.memset(xpad[:, :, :, 0:3], 0.0).then_inc(pad_set, 1)
            norm_block(c, "n0", lambda k, b: xpad[:, k, b:b + 1, 3:3 + T])

            weights = c.sem("a0_weights")
            conv_sem = c.sem("a0_conv")
            angle_sem = c.sem("a0_angle")
            abs_sem = c.sem("a0_angle_abs")
            cos_sem = c.sem("a0_cos_ready")
            decay_rows = c.sem("a0_decay_rows")
            spread = c.sem("a0_spread")
            spread_used = c.sem("a0_spread_used")
            ang = c.sb(ctx2, "a0_ang", [P, ET, T])
            turns = c.sb(ctx2, "a0_turns", [P, ET, T])
            gam = c.sb(ctx2, "a0_gam", [32, T])
            dec = c.sb(ctx2, "a0_dec", [32, 2, T])
            dece = c.sb(ctx2, "a0_dece", [32, T])
            zero = c.sb(ctx2, "a0_zero", [32, T])
            with nc.Block() as block:
                @block.sync
                def _(sp):
                    for dst, name in ((wq, "a0_wq"), (wv, "a0_wv"), (wg, "a0_wg"), (wo, "a0_wo"),
                                      (head_in, "head_in"), (head_out, "head_out")):
                        sp.dma_start(dst[:, :, :], dram[name]).then_inc(weights, 16)
                    sp.wait_ge(weights, 96)

                @block.vector
                def _(dve):
                    nc.vector.memset(zero[:, :], 0.0).then_inc(decay_rows, 1)
                    nc.vector.memset(dec[:, 0, 0:1], 1.0).then_inc(decay_rows, 1)
                    nc.vector.memset(half_pi[:, :], float(np.pi / 2)).then_inc(decay_rows, 1)
                    dve.wait_ge(decay_rows, 3)
                    nc.vector.tensor_scalar(gam[:, :], zero[:, :], c.col("gamma", p=32), None,
                                            ALU.add).then_inc(decay_rows, 1)
                    dve.wait_ge(decay_rows, 4)
                    nc.vector.tensor_tensor_scan(dec[:, 0, 1:T], gam[:, 1:T], zero[:, 1:T], 1.0,
                                                 ALU.mult, ALU.add).then_inc(decay_rows, 1)
                    dve.wait_ge(decay_rows, 5)
                    nc.vector.tensor_scalar(dece[:, :], dec[:, 0, :], 1e-6, None, ALU.add).then_inc(decay_rows, 1)
                    dve.wait_ge(decay_rows, 6)
                    nc.vector.reciprocal(dec[:, 1, :], dece[:, :]).then_inc(decay_rows, 1)
                    for e in range(ET):
                        nc.vector.tensor_scalar(ang[:, e, :], c.row("steps"), c.col("freqs", e), None,
                                                ALU.mult).then_inc(angle_sem, 1)
                    dve.wait_ge(angle_sem, ET)
                    nc.vector.tensor_scalar(turns[:, :, :], ang[:, :, :], float(0.5 / np.pi), MAGIC,
                                            ALU.mult, ALU.add).then_inc(angle_sem, 1)
                    dve.wait_ge(angle_sem, ET + 1)
                    nc.vector.tensor_scalar(turns[:, :, :], turns[:, :, :], MAGIC, None,
                                            ALU.subtract).then_inc(angle_sem, 1)
                    for i, part in enumerate((TWO_PI_HI, TWO_PI_MID, TWO_PI_LO)):
                        dve.wait_ge(angle_sem, ET + 2 + i)
                        nc.vector.scalar_tensor_tensor(out=ang[:, :, :], in0=turns[:, :, :], scalar=-float(part),
                                                       in1=ang[:, :, :], op0=ALU.mult,
                                                       op1=ALU.add).then_inc(angle_sem, 1)
                    for k in range(KD):
                        nc.vector.tensor_scalar(xc[:, k], xpad[:, k, :, 3:3 + T], c.col("conv_w", 4 * k + 3),
                                                c.col("conv_b", k), ALU.mult, ALU.add).then_inc(conv_sem, 1)
                    for j in range(3):
                        for k in range(KD):
                            dve.wait_ge(conv_sem, KD * j + k + 1)
                            nc.vector.scalar_tensor_tensor(out=xc[:, k], in0=xpad[:, k, :, j:j + T],
                                                           scalar=c.col("conv_w", 4 * k + j), in1=xc[:, k],
                                                           op0=ALU.mult, op1=ALU.add).then_inc(conv_sem, 1)

                @block.tensor
                def _(pe):
                    pe.wait_ge(decay_rows, 7)
                    pe.wait_ge(weights, 96)
                    for w in range(2):
                        for e in range(ET):
                            nc.tensor.matmul(c.bank[:, ET * w + e, :], head_out[0:32, e, :], dec[:, w, :],
                                             start=True, stop=True).then_inc(spread, 1)

                @block.scalar
                def _(act):
                    for w, dst in enumerate((decay, undecay)):
                        for e in range(ET):
                            act.wait_ge(spread, ET * w + e + 1)
                            nc.scalar.activation(dst[:, e, :], c.bank[:, ET * w + e, :],
                                                 ACT.Copy).then_inc(spread_used, 1)
                    act.wait_ge(angle_sem, ET + 5)
                    nc.scalar.activation(turns[:, :, :], ang[:, :, :], ACT.Abs).then_inc(abs_sem, 1)
                    act.wait_ge(abs_sem, 1)
                    nc.scalar.activation(cos[:, :, :], turns[:, :, :], ACT.Sin, bias=half_pi[:, 0:1],
                                         scale=-1.0).then_inc(cos_sem, 1)

        gate_ps = c.sem("a0_gate_ps")
        gate_sem = c.sem("a0_gate_ready")
        decayed = c.sem("a0_gate_decayed")
        with nc.Block() as block:
            @block.tensor
            def _(pe):
                for u in range(B * ET):
                    b, e = divmod(u, ET)
                    if u >= 8:
                        pe.wait_ge(gate_sem, u - 7)
                    for k in range(KD):
                        mm = nc.tensor.matmul(c.bank[:, u % 8, :], wg[:, k, e * P:(e + 1) * P], xc[:, k, b, :],
                                              start=(k == 0), stop=(k == KD - 1))
                    mm.then_inc(gate_ps, 1)

            @block.scalar
            def _(act):
                for u in range(B * ET):
                    b, e = divmod(u, ET)
                    act.wait_ge(gate_ps, u + 1)
                    nc.scalar.activation(gate[:, e, b, :], c.bank[:, u % 8, :], ACT.Sigmoid,
                                         bias=c.col("g_b", e)).then_inc(gate_sem, 1)

            @block.gpsimd
            def _(pool):
                for u in range(B * ET):
                    b, e = divmod(u, ET)
                    pool.wait_ge(gate_sem, u + 1)
                    nc.gpsimd.tensor_tensor(gate[:, e, b, :], gate[:, e, b, :], decay[:, e, :],
                                            ALU.mult).then_inc(decayed, 1)

        with ExitStack() as ctx2:
            qk = c.sb(ctx2, "a0_qk", [P, ET, B, 1 + T])
            sq = c.xn_f[:, :, :].rearrange("p k (e t) -> p k e t", e=ET)
            nrm = c.sb(ctx2, "a0_nrm", [P, T])
            rnrm = c.sb(ctx2, "a0_rnrm", [P, T])
            s1, s2, s3, w1 = (c.xn[:, 4 * i:4 * i + 4, :].rearrange("p (s a) d -> p s (a d)", s=2)
                              for i in range(4))
            q_ps = c.sem("a0_q_ps")
            q_zero = c.sem("a0_q_zero")
            q_copy = c.sem("a0_q_copy")
            q_square = c.sem("a0_q_square")
            norm_ps = c.sem("a0_norm_ps")
            norm_root = c.sem("a0_norm_root")
            norm_clip = c.sem("a0_norm_clip")
            norm_inv = c.sem("a0_norm_inv")
            inv_ps = c.sem("a0_inv_ps")
            q_normed = c.sem("a0_q_normed")
            v_ps = c.sem("a0_v_ps")
            phase_sum = c.sem("a0_phase_sum")
            valued = c.sem("a0_valued")
            gated = c.sem("a0_gated")
            scanned = c.sem("a0_scanned")
            undecayed = c.sem("a0_undecayed")
            mixed = c.sem("a0_mixed")
            U = B * ET
            with nc.Block() as block:
                @block.tensor
                def _(pe):
                    for b in range(B):
                        for e in range(ET):
                            u = ET * b + e
                            if u >= 4:
                                pe.wait_ge(q_square, u - 3)
                                pe.wait_ge(q_copy, u - 3)
                            for k in range(KD):
                                mm = nc.tensor.matmul(c.bank[:, u % 4, :], wq[:, k, e * P:(e + 1) * P],
                                                      xc[:, k, b, :], start=(k == 0), stop=(k == KD - 1))
                            mm.then_inc(q_ps, 1)
                        for e in range(ET):
                            pe.wait_ge(q_square, ET * b + e + 1)
                            mm = nc.tensor.matmul(c.bank[32 * b:32 * b + 32, 4, :], head_in[:, e, :],
                                                  sq[:, b % 2, e, :], start=(e == 0), stop=(e == ET - 1))
                        mm.then_inc(norm_ps, 1)
                    pe.wait_ge(norm_inv, 1)
                    for u in range(U):
                        b, e = divmod(u, ET)
                        if u >= 4:
                            pe.wait_ge(q_normed, u - 3)
                        nc.tensor.matmul(c.bank[:, u % 4, :], head_out[32 * b:32 * b + 32, e, :],
                                         rnrm[32 * b:32 * b + 32, :], start=True, stop=True).then_inc(inv_ps, 1)
                        if u >= 3:
                            pe.wait_ge(valued, u - 2)
                        for k in range(KD):
                            mm = nc.tensor.matmul(c.bank[:, 5 + u % 3, :], wv[:, k, e * P:(e + 1) * P],
                                                  xc[:, k, b, :], start=(k == 0), stop=(k == KD - 1))
                        mm.then_inc(v_ps, 1)

                @block.scalar
                def _(act):
                    for b in range(B):
                        for e in range(ET):
                            u = ET * b + e
                            act.wait_ge(q_ps, u + 1)
                            nc.scalar.activation(qk[:, e, b, 1:1 + T], c.bank[:, u % 4, :],
                                                 ACT.Copy).then_inc(q_copy, 1)
                            if b >= 2:
                                act.wait_ge(norm_ps, b - 1)
                            nc.scalar.activation(sq[:, b % 2, e, :], c.bank[:, u % 4, :],
                                                 ACT.Square).then_inc(q_square, 1)
                    act.wait_ge(norm_ps, B)
                    nc.scalar.activation(nrm[:, :], c.bank[:, 4, :], ACT.Sqrt).then_inc(norm_root, 1)

                @block.vector
                def _(dve):
                    dve.wait_ge(norm_root, 1)
                    nc.vector.tensor_scalar(nrm[:, :], nrm[:, :], 1e-12, None, ALU.max).then_inc(norm_clip, 1)
                    dve.wait_ge(norm_clip, 1)
                    nc.vector.reciprocal(rnrm[:, :], nrm[:, :]).then_inc(norm_inv, 1)

                    def unit_q(u):
                        b, e = divmod(u, ET)
                        dve.wait_ge(inv_ps, u + 1)
                        dve.wait_ge(q_copy, u + 1)
                        nc.vector.tensor_tensor(qk[:, e, b, 1:1 + T], qk[:, e, b, 1:1 + T], c.bank[:, u % 4, :],
                                                ALU.mult).then_inc(q_normed, 1)

                    def unit_v(u):
                        dve.wait_ge(v_ps, u + 1)
                        dve.wait_ge(phase_sum, u + 1)
                        if u >= 2:
                            dve.wait_ge(gated, u - 1)
                        nc.vector.tensor_tensor(s2[:, u % 2, :], c.bank[:, 5 + u % 3, :], s1[:, u % 2, :],
                                                ALU.mult).then_inc(valued, 1)

                    def unit_scan(u):
                        b, e = divmod(u, ET)
                        dve.wait_ge(gated, u + 1)
                        nc.vector.tensor_tensor_scan(gate[:, e, b, :], s3[:, u % 2, :], s3[:, u % 2, :], 0.0,
                                                     ALU.add, ALU.bypass).then_inc(scanned, 1)

                    def unit_mix(u):
                        b, e = divmod(u, ET)
                        dve.wait_ge(scanned, u + 1)
                        dve.wait_ge(undecayed, u + 1)
                        nc.vector.tensor_tensor(gate[:, e, b, :], gate[:, e, b, :], w1[:, u % 2, :],
                                                ALU.mult).then_inc(mixed, 1)

                    for i in range(U + 2):
                        if i < U:
                            unit_q(i)
                        if 1 <= i <= U:
                            unit_v(i - 1)
                        if i >= 2:
                            unit_scan(i - 2)
                            unit_mix(i - 2)

                @block.gpsimd
                def _(pool):
                    nc.gpsimd.memset(qk[:, :, :, 0:1], 0.0).then_inc(q_zero, 1)
                    pool.wait_ge(q_zero, 1)

                    def unit_phase(u):
                        b, e = divmod(u, ET)
                        pool.wait_ge(q_normed, u + 1)
                        if u >= 2:
                            pool.wait_ge(valued, u - 1)
                        nc.gpsimd.tensor_tensor(s1[:, u % 2, :], cos[:, e, :], qk[:, e, b, 0:T],
                                                ALU.add).then_inc(phase_sum, 1)

                    def unit_gate(u):
                        b, e = divmod(u, ET)
                        pool.wait_ge(valued, u + 1)
                        if u >= 2:
                            pool.wait_ge(scanned, u - 1)
                        nc.gpsimd.tensor_tensor(s3[:, u % 2, :], s2[:, u % 2, :], gate[:, e, b, :],
                                                ALU.mult).then_inc(gated, 1)
                        if u >= 2:
                            pool.wait_ge(mixed, u - 1)
                        nc.gpsimd.tensor_tensor(w1[:, u % 2, :], qk[:, e, b, 1:1 + T], undecay[:, e, :],
                                                ALU.mult).then_inc(undecayed, 1)

                    for i in range(U + 1):
                        if i < U:
                            unit_phase(i)
                        if i >= 1:
                            unit_gate(i - 1)

        with ExitStack() as ctx2:
            parts = c.sb(ctx2, "a0_parts", [P, NT, 6])
            mom = c.sb(ctx2, "a0_mom", [P, NT, 2])
            sd = c.sb(ctx2, "a0_sd", [P, NT])
            rs = c.sb(ctx2, "a0_rs", [P, NT])
            y = c.sb(ctx2, "a0_y", [P, NT, D])
            out_ps = c.sem("a0_out_ps")
            parts_sem = c.sem("a0_parts_in")
            mom_sem = c.sem("a0_mom_in")
            std_sem = c.sem("a0_std")
            rstd_sem = c.sem("a0_rstd")
            y_sem = c.sem("a0_y_ready")
            gain_sem = c.sem("a0_gain")
            off_sem = c.sem("a0_offset")
            added = c.sem("a0_added")

            def out(t):
                return c.bank[:, t % 8, 0:D]

            with nc.Block() as block:
                @block.tensor
                def _(pe):
                    for t in range(NT):
                        b, i = divmod(t, TB)
                        if t >= 8:
                            pe.wait_ge(y_sem, t - 7)
                        for e in range(ET):
                            mm = nc.tensor.matmul(out(t), gate[:, e, b, i * P:(i + 1) * P], wo[:, e, :],
                                                  start=(e == 0), stop=(e == ET - 1))
                        mm.then_inc(out_ps, 1)

                @block.scalar
                def _(act):
                    for b in range(B):
                        act.wait_ge(mom_sem, TB * (b + 1))
                        nc.scalar.activation(sd[:, TB * b:TB * b + TB], mom[:, TB * b:TB * b + TB, 1], ACT.Sqrt,
                                             bias=c.eps[:, 0:1]).then_inc(std_sem, 1)

                @block.vector
                def _(dve):
                    for b in range(B):
                        ts = range(TB * b, TB * b + TB)
                        for t in ts:
                            dve.wait_ge(out_ps, t + 1)
                            nc.vector.bn_stats(parts[:, t, :], out(t)).then_inc(parts_sem, 1)
                        for t in ts:
                            dve.wait_ge(parts_sem, t + 1)
                            nc.vector.bn_aggr(mom[:, t, :], parts[:, t, :]).then_inc(mom_sem, 1)
                        dve.wait_ge(std_sem, b + 1)
                        nc.vector.reciprocal(rs[:, TB * b:TB * b + TB],
                                             sd[:, TB * b:TB * b + TB]).then_inc(rstd_sem, 1)
                        dve.wait_ge(rstd_sem, b + 1)
                        for t in ts:
                            nc.vector.tensor_scalar(y[:, t, :], out(t), mom[:, t, 0:1], rs[:, t:t + 1],
                                                    ALU.subtract, ALU.mult).then_inc(y_sem, 1)

                @block.gpsimd
                def _(pool):
                    for t in range(NT):
                        nc.gpsimd.tensor_tensor(c.X[:, t, :], c.X[:, t, :], c.row("ln_b"),
                                                ALU.add).then_inc(off_sem, 1)
                    for t in range(NT):
                        pool.wait_ge(y_sem, t + 1)
                        nc.gpsimd.tensor_tensor(y[:, t, :], y[:, t, :], c.row("ln_g"),
                                                ALU.mult).then_inc(gain_sem, 1)
                        pool.wait_ge(gain_sem, t + 1)
                        pool.wait_ge(off_sem, t + 1)
                        nc.gpsimd.tensor_tensor(c.X[:, t, :], c.X[:, t, :], y[:, t, :],
                                                ALU.add).then_inc(added, 1)


STACKS = 3
LAG = HX + 3
SPLIT_Q = (0, 0, 1, 0, 2, 1)
SPLIT_K = (0, 1, 0, 2, 0, 1)
NS = len(SPLIT_Q)
KS = NS * DX
RM = KS


def cross_attention_blocks(c):
    nc, dram = c.nc, c.dram
    norm_block(c, "n1")
    with ExitStack() as ctx:
        values = c.sb(ctx, "x_values", [P, NT, HX, DX + 1])
        O = c.xn
        with ExitStack() as ctx2:
            wq = c.sb(ctx2, "x_wq", [P, KD, D])
            wk = c.sb(ctx2, "x_wk", [CK, 2, D])
            wv = c.sb(ctx2, "x_wv", [CK, 2, D])
            ctx_f = c.sb(ctx2, "x_ctx", [CK, 2, N])
            full = c.sb(ctx2, "x_full", [P, 4, T])
            rest = c.sb(ctx2, "x_rest", [P, 4, T])
            parts = c.sb(ctx2, "x_split", [P, 2, 3, KD, N], BF16)
            bq4 = c.sb(ctx2, "x_bq4", [P, KD])
            weights = c.sem("x_weights")
            ones_set = c.sem("x_ones_set")
            bq_sem = c.sem("x_bq4_ready")
            proj_ps = c.sem("x_proj_ps")
            full_sem = c.sem("x_full_ready")
            high = c.sem("x_high")
            rest1 = c.sem("x_rest_ready")
            mid = c.sem("x_mid")
            low = c.sem("x_low")
            v_ps = c.sem("x_v_ps")
            v_sem = c.sem("x_v_ready")
            spilled = c.sem("x_spilled")
            U = 2 * B * KD

            def place(u):
                b, r = divmod(u, 2 * KD)
                w, m = divmod(r, KD)
                return b, w, m

            with nc.Block() as block:
                @block.sync
                def _(sp):
                    for dst, name in ((wq, "x_wq"), (wk, "x_wk"), (wv, "x_wv"), (ctx_f, "ctx_f")):
                        sp.dma_start(dst[:, :, :], dram[name]).then_inc(weights, 16)
                    for b in range(B):
                        sp.wait_ge(low, 2 * KD * (b + 1))
                        sp.wait_ge(mid, 2 * KD * (b + 1))
                        sp.wait_ge(high, 2 * KD * (b + 1))
                        for w in range(2):
                            for s in range(3):
                                for m in range(KD):
                                    sp.dma_start(dram["split"][w, s, m * P:(m + 1) * P, b * T:(b + 1) * T],
                                                 parts[:, w, s, m, b * T:(b + 1) * T]).then_inc(spilled, 16)
                    sp.wait_ge(spilled, 16 * 6 * KD * B)

                @block.tensor
                def _(pe):
                    pe.wait_ge(weights, 64)
                    for u in range(U):
                        b, w, m = place(u)
                        if u >= 4:
                            pe.wait_ge(high, u - 3)
                        for k in range(2):
                            lhs = (wq, wk)[w][:, k, m * P:(m + 1) * P]
                            rhs = (c.xn_f, ctx_f)[w][:, k, b * T:(b + 1) * T]
                            mm = nc.tensor.matmul(c.bank[:, u % 4, :], lhs, rhs, start=(k == 0), stop=(k == 1))
                        mm.then_inc(proj_ps, 1)
                        t = u
                        if t >= 4:
                            pe.wait_ge(v_sem, t - 3)
                        for k in range(2):
                            mm = nc.tensor.matmul(c.bank[:, 4 + t % 4, 0:D], ctx_f[:, k, t * P:(t + 1) * P],
                                                  wv[:, k, :], start=(k == 0), stop=(k == 1))
                        mm.then_inc(v_ps, 1)

                @block.scalar
                def _(act):
                    act.wait_ge(bq_sem, 1)
                    for u in range(U):
                        b, w, m = place(u)
                        act.wait_ge(proj_ps, u + 1)
                        if u >= 4:
                            act.wait_ge(rest1, u - 3)
                        bias = bq4[:, m:m + 1] if w == 0 else c.col("bk", m)
                        scale = float(DX) ** -0.5 if w == 0 else 1.0
                        nc.scalar.activation(full[:, u % 4, :], c.bank[:, u % 4, :], ACT.Identity, bias=bias,
                                             scale=scale).then_inc(full_sem, 1)
                        nc.scalar.activation(parts[:, w, 0, m, b * T:(b + 1) * T], c.bank[:, u % 4, :],
                                             ACT.Identity, bias=bias, scale=scale).then_inc(high, 1)
                        act.wait_ge(v_ps, u + 1)
                        nc.scalar.activation(values[:, u, :, 0:DX],
                                             c.bank[:, 4 + u % 4, 0:D].rearrange("p (h d) -> p h d", h=HX),
                                             ACT.Copy).then_inc(v_sem, 1)

                @block.vector
                def _(dve):
                    nc.vector.tensor_scalar(bq4[:, :], c.col("bq", 0, KD), float(DX) ** -0.5, None,
                                            ALU.mult).then_inc(bq_sem, 1)
                    for u in range(U):
                        b, w, m = place(u)
                        cols = slice(b * T, (b + 1) * T)
                        dve.wait_ge(full_sem, u + 1)
                        dve.wait_ge(high, u + 1)
                        if u >= 4:
                            dve.wait_ge(low, u - 3)
                        nc.vector.tensor_tensor(rest[:, u % 4, :], full[:, u % 4, :], parts[:, w, 0, m, cols],
                                                ALU.subtract).then_inc(rest1, 1)
                        dve.wait_ge(rest1, u + 1)
                        nc.vector.tensor_copy(parts[:, w, 1, m, cols], rest[:, u % 4, :]).then_inc(mid, 1)
                        dve.wait_ge(mid, u + 1)
                        nc.vector.tensor_tensor(parts[:, w, 2, m, cols], rest[:, u % 4, :],
                                                parts[:, w, 1, m, cols], ALU.subtract).then_inc(low, 1)

                @block.gpsimd
                def _(pool):
                    nc.gpsimd.memset(values[:, :, :, DX:DX + 1], 1.0).then_inc(ones_set, 1)

        with ExitStack() as ctx2:
            qst = c.sb(ctx2, "x_qst", [P, STACKS, HX, T], BF16)
            kst = c.sb(ctx2, "x_kst", [P, STACKS, HX, T], BF16)
            mx = c.sb(ctx2, "x_mx", [P, 2, HX * TB])
            mcl = c.sb(ctx2, "x_mcl", [P, 2, HX * TB])
            neg = c.sb(ctx2, "x_neg", [HX * TB, 2, P])
            nparts = c.sb(ctx2, "x_nparts", [HX * TB, 2, 3, P], BF16)
            floor = c.sb(ctx2, "x_floor", [P, 2, T])
            shifted = c.sb(ctx2, "x_shifted", [P, 2, 2, T])
            probs = c.sb(ctx2, "x_probs", [P, 3, TB, T])
            rsum = c.sb(ctx2, "x_rsum", [P, 2, TB])
            neg_clamp = c.sb(ctx2, "x_neg_clamp", [P, 1])
            const_set = c.sem("x_const_set")
            q_in = [c.sem(f"x_q_in{i}") for i in range(STACKS)]
            k_in = [c.sem(f"x_k_in{i}") for i in range(STACKS)]
            score_ps = c.sem("x_score_ps")
            max_sem = c.sem("x_max")
            clip_sem = c.sem("x_clip")
            turn_ps = c.sem("x_turn_ps")
            neg_sem = c.sem("x_neg_ready")
            nhigh = c.sem("x_nhigh")
            nrest = c.sem("x_nrest")
            nmid = c.sem("x_nmid")
            nlow = c.sem("x_nlow")
            neg_out = c.sem("x_neg_out")
            neg_in = c.sem("x_neg_in")
            floor_ps = c.sem("x_floor_ps")
            floor_sem = c.sem("x_floor_ready")
            keyed_ps = c.sem("x_keyed_ps")
            shift_sem = c.sem("x_shift")
            exp_sem = c.sem("x_exp")
            pv_ps = c.sem("x_pv_ps")
            rsum_sem = c.sem("x_rsum_ready")
            out_sem = c.sem("x_out")
            NH = B * HX

            def s_bank(half):
                return c.bank[:, 0:2, :]

            def t_bank(j):
                return c.bank[:, 2 + 2 * (j % 2):4 + 2 * (j % 2), :]

            FB, PVB = 6, 7

            def pv_out(g):
                return c.bank[:, PVB, 0:TB * (DX + 1)].rearrange("p (i d) -> p i d", i=TB)

            with nc.Block() as block:
                @block.sync
                def _(sp):
                    def stacks(b):
                        s = b % STACKS
                        if b >= STACKS:
                            sp.wait_ge(keyed_ps, 2 * HX * (b - STACKS + 1))
                        for j in range(NS):
                            for w, dst, order, sem in ((0, qst, SPLIT_Q, q_in), (1, kst, SPLIT_K, k_in)):
                                src = dram["split"][w, order[j], :, b * T:(b + 1) * T]
                                sp.dma_start(dst[j * DX:(j + 1) * DX, s, :, :],
                                             src.rearrange("(h d) t -> d h t", d=DX)).then_inc(sem[s], 16)

                    def maxima(b):
                        sp.wait_ge(nhigh, b + 1)
                        sp.wait_ge(nmid, b + 1)
                        sp.wait_ge(nlow, b + 1)
                        sp.dma_start(dram["negmax"][b].rearrange("s r q -> r s q"),
                                     nparts[:, b % 2, :, :]).then_inc(neg_out, 16)
                        sp.wait_ge(neg_out, 16 * (b + 1))
                        sp.dma_start(qst[RM:RM + 3, b % STACKS, :, :],
                                     dram["negmax"][b].rearrange("s (h i) q -> s h (i q)", i=TB)).then_inc(neg_in, 16)

                    for b in range(STACKS):
                        stacks(b)
                    for b in range(B):
                        maxima(b)
                        if b >= 1 and b + STACKS - 1 < B:
                            stacks(b + STACKS - 1)

                @block.tensor
                def _(pe):
                    def scores(g):
                        b, h = divmod(g, HX)
                        if h == 0:
                            pe.wait_ge(q_in[b % STACKS], 16 * NS * (b // STACKS + 1))
                            pe.wait_ge(k_in[b % STACKS], 16 * NS * (b // STACKS + 1))
                        for half in range(2):
                            j = 2 * g + half
                            if j >= 1:
                                pe.wait_ge(max_sem, j)
                            for i in range(2):
                                q0 = (2 * half + i) * P
                                mm = nc.tensor.matmul(c.bank[:, i, :], qst[0:KS, b % STACKS, h, q0:q0 + P],
                                                      kst[0:KS, b % STACKS, h, :], start=True, stop=True)
                            mm.then_inc(score_ps, 1)

                    def turn(b):
                        pe.wait_ge(clip_sem, b + 1)
                        if b >= 1:
                            pe.wait_ge(floor_sem, HX * (b + 1) - LAG)
                        nc.tensor.transpose(c.bank[0:HX * TB, FB, 0:P], mcl[:, b % 2, :],
                                            c.ident[:, :]).then_inc(turn_ps, 1)

                    def weigh(g):
                        b, h = divmod(g, HX)
                        if h == 0:
                            pe.wait_ge(neg_in, 16 * (b + 1))
                        pe.wait_ge(const_set, 1 + STACKS)
                        if g >= 1:
                            pe.wait_ge(floor_sem, g)
                        pe.wait_ge(neg_sem, min(B, (g + LAG) // HX))
                        nc.tensor.matmul(c.bank[:, FB, :], kst[RM:RM + 3, b % STACKS, h, 0:P],
                                         qst[RM:RM + 3, b % STACKS, h, :], start=True, stop=True).then_inc(floor_ps, 1)
                        for half in range(2):
                            j = 2 * g + half
                            if j >= 2:
                                pe.wait_ge(shift_sem, j - 1)
                            for i in range(2):
                                k0 = (2 * half + i) * P
                                mm = nc.tensor.matmul(t_bank(j)[:, i, :], kst[0:RM + 3, b % STACKS, h, k0:k0 + P],
                                                      qst[0:RM + 3, b % STACKS, h, :], start=True, stop=True)
                            mm.then_inc(keyed_ps, 1)

                    def apply(g):
                        b, h = divmod(g, HX)
                        pe.wait_ge(exp_sem, 2 * g + 2)
                        if g >= 1:
                            pe.wait_ge(out_sem, g)
                        for i in range(TB):
                            for k in range(TB):
                                mm = nc.tensor.matmul(pv_out(g)[:, i, :], probs[:, g % 3, k, i * P:(i + 1) * P],
                                                      values[:, TB * b + k, h, :], start=(k == 0),
                                                      stop=(k == TB - 1))
                        mm.then_inc(pv_ps, 1)

                    for g in range(NH + LAG + 2):
                        if g < NH:
                            scores(g)
                        if LAG <= g < NH + LAG:
                            weigh(g - LAG)
                        if g < NH and g % HX == HX - 1:
                            turn(g // HX)
                        if g >= LAG + 2:
                            apply(g - LAG - 2)

                @block.scalar
                def _(act):
                    def negate(b):
                        act.wait_ge(turn_ps, b + 1)
                        nc.scalar.activation(neg[:, b % 2, :], c.bank[0:HX * TB, FB, 0:P], ACT.Copy,
                                             scale=-1.0).then_inc(neg_sem, 1)

                    def weights_of(g):
                        act.wait_ge(floor_ps, g + 1)
                        if g >= 2:
                            act.wait_ge(shift_sem, 2 * g - 2)
                        nc.scalar.activation(floor[:, g % 2, :], c.bank[:, FB, :], ACT.Identity,
                                             bias=neg_clamp[:, 0:1]).then_inc(floor_sem, 1)
                        for half in range(2):
                            j = 2 * g + half
                            act.wait_ge(shift_sem, j + 1)
                            if g >= 3:
                                act.wait_ge(pv_ps, g - 2)
                            nc.scalar.activation(probs[:, g % 3, 2 * half:2 * half + 2, :], shifted[:, j % 2, :, :],
                                                 ACT.Exp).then_inc(exp_sem, 1)

                    act.wait_ge(const_set, 1 + STACKS)
                    for g in range(NH + LAG):
                        if g >= LAG:
                            weights_of(g - LAG)
                        if g < NH and g % HX == HX - 1:
                            negate(g // HX)

                @block.vector
                def _(dve):
                    def maxima(g):
                        b, h = divmod(g, HX)
                        for half in range(2):
                            j = 2 * g + half
                            dve.wait_ge(score_ps, j + 1)
                            nc.vector.tensor_reduce(mx[:, b % 2, TB * h + 2 * half:TB * h + 2 * half + 2],
                                                    c.bank[:, 0:2, :], AX.X, ALU.max).then_inc(max_sem, 1)

                    def clip(b):
                        dve.wait_ge(max_sem, 2 * HX * (b + 1))
                        nc.vector.tensor_scalar(mcl[:, b % 2, :], mx[:, b % 2, :], CLAMP, -CLAMP, ALU.min,
                                                ALU.max).then_inc(clip_sem, 1)

                    def split(b):
                        dve.wait_ge(neg_sem, b + 1)
                        if b >= 2:
                            dve.wait_ge(neg_out, 16 * (b - 1))
                        nc.vector.tensor_copy(nparts[:, b % 2, 0, :], neg[:, b % 2, :]).then_inc(nhigh, 1)
                        dve.wait_ge(nhigh, b + 1)
                        nc.vector.tensor_tensor(neg[:, b % 2, :], neg[:, b % 2, :], nparts[:, b % 2, 0, :],
                                                ALU.subtract).then_inc(nrest, 1)
                        dve.wait_ge(nrest, b + 1)
                        nc.vector.tensor_copy(nparts[:, b % 2, 1, :], neg[:, b % 2, :]).then_inc(nmid, 1)
                        dve.wait_ge(nmid, b + 1)
                        nc.vector.tensor_tensor(nparts[:, b % 2, 2, :], neg[:, b % 2, :], nparts[:, b % 2, 1, :],
                                                ALU.subtract).then_inc(nlow, 1)

                    def shift(g):
                        dve.wait_ge(floor_sem, g + 1)
                        for half in range(2):
                            j = 2 * g + half
                            dve.wait_ge(keyed_ps, j + 1)
                            if j >= 2:
                                dve.wait_ge(exp_sem, j - 1)
                            nc.vector.scalar_tensor_tensor(
                                out=shifted[:, j % 2, :, :], in0=t_bank(j), scalar=0.0,
                                in1=floor[:, g % 2:g % 2 + 1, :].to_broadcast([P, 2, T]),
                                op0=ALU.min, op1=ALU.max).then_inc(shift_sem, 1)

                    def finish(g):
                        b, h = divmod(g, HX)
                        dve.wait_ge(pv_ps, g + 1)
                        nc.vector.reciprocal(rsum[:, g % 2, :], pv_out(g)[:, :, DX]).then_inc(rsum_sem, 1)
                        dve.wait_ge(rsum_sem, g + 1)
                        nc.vector.tensor_tensor(O[:, TB * b:TB * b + TB, h * DX:(h + 1) * DX],
                                                pv_out(g)[:, :, 0:DX],
                                                rsum[:, g % 2, :].unsqueeze(2).to_broadcast([P, TB, DX]),
                                                ALU.mult).then_inc(out_sem, 1)

                    for g in range(NH + LAG + 3):
                        if g >= LAG + 3:
                            finish(g - LAG - 3)
                        if g < NH:
                            maxima(g)
                        if g < NH and g % HX == HX - 1:
                            clip(g // HX)
                        if LAG <= g < NH + LAG:
                            shift(g - LAG)
                        if g < NH and g % HX == HX - 1:
                            split(g // HX)

                @block.gpsimd
                def _(pool):
                    nc.gpsimd.memset(neg_clamp[:, :], -CLAMP).then_inc(const_set, 1)
                    for s in range(STACKS):
                        pool.wait_ge(const_set, 1 + s)
                        nc.gpsimd.memset(kst[RM:P, s, :, :], 1.0).then_inc(const_set, 1)

        with ExitStack() as ctx2:
            wo = c.sb(ctx2, "x_wo", [P, KD, D])
            weights = c.sem("x_wo_in")
            turned = c.sem("x_o_turned")
            stored = c.sem("x_o_stored")
            out_ps = c.sem("x_out_ps")
            off_sem = c.sem("x_offset")
            added = c.sem("x_added")
            with nc.Block() as block:
                @block.sync
                def _(sp):
                    sp.dma_start(wo[:, :, :], dram["x_wo"]).then_inc(weights, 16)

                @block.tensor
                def _(pe):
                    def turn(b):
                        for k in range(KD):
                            if b >= 2:
                                pe.wait_ge(stored, KD * (b - 2) + k + 1)
                            for i in range(TB):
                                tr = nc.tensor.transpose(c.bank[:, KD * (b % 2) + k, i * P:(i + 1) * P],
                                                         O[:, TB * b + i, k * P:(k + 1) * P], c.ident[:, :])
                            tr.then_inc(turned, 1)

                    turn(0)
                    pe.wait_ge(weights, 16)
                    for b in range(B):
                        if b + 1 < B:
                            turn(b + 1)
                        pe.wait_ge(stored, KD * (b + 1))
                        for t in range(TB * b, TB * b + TB):
                            if t >= 4:
                                pe.wait_ge(added, t - 3)
                            for k in range(KD):
                                mm = nc.tensor.matmul(c.bank[:, 4 + t % 4, 0:D], c.xn_f[:, k, t * P:(t + 1) * P],
                                                      wo[:, k, :], start=(k == 0), stop=(k == KD - 1))
                            mm.then_inc(out_ps, 1)

                @block.scalar
                def _(act):
                    for b in range(B):
                        for k in range(KD):
                            act.wait_ge(turned, KD * b + k + 1)
                            nc.scalar.activation(c.xn_f[:, k, b * T:(b + 1) * T], c.bank[:, KD * (b % 2) + k, :],
                                                 ACT.Identity, bias=c.col("bv", k)).then_inc(stored, 1)

                @block.gpsimd
                def _(pool):
                    for t in range(NT):
                        nc.gpsimd.tensor_tensor(c.X[:, t, :], c.X[:, t, :], c.row("bo"),
                                                ALU.add).then_inc(off_sem, 1)

                @block.vector
                def _(dve):
                    for t in range(NT):
                        dve.wait_ge(out_ps, t + 1)
                        dve.wait_ge(off_sem, t + 1)
                        nc.vector.tensor_tensor(c.X[:, t, :], c.X[:, t, :], c.bank[:, 4 + t % 4, 0:D],
                                                ALU.add).then_inc(added, 1)


def route_block(c, ctx, tag, n_all, w_name, bias):
    nc, dram = c.nc, c.dram
    gates = c.sb(ctx, tag + "_gates", [P, NT, n_all])
    with ExitStack() as ctx2:
        wg = c.sb(ctx2, tag + "_wg", [P, KD, n_all])
        lg = c.sb(ctx2, tag + "_lg", [P, NT, n_all])
        rest = c.sb(ctx2, tag + "_rest", [P, NT, n_all])
        cand = c.sb(ctx2, tag + "_cand", [P, NT, n_all])
        pick = c.sb(ctx2, tag + "_pick", [P, 2, NT, n_all])
        top = c.sb(ctx2, tag + "_top", [P, 2, NT])
        at = c.sb(ctx2, tag + "_at", [P, 2, NT])
        ex = c.sb(ctx2, tag + "_ex", [P, NT])
        den = c.sb(ctx2, tag + "_den", [P, NT])
        share = c.sb(ctx2, tag + "_share", [P, 2, NT])
        weights, weights0 = c.tally("route_wg_in", 16)
        logits, logits0 = c.tally("route_logits", 1)
        step, step0 = c.tally("route_step", 18)
        gap, gap0 = c.tally("route_gap", 1)
        exp_sem, exp_sem0 = c.tally("route_exp", 1)

        def wide(ap):
            return ap.unsqueeze(2).to_broadcast([P, NT, n_all])

        index = c.row("expert_index")[:, 0:n_all].unsqueeze(1).to_broadcast([P, NT, n_all])
        with nc.Block() as block:
            @block.sync
            def _(sp):
                sp.dma_start(wg[:, :, :], dram[w_name]).then_inc(weights, 16)

            @block.tensor
            def _(pe):
                pe.wait_ge(weights, weights0 + 16)
                for t in range(NT):
                    for k in range(KD):
                        mm = nc.tensor.matmul(c.bank[:, 0, t * n_all:(t + 1) * n_all],
                                              c.xn_f[:, k, t * P:(t + 1) * P], wg[:, k, :],
                                              start=(k == 0), stop=(k == KD - 1))
                mm.then_inc(logits, 1)

            @block.vector
            def _(dve):
                done = [0]

                def then(ins):
                    done[0] += 1
                    ins.then_inc(step, 1)
                    dve.wait_ge(step, step0 + done[0])

                dve.wait_ge(logits, logits0 + 1)
                ps = c.bank[:, 0, 0:NT * n_all].rearrange("p (t e) -> p t e", t=NT)
                if bias:
                    then(nc.vector.tensor_tensor(lg[:, :, :], ps,
                                                 c.row("expert_bias").unsqueeze(1).to_broadcast([P, NT, n_all]),
                                                 ALU.add))
                else:
                    then(nc.vector.tensor_copy(lg[:, :, :], ps))
                left = lg
                for r in range(2):
                    then(nc.vector.tensor_reduce(top[:, r, :], left[:, :, :], AX.X, ALU.max))
                    then(nc.vector.tensor_tensor(cand[:, :, :], left[:, :, :], wide(top[:, r, :]), ALU.is_lt))
                    then(nc.vector.scalar_tensor_tensor(out=cand[:, :, :], in0=cand[:, :, :], scalar=float(n_all),
                                                        in1=index, op0=ALU.mult, op1=ALU.add))
                    then(nc.vector.tensor_reduce(at[:, r, :], cand[:, :, :], AX.X, ALU.min))
                    then(nc.vector.tensor_tensor(pick[:, r], cand[:, :, :], wide(at[:, r, :]), ALU.is_equal))
                    if r == 0:
                        then(nc.vector.scalar_tensor_tensor(out=rest[:, :, :], in0=pick[:, 0], scalar=-3.0e38,
                                                            in1=lg[:, :, :], op0=ALU.mult, op1=ALU.add))
                        left = rest
                nc.vector.tensor_tensor(ex[:, :], top[:, 1, :], top[:, 0, :], ALU.subtract).then_inc(gap, 1)
                dve.wait_ge(exp_sem, exp_sem0 + 1)
                then(nc.vector.tensor_scalar(den[:, :], ex[:, :], 1.0, None, ALU.add))
                then(nc.vector.reciprocal(share[:, 0, :], den[:, :]))
                then(nc.vector.tensor_tensor(share[:, 1, :], share[:, 0, :], ex[:, :], ALU.mult))
                then(nc.vector.tensor_tensor(pick[:, 0], pick[:, 0], wide(share[:, 0, :]), ALU.mult))
                then(nc.vector.tensor_tensor(pick[:, 1], pick[:, 1], wide(share[:, 1, :]), ALU.mult))
                then(nc.vector.tensor_tensor(gates[:, :, :], pick[:, 0], pick[:, 1], ALU.add))
                assert done[0] == 18

            @block.scalar
            def _(act):
                act.wait_ge(gap, gap0 + 1)
                nc.scalar.activation(ex[:, :], ex[:, :], ACT.Exp).then_inc(exp_sem, 1)
    return gates


def experts_blocks(c):
    nc, dram = c.nc, c.dram
    norm_block(c, "n2")
    FT = FF0 // P
    with ExitStack() as ctx:
        gates = route_block(c, ctx, "r0", NE_ALL, "e0_gate", True)
        w1 = c.sb(ctx, "e0_w1", [P, 2, KD, FF0])
        w2 = c.sb(ctx, "e0_w2", [P, 2, FT, D])
        hid = c.sb(ctx, "e0_hid", [P, 2, FT, T])
        zero_w = c.sb(ctx, "e0_zero_w", [P, NT])
        w1_in = [c.sem(f"e0_w1_in{i}") for i in range(2)]
        w2_in = [c.sem(f"e0_w2_in{i}") for i in range(2)]
        hid_ps = c.sem("e0_hid_ps")
        hid_sem = c.sem("e0_hid_ready")
        out_ps = c.sem("e0_out_ps")
        added = c.sem("e0_added")
        zero_sem = c.sem("e0_zero")
        with nc.Block() as block:
            @block.sync
            def _(sp):
                for e in range(NE):
                    if e >= 2:
                        sp.wait_ge(out_ps, NT * (e - 1))
                    sp.dma_start(w1[:, e % 2], dram["e0_w1"][e]).then_inc(w1_in[e % 2], 16)
                    sp.dma_start(w2[:, e % 2], dram["e0_w2"][e]).then_inc(w2_in[e % 2], 16)

            @block.tensor
            def _(pe):
                def hidden(u):
                    e, b = divmod(u, B)
                    if b == 0:
                        pe.wait_ge(w1_in[e % 2], 16 * (e // 2 + 1))
                    for f in range(FT):
                        n = FT * u + f
                        if n >= 4:
                            pe.wait_ge(hid_sem, n - 3)
                        for k in range(KD):
                            mm = nc.tensor.matmul(c.bank[:, n % 4, :], w1[:, e % 2, k, f * P:(f + 1) * P],
                                                  c.xn_f[:, k, b * T:(b + 1) * T], start=(k == 0),
                                                  stop=(k == KD - 1))
                        mm.then_inc(hid_ps, 1)

                def output(u):
                    e, b = divmod(u, B)
                    if b == 0:
                        pe.wait_ge(w2_in[e % 2], 16 * (e // 2 + 1))
                    pe.wait_ge(hid_sem, FT * (u + 1))
                    for i in range(TB):
                        n = TB * u + i
                        if n >= 4:
                            pe.wait_ge(added, n - 3)
                        for f in range(FT):
                            mm = nc.tensor.matmul(c.bank[:, 4 + n % 4, 0:D], hid[:, u % 2, f, i * P:(i + 1) * P],
                                                  w2[:, e % 2, f, :], start=(f == 0), stop=(f == FT - 1))
                        mm.then_inc(out_ps, 1)

                hidden(0)
                for u in range(NE * B):
                    if u + 1 < NE * B:
                        hidden(u + 1)
                    output(u)

            @block.scalar
            def _(act):
                for u in range(NE * B):
                    for f in range(FT):
                        n = FT * u + f
                        act.wait_ge(hid_ps, n + 1)
                        if u >= 2:
                            act.wait_ge(out_ps, TB * (u - 1))
                        nc.scalar.activation(hid[:, u % 2, f, :], c.bank[:, n % 4, :],
                                             ACT.Silu).then_inc(hid_sem, 1)

            @block.vector
            def _(dve):
                nc.vector.tensor_reduce(zero_w[:, :], gates[:, :, NE:NE_ALL], AX.X, ALU.add).then_inc(zero_sem, 1)
                dve.wait_ge(zero_sem, 1)
                for t in range(NT):
                    nc.vector.scalar_tensor_tensor(out=c.X[:, t, :], in0=c.xn[:, t, :], scalar=zero_w[:, t:t + 1],
                                                   in1=c.X[:, t, :], op0=ALU.mult,
                                                   op1=ALU.add).then_inc(zero_sem, 1)
                for u in range(NE * B):
                    e, b = divmod(u, B)
                    for i in range(TB):
                        n, t = TB * u + i, TB * b + i
                        dve.wait_ge(out_ps, n + 1)
                        if e == 0:
                            dve.wait_ge(zero_sem, t + 2)
                        else:
                            dve.wait_ge(added, NT * (e - 1) + t + 1)
                        nc.vector.scalar_tensor_tensor(out=c.X[:, t, :], in0=c.bank[:, 4 + n % 4, 0:D],
                                                       scalar=gates[:, t, e:e + 1], in1=c.X[:, t, :],
                                                       op0=ALU.mult, op1=ALU.add).then_inc(added, 1)


def gru_blocks(c):
    nc, dram = c.nc, c.dram
    norm_block(c, "n3")
    with ExitStack() as ctx:
        wf = c.sb(ctx, "g_wf", [P, KD, 2 * EG])
        wd = c.sb(ctx, "g_wd", [P, GT, D])
        state = c.sb(ctx, "g_state", [P, GT, B, T])
        z = c.sb(ctx, "g_z", [P, 2, T])
        keep = c.sb(ctx, "g_keep", [P, 4, T])
        soft = c.sb(ctx, "g_soft", [P, 2, T])
        lin = c.sb(ctx, "g_lin", [P, 2, T])
        cand = c.sb(ctx, "g_cand", [P, 2, T])
        val = c.sb(ctx, "g_val", [P, 2, T])
        neg_b = c.sb(ctx, "g_neg_b", [P, GT])
        weights = c.sem("g_weights")
        neg_sem = c.sem("g_neg_b_ready")
        kz_ps = c.sem("g_kz_ps")
        hx_ps = c.sem("g_hx_ps")
        z_sem = c.sem("g_z_ready")
        keep_sem = c.sem("g_keep_ready")
        soft_sem = c.sem("g_soft_ready")
        lin_sem = c.sem("g_lin_ready")
        cand_sem = c.sem("g_cand_ready")
        val_sem = c.sem("g_val_ready")
        scanned = c.sem("g_scanned")
        out_ps = c.sem("g_out_ps")
        added = c.sem("g_added")
        U = B * GT
        with nc.Block() as block:
            @block.sync
            def _(sp):
                sp.dma_start(wf[:, :, :], dram["g_wf"]).then_inc(weights, 16)
                sp.dma_start(wd[:, :, :], dram["g_wd"]).then_inc(weights, 16)

            @block.tensor
            def _(pe):
                pe.wait_ge(weights, 32)
                for u in range(U):
                    b, m = divmod(u, GT)
                    for bank, off, sem, used in ((0, 0, kz_ps, keep_sem), (2, EG, hx_ps, lin_sem)):
                        if u >= 2:
                            pe.wait_ge(used, u - 1)
                            if off:
                                pe.wait_ge(soft_sem, u - 1)
                        for k in range(KD):
                            mm = nc.tensor.matmul(c.bank[:, bank + u % 2, :],
                                                  wf[:, k, off + m * P:off + (m + 1) * P],
                                                  c.xn_f[:, k, b * T:(b + 1) * T], start=(k == 0),
                                                  stop=(k == KD - 1))
                        mm.then_inc(sem, 1)
                for t in range(NT):
                    b, i = divmod(t, TB)
                    pe.wait_ge(scanned, GT * (b + 1))
                    if t >= 4:
                        pe.wait_ge(added, t - 3)
                    for m in range(GT):
                        mm = nc.tensor.matmul(c.bank[:, 4 + t % 4, 0:D], state[:, m, b, i * P:(i + 1) * P],
                                              wd[:, m, :], start=(m == 0), stop=(m == GT - 1))
                    mm.then_inc(out_ps, 1)

            @block.scalar
            def _(act):
                act.wait_ge(neg_sem, 1)
                for u in range(U):
                    b, m = divmod(u, GT)
                    act.wait_ge(kz_ps, u + 1)
                    if u >= 2:
                        act.wait_ge(val_sem, u - 1)
                    nc.scalar.activation(z[:, u % 2, :], c.bank[:, u % 2, :], ACT.Sigmoid,
                                         bias=c.col("b_f", m)).then_inc(z_sem, 1)
                    if u >= 4:
                        act.wait_ge(scanned, u - 3)
                    nc.scalar.activation(keep[:, u % 4, :], c.bank[:, u % 2, :], ACT.Sigmoid,
                                         bias=neg_b[:, m:m + 1], scale=-1.0).then_inc(keep_sem, 1)
                    act.wait_ge(lin_sem, u + 1)
                    if u >= 2:
                        act.wait_ge(cand_sem, u - 1)
                    nc.scalar.activation(soft[:, u % 2, :], c.bank[:, 2 + u % 2, :], ACT.Sigmoid,
                                         bias=c.col("b_f", GT + m)).then_inc(soft_sem, 1)

            @block.vector
            def _(dve):
                nc.vector.tensor_scalar(neg_b[:, :], c.col("b_f", 0, GT), -1.0, None,
                                        ALU.mult).then_inc(neg_sem, 1)

                def candidate(u):
                    b, m = divmod(u, GT)
                    dve.wait_ge(hx_ps, u + 1)
                    if u >= 2:
                        dve.wait_ge(cand_sem, u - 1)
                    nc.vector.tensor_scalar(lin[:, u % 2, :], c.bank[:, 2 + u % 2, :], c.col("b_f", GT + m), 0.0,
                                            ALU.add, ALU.max).then_inc(lin_sem, 1)
                    dve.wait_ge(lin_sem, u + 1)
                    dve.wait_ge(soft_sem, u + 1)
                    if u >= 2:
                        dve.wait_ge(val_sem, u - 1)
                    nc.vector.scalar_tensor_tensor(out=cand[:, u % 2, :], in0=soft[:, u % 2, :], scalar=0.5,
                                                   in1=lin[:, u % 2, :], op0=ALU.min,
                                                   op1=ALU.add).then_inc(cand_sem, 1)

                def scan(u):
                    b, m = divmod(u, GT)
                    dve.wait_ge(val_sem, u + 1)
                    dve.wait_ge(keep_sem, u + 1)
                    nc.vector.tensor_tensor_scan(state[:, m, b, :], keep[:, u % 4, :], val[:, u % 2, :], 0.5,
                                                 ALU.mult, ALU.add).then_inc(scanned, 1)

                for u in range(U + 1):
                    if u < U:
                        candidate(u)
                    if u >= 1:
                        scan(u - 1)
                for t in range(NT):
                    dve.wait_ge(out_ps, t + 1)
                    nc.vector.tensor_tensor(c.X[:, t, :], c.X[:, t, :], c.bank[:, 4 + t % 4, 0:D],
                                            ALU.add).then_inc(added, 1)

            @block.gpsimd
            def _(pool):
                for u in range(U):
                    pool.wait_ge(cand_sem, u + 1)
                    pool.wait_ge(z_sem, u + 1)
                    if u >= 2:
                        pool.wait_ge(scanned, u - 1)
                    nc.gpsimd.tensor_tensor(val[:, u % 2, :], cand[:, u % 2, :], z[:, u % 2, :],
                                            ALU.mult).then_inc(val_sem, 1)


TERNARY = (("t_d2v", CK, 2, D), ("t_img", P, KD, D), ("t_txt", P, KD, D), ("t_att0", P, KD, P),
           ("t_att1", P, KD, P), ("t_f1", P, 2 * KD, FX), ("t_f2", P, FX // P, D))
W_D2V, W_IMG, W_TXT, W_ATT0, W_ATT1, W_F1, W_F2 = range(len(TERNARY))


def ternary_weights_block(c, ctx):
    nc, dram = c.nc, c.dram
    n = len(TERNARY)
    tern = [c.sb(ctx, name + "_q", [p, k, w], BF16) for name, p, k, w in TERNARY]
    scale = c.sb(ctx, "t_scale", [P, n])
    with ExitStack() as ctx2:
        full = [c.sb(ctx2, name, [p, k, w]) for name, p, k, w in TERNARY]
        below = [c.sb(ctx2, name + "_b", [p, k, w], BF16) for name, p, k, w in TERNARY]
        sums = c.sb(ctx2, "t_sums", [P, n])
        total = c.sb(ctx2, "t_total", [P, n])
        half = c.sb(ctx2, "t_half", [P, 2, n])
        loaded = [c.sem(f"t_loaded{i}") for i in range(n)]
        zero_sem = c.sem("t_zero")
        sum_sem = c.sem("t_sum")
        total_sem = c.sem("t_total_ready")
        scale_sem = c.sem("t_scale_ready")
        half_sem = c.sem("t_half_ready")
        below_sem = c.sem("t_below")
        tern_sem = c.sem("t_tern")
        with nc.Block() as block:
            @block.sync
            def _(sp):
                for i, (name, p, k, w) in enumerate(TERNARY):
                    sp.dma_start(full[i][:, :, :], dram[name]).then_inc(loaded[i], 16)

            @block.gpsimd
            def _(pool):
                pool.wait_ge(sum_sem, n)
                nc.gpsimd.partition_all_reduce(total[:, :], sums[:, :], P, RED.add).then_inc(total_sem, 1)

            @block.vector
            def _(dve):
                nc.vector.memset(sums[:, :], 0.0).then_inc(zero_sem, 1)
                dve.wait_ge(zero_sem, 1)
                for i, (name, p, k, w) in enumerate(TERNARY):
                    dve.wait_ge(loaded[i], 16)
                    nc.vector.tensor_reduce(sums[0:p, i:i + 1], full[i][:, :, :], AX.XY, ALU.add,
                                            apply_absolute_value=True).then_inc(sum_sem, 1)
                dve.wait_ge(total_sem, 1)
                for i, (name, p, k, w) in enumerate(TERNARY):
                    nc.vector.tensor_scalar(scale[:, i:i + 1], total[:, i:i + 1], 1.0 / (p * k * w), 1e-5,
                                            ALU.mult, ALU.max).then_inc(scale_sem, 1)
                dve.wait_ge(scale_sem, n)
                nc.vector.tensor_scalar(half[:, 0, :], scale[:, :], 0.5, None, ALU.mult).then_inc(half_sem, 1)
                nc.vector.tensor_scalar(half[:, 1, :], scale[:, :], -0.5, None, ALU.mult).then_inc(half_sem, 1)
                dve.wait_ge(half_sem, 2)
                for i, (name, p, k, w) in enumerate(TERNARY):
                    nc.vector.tensor_scalar(below[i][:, :, :], full[i][:, :, :], half[0:p, 1, i:i + 1], None,
                                            ALU.is_lt).then_inc(below_sem, 1)
                for i, (name, p, k, w) in enumerate(TERNARY):
                    dve.wait_ge(below_sem, i + 1)
                    nc.vector.scalar_tensor_tensor(
                        out=tern[i][:, :, :].rearrange("p k w -> p (k w)"),
                        in0=full[i][:, :, :].rearrange("p k w -> p (k w)"), scalar=half[0:p, 0, i:i + 1],
                        in1=below[i][:, :, :].rearrange("p k w -> p (k w)"), op0=ALU.is_gt,
                        op1=ALU.subtract).then_inc(tern_sem, 1)
    return tern, scale


def quantise_block(c, tag, sources, scale, i_w, scratch):
    nc = c.nc
    peak, top, step, inv, out_scale, magic = scratch
    n = len(sources)
    peak_zero, peak_zero0 = c.tally("quant_peak_zero", 1)
    peak_sem, peak_sem0 = c.tally("quant_peak", n)
    peak1_sem, peak1_sem0 = c.tally("quant_peak1", 1)
    top_sem, top_sem0 = c.tally("quant_top", 1)
    step_sem, step_sem0 = c.tally("quant_step", 1)
    inv_sem, inv_sem0 = c.tally("quant_inv", 1)
    scale_sem, scale_sem0 = c.tally("quant_scale", 1)
    up_sem, up_sem0 = c.tally("quant_up", n)
    clip_sem, clip_sem0 = c.tally("quant_clip", n)
    down_sem, down_sem0 = c.tally("quant_down", n)
    with nc.Block() as block:
        @block.vector
        def _(dve):
            nc.vector.memset(peak[:, :], 0.0).then_inc(peak_zero, 1)
            dve.wait_ge(peak_zero, peak_zero0 + 1)
            for i, (src, dst) in enumerate(sources):
                axis = AX.X if len(src.shape) == 2 else AX.XY
                nc.vector.tensor_reduce(peak[0:src.shape[0], i:i + 1], src, axis, ALU.max,
                                        apply_absolute_value=True).then_inc(peak_sem, 1)
            dve.wait_ge(peak_sem, peak_sem0 + n)
            nc.vector.tensor_reduce(top[:, 0:1], peak[:, 0:n], AX.X, ALU.max).then_inc(peak1_sem, 1)
            dve.wait_ge(top_sem, top_sem0 + 1)
            nc.vector.tensor_scalar(step[:, 0:1], top[:, 1:2], 1e-8, 1.0 / 127.0, ALU.max,
                                    ALU.mult).then_inc(step_sem, 1)
            dve.wait_ge(step_sem, step_sem0 + 1)
            nc.vector.reciprocal(inv[:, 0:1], step[:, 0:1]).then_inc(inv_sem, 1)
            nc.vector.tensor_tensor(out_scale[:, 0:1], step[:, 0:1], scale[:, i_w:i_w + 1],
                                    ALU.mult).then_inc(scale_sem, 1)
            for i, (src, dst) in enumerate(sources):
                dve.wait_ge(up_sem, up_sem0 + i + 1)
                nc.vector.tensor_scalar(src, src, MAGIC - 128.0, MAGIC + 127.0, ALU.max,
                                        ALU.min).then_inc(clip_sem, 1)

        @block.gpsimd
        def _(pool):
            pool.wait_ge(peak1_sem, peak1_sem0 + 1)
            nc.gpsimd.partition_all_reduce(top[:, 1:2], top[:, 0:1], P, RED.max).then_inc(top_sem, 1)
            for i, (src, dst) in enumerate(sources):
                pool.wait_ge(clip_sem, clip_sem0 + i + 1)
                nc.gpsimd.tensor_scalar(dst, src, 1.0, -MAGIC, ALU.mult, ALU.add).then_inc(down_sem, 1)

        @block.scalar
        def _(act):
            act.wait_ge(inv_sem, inv_sem0 + 1)
            for i, (src, dst) in enumerate(sources):
                p = src.shape[0]
                nc.scalar.activation(src, src, ACT.Identity, bias=magic[0:p, 0:1],
                                     scale=inv[0:p, 0:1]).then_inc(up_sem, 1)


def product_block(c, tag, units, out_scale, func=ACT.Identity):
    nc = c.nc
    ps, ps0 = c.tally("product_ps", len(units))
    done, done0 = c.tally("product_done", len(units))
    with nc.Block() as block:
        @block.tensor
        def _(pe):
            for u, (pairs, out, bias) in enumerate(units):
                if u >= 8:
                    pe.wait_ge(done, done0 + u - 7)
                for k, (lhs, rhs) in enumerate(pairs):
                    mm = nc.tensor.matmul(c.bank[:, u % 8, :], lhs, rhs, start=(k == 0),
                                          stop=(k == len(pairs) - 1))
                mm.then_inc(ps, 1)

        @block.scalar
        def _(act):
            for u, (pairs, out, bias) in enumerate(units):
                act.wait_ge(ps, ps0 + u + 1)
                nc.scalar.activation(out, c.bank[:, u % 8, :], func, bias=bias,
                                     scale=out_scale[:, 0:1]).then_inc(done, 1)


def ternary_cross_blocks(c):
    nc, dram = c.nc, c.dram
    norm_block(c, "n4")
    with ExitStack() as ctx:
        tern, scale = ternary_weights_block(c, ctx)
        peak = c.sb(ctx, "t_peak", [P, 32])
        top = c.sb(ctx, "t_top", [P, 2])
        step = c.sb(ctx, "t_step", [P, 1])
        inv = c.sb(ctx, "t_inv", [P, 1])
        magic = c.sb(ctx, "t_magic", [P, 1])
        out_scale = c.sb(ctx, "t_out_scale", [P, 1])
        scratch = (peak, top, step, inv, out_scale, magic)
        fused = c.sb(ctx, "t_fused", [P, KD, N])
        mean_img = c.sb(ctx, "t_mean_img", [P, KD, B])
        keys_ctx = ExitStack()
        keys_f = c.sb(keys_ctx, "t_keys_f", [P, 2, N])
        keys_t = c.sb(keys_ctx, "t_keys_t", [P, 2, NT, P])

        def cut(ap, b):
            return ap[:, b * T:(b + 1) * T]

        with ExitStack() as ctx2:
            cf = c.sb(ctx2, "t_ctx", [CK, 2, N])
            qb = c.sb(ctx2, "t_q", [P, KD, N], BF16)
            img = c.sb(ctx2, "t_img_f", [P, KD, N])
            ctx_in = c.sem("t_ctx_in")
            magic_set = c.sem("t_magic_set")
            mean_sum = c.sem("t_mean_sum")
            mean_sem = c.sem("t_mean")
            turned = c.sem("t_keys_turned")
            turned_out = c.sem("t_keys_stored")
            with nc.Block() as block:
                @block.sync
                def _(sp):
                    sp.dma_start(cf[:, :, :], dram["ctx_f"]).then_inc(ctx_in, 16)
                    sp.wait_ge(ctx_in, 16)

                @block.gpsimd
                def _(pool):
                    nc.gpsimd.memset(magic[:, :], MAGIC).then_inc(magic_set, 1)

            def project(tag, src, rows, i_w, i_b, dst, halves=KD):
                quantise_block(c, tag + "q", [(cut(src[:, k, :], b), cut(qb[0:rows, k, :], b))
                                              for k in range(2) for b in range(B)], scale, i_w, scratch)
                product_block(c, tag, [([(tern[i_w][:, k, m * P:(m + 1) * P], cut(qb[0:rows, k, :], b))
                                         for k in range(2)], cut(dst[:, m, :], b), c.col(i_b, m))
                                       for b in range(B) for m in range(halves)], out_scale)

            project("td", cf, CK, W_D2V, "b_d2v", fused)
            project("ti", fused, P, W_IMG, "b_img", img)
            with nc.Block() as block:
                @block.vector
                def _(dve):
                    nc.vector.tensor_reduce(mean_img[:, :, :], img[:, :, :].rearrange("p k (b t) -> p k b t", b=B),
                                            AX.X, ALU.add).then_inc(mean_sum, 1)
                    dve.wait_ge(mean_sum, 1)
                    nc.vector.tensor_scalar(mean_img[:, :, :], mean_img[:, :, :], 1.0 / T, None,
                                            ALU.mult).then_inc(mean_sem, 1)
            quantise_block(c, "tkq", [(cut(img[:, k, :], b), cut(qb[:, k, :], b))
                                      for k in range(2) for b in range(B)], scale, W_ATT0, scratch)
            product_block(c, "tk0", [([(tern[W_ATT0][:, k, :], cut(qb[:, k, :], b)) for k in range(2)],
                                      cut(keys_f[:, 0, :], b), c.col("b_att0")) for b in range(B)], out_scale)
            scale1 = c.sem("t_scale1")
            with nc.Block() as block:
                @block.vector
                def _(dve):
                    nc.vector.tensor_tensor(out_scale[:, 0:1], step[:, 0:1], scale[:, W_ATT1:W_ATT1 + 1],
                                            ALU.mult).then_inc(scale1, 1)
            product_block(c, "tk1", [([(tern[W_ATT1][:, k, :], cut(qb[:, k, :], b)) for k in range(2)],
                                      cut(keys_f[:, 1, :], b), c.col("b_att1")) for b in range(B)], out_scale)
            with nc.Block() as block:
                @block.tensor
                def _(pe):
                    for j in range(2 * B):
                        r, b = divmod(j, B)
                        for i in range(TB):
                            tr = nc.tensor.transpose(c.bank[:, j, i * P:(i + 1) * P],
                                                     keys_f[:, r, b * T + i * P:b * T + (i + 1) * P],
                                                     c.ident[:, :])
                        tr.then_inc(turned, 1)

                @block.scalar
                def _(act):
                    for j in range(2 * B):
                        r, b = divmod(j, B)
                        act.wait_ge(turned, j + 1)
                        nc.scalar.activation(keys_t[:, r, TB * b:TB * b + TB, :],
                                             c.bank[:, j, :].rearrange("p (i d) -> p i d", i=TB),
                                             ACT.Copy).then_inc(turned_out, 1)
            project("tt", c.xn_f, P, W_TXT, "b_txt", fused)

        with ExitStack() as ctx2:
            qsum = c.sb(ctx2, "t_qsum", [P, 2, T])
            mx = c.sb(ctx2, "t_mx", [P, 2 * NT])
            neg = c.sb(ctx2, "t_neg", [P, 2 * NT])
            ex = c.sb(ctx2, "t_ex", [P, 2, T])
            rsum = c.sb(ctx2, "t_rsum", [P, 2 * NT])
            rinv = c.sb(ctx2, "t_rinv", [P, 2 * NT])
            probs = c.sb(ctx2, "t_probs", [P, 2, T])
            probs_f = c.sb(ctx2, "t_probs_f", [P, 2, TB, T])
            qsum_sem = c.sem("t_qsum_ready")
            score_ps = c.sem("t_score_ps")
            max_sem = c.sem("t_max")
            neg_sem = c.sem("t_neg_ready")
            exp_sem = c.sem("t_exp")
            inv_sem = c.sem("t_rinv_ready")
            prob_sem = c.sem("t_prob")
            turn_ps = c.sem("t_turn_ps")
            turn_out = c.sem("t_turn_out")
            att_ps = c.sem("t_att_ps")
            add_sem = c.sem("t_add")
            inv_sqrt = 1.0 / float(np.sqrt(D))
            with nc.Block() as block:
                @block.tensor
                def _(pe):
                    def score(u):
                        r, b, i = u // NT, (u // TB) % B, u % TB
                        g = u // TB
                        pe.wait_ge(qsum_sem, g + 1)
                        if u >= 2:
                            pe.wait_ge(exp_sem, u - 1)
                        nc.tensor.matmul(c.bank[:, u % 2, :], qsum[:, g % 2, i * P:(i + 1) * P],
                                         cut(keys_f[:, r, :], b), start=True, stop=True).then_inc(score_ps, 1)

                    def turn(u):
                        pe.wait_ge(prob_sem, u + 1)
                        if u >= 2:
                            pe.wait_ge(turn_out, u - 1)
                        for k in range(TB):
                            tr = nc.tensor.transpose(c.bank[:, 2 + u % 2, k * P:(k + 1) * P],
                                                     probs[:, u % 2, k * P:(k + 1) * P], c.ident[:, :])
                        tr.then_inc(turn_ps, 1)

                    def apply(g):
                        r, b = divmod(g, B)
                        pe.wait_ge(turn_out, TB * (g + 1))
                        if g >= 2:
                            pe.wait_ge(add_sem, KD * (g - 1))
                        for k in range(TB):
                            mm = nc.tensor.matmul(c.bank[:, 6 + g % 2, :], keys_t[:, r, TB * b + k, :],
                                                  probs_f[:, g % 2, k, :], start=(k == 0), stop=(k == TB - 1))
                        mm.then_inc(att_ps, 1)

                    score(0)
                    for u in range(2 * NT):
                        if u + 1 < 2 * NT:
                            score(u + 1)
                        turn(u)
                        if u % TB == TB - 1:
                            apply(u // TB)

                @block.vector
                def _(dve):
                    def sum_q(g):
                        r, b = divmod(g, B)
                        if g >= 2:
                            dve.wait_ge(score_ps, TB * (g - 1))
                        if r:
                            dve.wait_ge(add_sem, KD * (b + 1))
                        nc.vector.tensor_tensor(qsum[:, g % 2, :], cut(fused[:, 0, :], b), cut(fused[:, 1, :], b),
                                                ALU.add).then_inc(qsum_sem, 1)

                    def top_of(u):
                        dve.wait_ge(score_ps, u + 1)
                        nc.vector.tensor_reduce(mx[:, u:u + 1], c.bank[:, u % 2, :], AX.X,
                                                ALU.max).then_inc(max_sem, 1)
                        dve.wait_ge(max_sem, u + 1)
                        nc.vector.tensor_scalar(neg[:, u:u + 1], mx[:, u:u + 1], -inv_sqrt, None,
                                                ALU.mult).then_inc(neg_sem, 1)

                    def divide(u):
                        dve.wait_ge(exp_sem, u + 1)
                        nc.vector.reciprocal(rinv[:, u:u + 1], rsum[:, u:u + 1]).then_inc(inv_sem, 1)
                        dve.wait_ge(inv_sem, u + 1)
                        if u >= 2:
                            dve.wait_ge(turn_ps, u - 1)
                        nc.vector.tensor_scalar(probs[:, u % 2, :], ex[:, u % 2, :], rinv[:, u:u + 1], 0.1,
                                                ALU.mult, ALU.mult).then_inc(prob_sem, 1)

                    def add(g):
                        r, b = divmod(g, B)
                        dve.wait_ge(att_ps, g + 1)
                        for k in range(KD):
                            nc.vector.tensor_tensor(cut(fused[:, k, :], b), cut(fused[:, k, :], b),
                                                    c.bank[:, 6 + g % 2, :], ALU.add).then_inc(add_sem, 1)

                    sum_q(0)
                    top_of(0)
                    for u in range(2 * NT):
                        g = u // TB
                        if u % TB == 0 and g + 1 < 2 * B:
                            sum_q(g + 1)
                        if u + 1 < 2 * NT:
                            top_of(u + 1)
                        divide(u)
                        if u % TB == 1 and g >= 1:
                            add(g - 1)
                    add(2 * B - 1)

                @block.scalar
                def _(act):
                    def weigh(u):
                        act.wait_ge(neg_sem, u + 1)
                        if u >= 2:
                            act.wait_ge(prob_sem, u - 1)
                        nc.scalar.activation(ex[:, u % 2, :], c.bank[:, u % 2, :], ACT.Exp, bias=neg[:, u:u + 1],
                                             scale=inv_sqrt, accum_out=rsum[:, u:u + 1]).then_inc(exp_sem, 1)

                    def store(u):
                        g, i = divmod(u, TB)
                        act.wait_ge(turn_ps, u + 1)
                        if g >= 2:
                            act.wait_ge(att_ps, g - 1)
                        nc.scalar.activation(probs_f[:, g % 2, :, i * P:(i + 1) * P],
                                             c.bank[:, 2 + u % 2, :].rearrange("p (k q) -> p k q", k=TB),
                                             ACT.Copy).then_inc(turn_out, 1)

                    for u in range(2 * NT + 1):
                        if u < 2 * NT:
                            weigh(u)
                        if u >= 1:
                            store(u - 1)

        keys_ctx.close()
        with ExitStack() as ctx2:
            hid = c.sb(ctx2, "t_hid", [P, FX // P, N])
            qh = c.sb(ctx2, "t_qh", [P, FX // P, N], BF16)
            qf = c.sb(ctx2, "t_qf", [P, KD, N], BF16)
            qm = c.sb(ctx2, "t_qm", [P, KD * B], BF16)
            mb = c.sb(ctx2, "t_mb", [P, FX // P, B])
            MF = FX // P
            quantise_block(c, "tfq", [(cut(fused[:, k, :], b), cut(qf[:, k, :], b))
                                      for k in range(KD) for b in range(B)]
                           + [(mean_img[:, :, :].rearrange("p k b -> p (k b)"), qm[:, :])], scale, W_F1, scratch)
            mean_ps = c.sem("t_mean_ps")
            mean_bias = c.sem("t_mean_bias")
            with nc.Block() as block:
                @block.tensor
                def _(pe):
                    for m in range(MF):
                        for k in range(KD):
                            mm = nc.tensor.matmul(c.bank[:, m, 0:B], tern[W_F1][:, KD + k, m * P:(m + 1) * P],
                                                  qm[:, k * B:(k + 1) * B], start=(k == 0), stop=(k == KD - 1))
                        mm.then_inc(mean_ps, 1)

                @block.scalar
                def _(act):
                    for m in range(MF):
                        act.wait_ge(mean_ps, m + 1)
                        nc.scalar.activation(mb[:, m, :], c.bank[:, m, 0:B], ACT.Identity, bias=c.col("b_f1", m),
                                             scale=out_scale[:, 0:1]).then_inc(mean_bias, 1)

            product_block(c, "tf1", [([(tern[W_F1][:, k, m * P:(m + 1) * P], cut(qf[:, k, :], b))
                                       for k in range(KD)], cut(hid[:, m, :], b), mb[:, m, b:b + 1])
                                     for b in range(B) for m in range(MF)], out_scale, ACT.Relu)
            quantise_block(c, "thq", [(hid[:, m, :], qh[:, m, :]) for m in range(MF)], scale, W_F2, scratch)
            out_ps = c.sem("t_out_ps")
            off_sem = c.sem("t_offset")
            added = c.sem("t_added")
            with nc.Block() as block:
                @block.tensor
                def _(pe):
                    for t in range(NT):
                        if t >= 8:
                            pe.wait_ge(added, t - 7)
                        for m in range(MF):
                            mm = nc.tensor.matmul(c.bank[:, t % 8, 0:D], qh[:, m, t * P:(t + 1) * P],
                                                  tern[W_F2][:, m, :], start=(m == 0), stop=(m == MF - 1))
                        mm.then_inc(out_ps, 1)

                @block.gpsimd
                def _(pool):
                    for t in range(NT):
                        nc.gpsimd.tensor_tensor(c.X[:, t, :], c.X[:, t, :], c.row("b_f2"),
                                                ALU.add).then_inc(off_sem, 1)

                @block.vector
                def _(dve):
                    for t in range(NT):
                        dve.wait_ge(out_ps, t + 1)
                        dve.wait_ge(off_sem, t + 1)
                        nc.vector.scalar_tensor_tensor(out=c.X[:, t, :], in0=c.bank[:, t % 8, 0:D],
                                                       scalar=out_scale[:, 0:1], in1=c.X[:, t, :],
                                                       op0=ALU.mult, op1=ALU.add).then_inc(added, 1)


def linear_experts_blocks(c):
    nc, dram = c.nc, c.dram
    norm_block(c, "n5")
    HT = FF1 // P
    with ExitStack() as ctx:
        gates = route_block(c, ctx, "r1", NE, "e1_gate", False)
        w_in = c.sb(ctx, "e1_w_in", [P, 2, HT, D])
        w_out = c.sb(ctx, "e1_w_out", [P, 2, HT, D])
        comb = c.sb(ctx, "e1_comb", [P, KD, NE, D])
        in_in = [c.sem(f"e1_in_in{i}") for i in range(2)]
        out_in = [c.sem(f"e1_out_in{i}") for i in range(2)]
        comb_ps = c.sem("e1_comb_ps")
        comb_sem = c.sem("e1_comb_ready")
        out_ps = c.sem("e1_out_ps")
        added = c.sem("e1_added")
        NP = NE // 2
        with nc.Block() as block:
            @block.sync
            def _(sp):
                for e in range(NE):
                    if e >= 2:
                        sp.wait_ge(comb_ps, KD * (e - 1))
                    sp.dma_start(w_in[:, e % 2], dram["e1_w_in"][e]).then_inc(in_in[e % 2], 16)
                    sp.dma_start(w_out[:, e % 2], dram["e1_w_out"][e]).then_inc(out_in[e % 2], 16)
                for t in range(NT):
                    sp.wait_ge(added, NE * (t + 1))
                    sp.dma_start(dram["out"][t * P:(t + 1) * P, :], c.X[:, t, :]).then_inc(c.saved, 16)
                sp.wait_ge(c.saved, 16 * NT)

            @block.tensor
            def _(pe):
                for e in range(NE):
                    pe.wait_ge(in_in[e % 2], 16 * (e // 2 + 1))
                    pe.wait_ge(out_in[e % 2], 16 * (e // 2 + 1))
                    for k in range(KD):
                        u = KD * e + k
                        if u >= 2:
                            pe.wait_ge(comb_sem, u - 1)
                        for h in range(HT):
                            mm = nc.tensor.matmul(c.bank[:, u % 2, 0:D], w_in[:, e % 2, h, k * P:(k + 1) * P],
                                                  w_out[:, e % 2, h, :], start=(h == 0), stop=(h == HT - 1))
                        mm.then_inc(comb_ps, 1)
                pe.wait_ge(comb_sem, KD * NE)
                for t in range(NT):
                    for p in range(NP):
                        n = NP * t + p
                        if n >= 6:
                            pe.wait_ge(added, 2 * (n - 5))
                        for k in range(KD):
                            mm = nc.tensor.matmul(c.bank[:, 2 + n % 6, :], c.xn_f[:, k, t * P:(t + 1) * P],
                                                  comb[:, k, 2 * p:2 * p + 2, :], start=(k == 0),
                                                  stop=(k == KD - 1))
                        mm.then_inc(out_ps, 1)

            @block.scalar
            def _(act):
                for u in range(KD * NE):
                    e, k = divmod(u, KD)
                    act.wait_ge(comb_ps, u + 1)
                    nc.scalar.activation(comb[:, k, e, :], c.bank[:, u % 2, 0:D], ACT.Copy).then_inc(comb_sem, 1)

            @block.vector
            def _(dve):
                for t in range(NT):
                    for e in range(NE):
                        n = NP * t + e // 2
                        dve.wait_ge(out_ps, n + 1)
                        if e:
                            dve.wait_ge(added, NE * t + e)
                        nc.vector.scalar_tensor_tensor(out=c.X[:, t, :],
                                                       in0=c.bank[:, 2 + n % 6, (e % 2) * D:(e % 2) * D + D],
                                                       scalar=gates[:, t, e:e + 1], in1=c.X[:, t, :],
                                                       op0=ALU.mult, op1=ALU.add).then_inc(added, 1)


def decoder_kernel(nc, dram):
    with ExitStack() as ctx:
        c = Core(nc, ctx, dram)
        load_block(c)
        attention_blocks(c)
        c.end_section()
        cross_attention_blocks(c)
        c.end_section()
        experts_blocks(c)
        c.end_section()
        gru_blocks(c)
        c.end_section()
        ternary_cross_blocks(c)
        c.end_section()
        linear_experts_blocks(c)


def _tiles(w, p=P):
    return w.reshape(w.shape[0] // p, p, *w.shape[1:]).swapaxes(0, 1)


def _layout(i):
    a = {k: np.asarray(v) for k, v in i.items()}
    f = np.float32
    cols = np.zeros((P, N_COLS), f)

    def put(name, v):
        lo, hi = COLS[name]
        cols[:v.shape[0], lo:hi] = v

    put("conv_w", a["L0_attn_conv_w"].reshape(KD, P, 4).swapaxes(0, 1).reshape(P, KD * 4))
    for name, key in (("conv_b", "L0_attn_conv_b"), ("g_b", "L0_attn_g_b"), ("bq", "L0_xattn_bq"),
                      ("bk", "L0_xattn_bk"), ("bv", "L0_xattn_bv"), ("b_f", "L1_attn_b_f"),
                      ("b_d2v", "L1_xattn_b_d2v"), ("b_img", "L1_xattn_b_img"), ("b_txt", "L1_xattn_b_txt"),
                      ("b_att0", "L1_xattn_b_att0"), ("b_att1", "L1_xattn_b_att1"), ("b_f1", "L1_xattn_b_f1")):
        put(name, a[key].reshape(-1, P).T)
    put("freqs", a["L0_attn_freqs"].reshape(-1, P).T)
    put("gamma", a["L0_attn_gamma"].reshape(H0, 1))
    rows = np.zeros((P, N_ROWS), f)
    for name, v in (("ln_g", a["L0_attn_ln_g"]), ("ln_b", a["L0_attn_ln_b"]), ("bo", a["L0_xattn_bo"]),
                    ("b_f2", a["L1_xattn_b_f2"]), ("expert_bias", a["L0_ffn_expert_bias"]),
                    ("steps", np.arange(T, dtype=f)), ("expert_index", np.arange(NE_ALL, dtype=f))):
        lo, hi = ROWS[name]
        rows[:, lo:hi] = np.broadcast_to(v, (P, hi - lo))
    head_in = np.zeros((P, ET, 32), f)
    head_out = np.zeros((P, ET, P), f)
    per = E0 // H0
    for e in range(ET):
        for p in range(P):
            h = (e * P + p) // per
            head_in[p, e, h] = 1.0
            for g in range(P // 32):
                head_out[32 * g + h, e, p] = 1.0
    return {
        "x": a["x"].reshape(N, D),
        "columns": cols,
        "rows": rows,
        "ident": np.eye(P, dtype=f),
        "head_in": head_in,
        "head_out": head_out,
        "a0_wq": _tiles(a["L0_attn_qk_w"].T),
        "a0_wv": _tiles(a["L0_attn_v_w"].T),
        "a0_wg": _tiles(a["L0_attn_g_w"].T),
        "a0_wo": _tiles(a["L0_attn_o_w"].T),
        "ctx_f": _tiles(a["ctx_768"].reshape(N, CTX).T, CK),
        "x_wq": _tiles(a["L0_xattn_Wq"]),
        "x_wk": _tiles(a["L0_xattn_Wk"], CK),
        "x_wv": _tiles(a["L0_xattn_Wv"], CK),
        "x_wo": _tiles(a["L0_xattn_Wo"]),
        "e0_gate": _tiles(a["L0_ffn_gate_w"].T),
        "e0_w1": np.stack([_tiles(w.T) for w in a["L0_ffn_w1"]]),
        "e0_w2": np.stack([_tiles(w.T) for w in a["L0_ffn_w2"]]),
        "g_wf": _tiles(a["L1_attn_W_f"].T),
        "g_wd": _tiles(a["L1_attn_W_down"].T),
        "t_d2v": _tiles(a["L1_xattn_W_d2v"].T, CK),
        "t_img": _tiles(a["L1_xattn_W_img"].T),
        "t_txt": _tiles(a["L1_xattn_W_txt"].T),
        "t_att0": _tiles(a["L1_xattn_W_att0"].T),
        "t_att1": _tiles(a["L1_xattn_W_att1"].T),
        "t_f1": _tiles(a["L1_xattn_W_f1"].T),
        "t_f2": _tiles(a["L1_xattn_W_f2"].T),
        "e1_gate": _tiles(a["L1_ffn_w_gate"].T),
        "e1_w_in": np.stack([_tiles(w) for w in a["L1_ffn_w_in"]]),
        "e1_w_out": np.stack([_tiles(w.T) for w in a["L1_ffn_w_out"]]),
    }


def kernel(**inputs):
    import concourse.bacc as _bacc
    from concourse.bass_utils import run_bass_kernel_spmd as _run

    nc = _bacc.Bacc("TRN2", target_bir_lowering=False, num_devices=1)
    arrays, dram = {}, {}
    for name, v in _layout(inputs).items():
        v = np.ascontiguousarray(v)
        arrays[f"in_{name}_dram"] = v
        dram[name] = nc.dram_tensor(f"in_{name}_dram", v.shape, mybir.dt.from_np(v.dtype), kind="ExternalInput").ap()
    dram["out"] = nc.dram_tensor("out_dram", (N, D), F32, kind="ExternalOutput").ap()
    dram["split"] = nc.dram_tensor("split_scratch", (2, 3, D, N), BF16, kind="Internal").ap()
    dram["negmax"] = nc.dram_tensor("negmax_scratch", (B, 3, HX * TB, P), BF16, kind="Internal").ap()
    decoder_kernel(nc, dram)
    r = _run(nc, [arrays], core_ids=[0])
    return r.results[0]["out_dram"].reshape(B, T, D)
```

```python
from contextlib import ExitStack

import numpy as np
import concourse.bass as bass
from concourse import mybir

F32 = mybir.dt.float32
BF16 = mybir.dt.bfloat16
F32R = mybir.dt.float32r
ALU = mybir.AluOpType
ACT = mybir.ActivationFunctionType
AX = mybir.AxisListType
RED = bass.bass_isa.ReduceOp

P = 128
B = 4
T = 512
N = B * T
NT = N // P
TB = T // P
D = 256
KD = D // P
E0 = 512
ET = E0 // P
H0 = 16
HX = 16
DX = D // HX
CTX = 192
CK = CTX // 2
NE = 8
NE_ALL = 12
FF0 = 512
FF1 = 1024
EG = 384
GT = EG // P
FX = 1024
CLAMP = 10000.0
MAGIC = 12582912.0
TWO_PI_HI = 6.28125
TWO_PI_MID = 0.0019350051879882812
TWO_PI_LO = 2.0 * np.pi - TWO_PI_HI - TWO_PI_MID
EPS = 1e-5

COLS = {}
_at = 0
for _name, _n in (("conv_w", KD * 4), ("conv_b", KD), ("g_b", ET), ("freqs", ET), ("bq", KD), ("bk", KD),
                  ("bv", KD), ("b_f", 2 * GT), ("b_d2v", KD), ("b_img", KD), ("b_txt", KD), ("b_att0", 1),
                  ("b_att1", 1), ("b_f1", FX // P), ("gamma", 1)):
    COLS[_name] = (_at, _at + _n)
    _at += _n
N_COLS = _at
ROWS = {}
_at = 0
for _name, _n in (("ln_g", D), ("ln_b", D), ("bo", D), ("b_f2", D), ("expert_bias", NE_ALL),
                  ("steps", T), ("expert_index", NE_ALL)):
    ROWS[_name] = (_at, _at + _n)
    _at += _n
N_ROWS = _at


class Core:

    def __init__(self, nc, ctx, dram):
        self.nc, self.ctx, self.dram = nc, ctx, dram
        self.tallies = {}
        self.section_sems = []
        self.saved = nc.alloc_semaphore(name="saved")
        self.bank = ctx.enter_context(nc.psum_tensor("bank", [P, 8, 512], F32))
        self.X = self.sb(ctx, "X", [P, NT, D])
        self.xn = self.sb(ctx, "xn", [P, NT, D])
        self.xn_f = self.sb(ctx, "xn_f", [P, KD, N])
        self.ident = self.sb(ctx, "ident", [P, P])
        self.cols = self.sb(ctx, "cols", [P, N_COLS])
        self.rows = self.sb(ctx, "rows", [P, N_ROWS])
        self.eps = self.sb(ctx, "eps", [P, 1])

    def sb(self, ctx, name, shape, dt=F32):
        return ctx.enter_context(self.nc.sbuf_tensor(name, shape, dt))

    def sem(self, name):
        handle = self.nc.alloc_semaphore(name=name)
        self.section_sems.append(handle)
        return handle

    def end_section(self):
        self.nc.clear_and_free_semaphores(self.section_sems)
        self.section_sems = []
        self.nc.all_engine_barrier()

    def tally(self, name, total):
        if name not in self.tallies:
            self.tallies[name] = [self.nc.alloc_semaphore(name=name), 0]
        sem, before = self.tallies[name]
        self.tallies[name][1] += total
        return sem, before

    def col(self, name, i=0, n=1, p=P):
        a = COLS[name][0] + i
        return self.cols[0:p, a:a + n]

    def row(self, name):
        a, b = ROWS[name]
        return self.rows[:, a:b]


def load_block(c):
    nc = c.nc
    loaded = c.sem("loaded")
    eps_set = c.sem("eps_set")
    with nc.Block() as block:
        @block.sync
        def _(sp):
            sp.dma_start(c.X[:, :, :], c.dram["x"].rearrange("(t p) d -> p t d", p=P)).then_inc(loaded, 16)
            sp.dma_start(c.ident[:, :], c.dram["ident"]).then_inc(loaded, 16)
            sp.dma_start(c.cols[:, :], c.dram["columns"]).then_inc(loaded, 16)
            sp.dma_start(c.rows[:, :], c.dram["rows"]).then_inc(loaded, 16)
            sp.wait_ge(loaded, 64)

        @block.vector
        def _(dve):
            nc.vector.memset(c.eps[:, :], EPS).then_inc(eps_set, 1)


def norm_block(c, tag, put=None):
    nc = c.nc
    if put is None:
        def put(k, b):
            return c.xn_f[:, k, b * T:(b + 1) * T]
    moments_in, moments_in0 = c.tally("norm_moments_in", NT)
    moments, moments0 = c.tally("norm_moments", NT)
    std, std0 = c.tally("norm_std", B)
    rstd, rstd0 = c.tally("norm_rstd", B)
    normed, normed0 = c.tally("norm_normed", NT)
    turned, turned0 = c.tally("norm_turned", KD * B)
    stored, stored0 = c.tally("norm_stored", KD * B)
    with ExitStack() as ctx:
        parts = c.sb(ctx, tag + "_parts", [P, NT, 6])
        mom = c.sb(ctx, tag + "_mom", [P, NT, 2])
        sd = c.sb(ctx, tag + "_sd", [P, NT])
        rs = c.sb(ctx, tag + "_rs", [P, NT])
        with nc.Block() as block:
            @block.vector
            def _(dve):
                def stats(b):
                    for t in range(TB * b, TB * b + TB):
                        nc.vector.bn_stats(parts[:, t, :], c.X[:, t, :]).then_inc(moments_in, 1)
                    for t in range(TB * b, TB * b + TB):
                        dve.wait_ge(moments_in, moments_in0 + t + 1)
                        nc.vector.bn_aggr(mom[:, t, :], parts[:, t, :]).then_inc(moments, 1)

                def scale(b):
                    dve.wait_ge(std, std0 + b + 1)
                    nc.vector.reciprocal(rs[:, TB * b:TB * b + TB], sd[:, TB * b:TB * b + TB]).then_inc(rstd, 1)
                    dve.wait_ge(rstd, rstd0 + b + 1)
                    for t in range(TB * b, TB * b + TB):
                        nc.vector.tensor_scalar(c.xn[:, t, :], c.X[:, t, :], mom[:, t, 0:1], rs[:, t:t + 1],
                                                ALU.subtract, ALU.mult).then_inc(normed, 1)

                stats(0)
                for b in range(B):
                    if b + 1 < B:
                        stats(b + 1)
                    scale(b)

            @block.scalar
            def _(act):
                def root(b):
                    act.wait_ge(moments, moments0 + TB * (b + 1))
                    nc.scalar.activation(sd[:, TB * b:TB * b + TB], mom[:, TB * b:TB * b + TB, 1], ACT.Sqrt,
                                         bias=c.eps[:, 0:1]).then_inc(std, 1)

                root(0)
                for b in range(B):
                    if b + 1 < B:
                        root(b + 1)
                    for k in range(KD):
                        act.wait_ge(turned, turned0 + KD * b + k + 1)
                        src = c.bank[:, KD * b + k, :]
                        if len(put(k, b).shape) == 3:
                            src = src.rearrange("p (a t) -> p a t", a=1)
                        nc.scalar.activation(put(k, b), src, ACT.Copy).then_inc(stored, 1)

            @block.tensor
            def _(pe):
                for b in range(B):
                    pe.wait_ge(normed, normed0 + TB * (b + 1))
                    for k in range(KD):
                        for i in range(TB):
                            tr = nc.tensor.transpose(c.bank[:, KD * b + k, i * P:(i + 1) * P],
                                                     c.xn[:, TB * b + i, k * P:(k + 1) * P], c.ident[:, :])
                        tr.then_inc(turned, 1)


def attention_blocks(c):
    nc, dram = c.nc, c.dram
    with ExitStack() as ctx:
        wo = c.sb(ctx, "a0_wo", [P, ET, D])
        wq = c.sb(ctx, "a0_wq", [P, KD, E0])
        wv = c.sb(ctx, "a0_wv", [P, KD, E0])
        wg = c.sb(ctx, "a0_wg", [P, KD, E0])
        head_in = c.sb(ctx, "a0_head_in", [P, ET, 32])
        head_out = c.sb(ctx, "a0_head_out", [P, ET, P])
        xc = c.sb(ctx, "a0_xc", [P, KD, B, T])
        cos = c.sb(ctx, "a0_cos", [P, ET, T])
        decay = c.sb(ctx, "a0_decay", [P, ET, T])
        undecay = c.sb(ctx, "a0_undecay", [P, ET, T])
        gate = c.sb(ctx, "a0_gate", [P, ET, B, T])
        half_pi = c.sb(ctx, "a0_half_pi", [P, 1])
        with ExitStack() as ctx2:
            xpad = c.sb(ctx2, "a0_xpad", [P, KD, B, 3 + T])
            pad_set = c.sem("a0_pad_set")
            with nc.Block() as block:
                @block.gpsimd
                def _(pool):
                    nc.gpsimd.memset(xpad[:, :, :, 0:3], 0.0).then_inc(pad_set, 1)
            norm_block(c, "n0", lambda k, b: xpad[:, k, b:b + 1, 3:3 + T])

            weights = c.sem("a0_weights")
            conv_sem = c.sem("a0_conv")
            angle_sem = c.sem("a0_angle")
            abs_sem = c.sem("a0_angle_abs")
            cos_sem = c.sem("a0_cos_ready")
            decay_rows = c.sem("a0_decay_rows")
            spread = c.sem("a0_spread")
            spread_used = c.sem("a0_spread_used")
            ang = c.sb(ctx2, "a0_ang", [P, ET, T])
            turns = c.sb(ctx2, "a0_turns", [P, ET, T])
            gam = c.sb(ctx2, "a0_gam", [32, T])
            dec = c.sb(ctx2, "a0_dec", [32, 2, T])
            dece = c.sb(ctx2, "a0_dece", [32, T])
            zero = c.sb(ctx2, "a0_zero", [32, T])
            with nc.Block() as block:
                @block.sync
                def _(sp):
                    for dst, name in ((wq, "a0_wq"), (wv, "a0_wv"), (wg, "a0_wg"), (wo, "a0_wo"),
                                      (head_in, "head_in"), (head_out, "head_out")):
                        sp.dma_start(dst[:, :, :], dram[name]).then_inc(weights, 16)
                    sp.wait_ge(weights, 96)

                @block.vector
                def _(dve):
                    nc.vector.memset(zero[:, :], 0.0).then_inc(decay_rows, 1)
                    nc.vector.memset(dec[:, 0, 0:1], 1.0).then_inc(decay_rows, 1)
                    nc.vector.memset(half_pi[:, :], float(np.pi / 2)).then_inc(decay_rows, 1)
                    dve.wait_ge(decay_rows, 3)
                    nc.vector.tensor_scalar(gam[:, :], zero[:, :], c.col("gamma", p=32), None,
                                            ALU.add).then_inc(decay_rows, 1)
                    dve.wait_ge(decay_rows, 4)
                    nc.vector.tensor_tensor_scan(dec[:, 0, 1:T], gam[:, 1:T], zero[:, 1:T], 1.0,
                                                 ALU.mult, ALU.add).then_inc(decay_rows, 1)
                    dve.wait_ge(decay_rows, 5)
                    nc.vector.tensor_scalar(dece[:, :], dec[:, 0, :], 1e-6, None, ALU.add).then_inc(decay_rows, 1)
                    dve.wait_ge(decay_rows, 6)
                    nc.vector.reciprocal(dec[:, 1, :], dece[:, :]).then_inc(decay_rows, 1)
                    for e in range(ET):
                        nc.vector.tensor_scalar(ang[:, e, :], c.row("steps"), c.col("freqs", e), None,
                                                ALU.mult).then_inc(angle_sem, 1)
                    dve.wait_ge(angle_sem, ET)
                    nc.vector.tensor_scalar(turns[:, :, :], ang[:, :, :], float(0.5 / np.pi), MAGIC,
                                            ALU.mult, ALU.add).then_inc(angle_sem, 1)
                    dve.wait_ge(angle_sem, ET + 1)
                    nc.vector.tensor_scalar(turns[:, :, :], turns[:, :, :], MAGIC, None,
                                            ALU.subtract).then_inc(angle_sem, 1)
                    for i, part in enumerate((TWO_PI_HI, TWO_PI_MID, TWO_PI_LO)):
                        dve.wait_ge(angle_sem, ET + 2 + i)
                        nc.vector.scalar_tensor_tensor(out=ang[:, :, :], in0=turns[:, :, :], scalar=-float(part),
                                                       in1=ang[:, :, :], op0=ALU.mult,
                                                       op1=ALU.add).then_inc(angle_sem, 1)
                    for k in range(KD):
                        nc.vector.tensor_scalar(xc[:, k], xpad[:, k, :, 3:3 + T], c.col("conv_w", 4 * k + 3),
                                                c.col("conv_b", k), ALU.mult, ALU.add).then_inc(conv_sem, 1)
                    for j in range(3):
                        for k in range(KD):
                            dve.wait_ge(conv_sem, KD * j + k + 1)
                            nc.vector.scalar_tensor_tensor(out=xc[:, k], in0=xpad[:, k, :, j:j + T],
                                                           scalar=c.col("conv_w", 4 * k + j), in1=xc[:, k],
                                                           op0=ALU.mult, op1=ALU.add).then_inc(conv_sem, 1)

                @block.tensor
                def _(pe):
                    pe.wait_ge(decay_rows, 7)
                    pe.wait_ge(weights, 96)
                    for w in range(2):
                        for e in range(ET):
                            nc.tensor.matmul(c.bank[:, ET * w + e, :], head_out[0:32, e, :], dec[:, w, :],
                                             start=True, stop=True).then_inc(spread, 1)

                @block.scalar
                def _(act):
                    for w, dst in enumerate((decay, undecay)):
                        for e in range(ET):
                            act.wait_ge(spread, ET * w + e + 1)
                            nc.scalar.activation(dst[:, e, :], c.bank[:, ET * w + e, :],
                                                 ACT.Copy).then_inc(spread_used, 1)
                    act.wait_ge(angle_sem, ET + 5)
                    nc.scalar.activation(turns[:, :, :], ang[:, :, :], ACT.Abs).then_inc(abs_sem, 1)
                    act.wait_ge(abs_sem, 1)
                    nc.scalar.activation(cos[:, :, :], turns[:, :, :], ACT.Sin, bias=half_pi[:, 0:1],
                                         scale=-1.0).then_inc(cos_sem, 1)

        gate_ps = c.sem("a0_gate_ps")
        gate_sem = c.sem("a0_gate_ready")
        decayed = c.sem("a0_gate_decayed")
        with nc.Block() as block:
            @block.tensor
            def _(pe):
                for u in range(B * ET):
                    b, e = divmod(u, ET)
                    if u >= 8:
                        pe.wait_ge(gate_sem, u - 7)
                    for k in range(KD):
                        mm = nc.tensor.matmul(c.bank[:, u % 8, :], wg[:, k, e * P:(e + 1) * P], xc[:, k, b, :],
                                              start=(k == 0), stop=(k == KD - 1))
                    mm.then_inc(gate_ps, 1)

            @block.scalar
            def _(act):
                for u in range(B * ET):
                    b, e = divmod(u, ET)
                    act.wait_ge(gate_ps, u + 1)
                    nc.scalar.activation(gate[:, e, b, :], c.bank[:, u % 8, :], ACT.Sigmoid,
                                         bias=c.col("g_b", e)).then_inc(gate_sem, 1)

            @block.gpsimd
            def _(pool):
                for u in range(B * ET):
                    b, e = divmod(u, ET)
                    pool.wait_ge(gate_sem, u + 1)
                    nc.gpsimd.tensor_tensor(gate[:, e, b, :], gate[:, e, b, :], decay[:, e, :],
                                            ALU.mult).then_inc(decayed, 1)

        with ExitStack() as ctx2:
            qk = c.sb(ctx2, "a0_qk", [P, ET, B, 1 + T])
            sq = c.xn_f[:, :, :].rearrange("p k (e t) -> p k e t", e=ET)
            nrm = c.sb(ctx2, "a0_nrm", [P, T])
            rnrm = c.sb(ctx2, "a0_rnrm", [P, T])
            s1, s2, s3, w1 = (c.xn[:, 4 * i:4 * i + 4, :].rearrange("p (s a) d -> p s (a d)", s=2)
                              for i in range(4))
            q_ps = c.sem("a0_q_ps")
            q_zero = c.sem("a0_q_zero")
            q_copy = c.sem("a0_q_copy")
            q_square = c.sem("a0_q_square")
            norm_ps = c.sem("a0_norm_ps")
            norm_root = c.sem("a0_norm_root")
            norm_clip = c.sem("a0_norm_clip")
            norm_inv = c.sem("a0_norm_inv")
            inv_ps = c.sem("a0_inv_ps")
            q_normed = c.sem("a0_q_normed")
            v_ps = c.sem("a0_v_ps")
            phase_sum = c.sem("a0_phase_sum")
            valued = c.sem("a0_valued")
            gated = c.sem("a0_gated")
            scanned = c.sem("a0_scanned")
            undecayed = c.sem("a0_undecayed")
            mixed = c.sem("a0_mixed")
            U = B * ET
            with nc.Block() as block:
                @block.tensor
                def _(pe):
                    for b in range(B):
                        for e in range(ET):
                            u = ET * b + e
                            if u >= 4:
                                pe.wait_ge(q_square, u - 3)
                                pe.wait_ge(q_copy, u - 3)
                            for k in range(KD):
                                mm = nc.tensor.matmul(c.bank[:, u % 4, :], wq[:, k, e * P:(e + 1) * P],
                                                      xc[:, k, b, :], start=(k == 0), stop=(k == KD - 1))
                            mm.then_inc(q_ps, 1)
                        for e in range(ET):
                            pe.wait_ge(q_square, ET * b + e + 1)
                            mm = nc.tensor.matmul(c.bank[32 * b:32 * b + 32, 4, :], head_in[:, e, :],
                                                  sq[:, b % 2, e, :], start=(e == 0), stop=(e == ET - 1))
                        mm.then_inc(norm_ps, 1)
                    pe.wait_ge(norm_inv, 1)
                    for u in range(U):
                        b, e = divmod(u, ET)
                        if u >= 4:
                            pe.wait_ge(q_normed, u - 3)
                        nc.tensor.matmul(c.bank[:, u % 4, :], head_out[32 * b:32 * b + 32, e, :],
                                         rnrm[32 * b:32 * b + 32, :], start=True, stop=True).then_inc(inv_ps, 1)
                        if u >= 3:
                            pe.wait_ge(valued, u - 2)
                        for k in range(KD):
                            mm = nc.tensor.matmul(c.bank[:, 5 + u % 3, :], wv[:, k, e * P:(e + 1) * P],
                                                  xc[:, k, b, :], start=(k == 0), stop=(k == KD - 1))
                        mm.then_inc(v_ps, 1)

                @block.scalar
                def _(act):
                    for b in range(B):
                        for e in range(ET):
                            u = ET * b + e
                            act.wait_ge(q_ps, u + 1)
                            nc.scalar.activation(qk[:, e, b, 1:1 + T], c.bank[:, u % 4, :],
                                                 ACT.Copy).then_inc(q_copy, 1)
                            if b >= 2:
                                act.wait_ge(norm_ps, b - 1)
                            nc.scalar.activation(sq[:, b % 2, e, :], c.bank[:, u % 4, :],
                                                 ACT.Square).then_inc(q_square, 1)
                    act.wait_ge(norm_ps, B)
                    nc.scalar.activation(nrm[:, :], c.bank[:, 4, :], ACT.Sqrt).then_inc(norm_root, 1)

                @block.vector
                def _(dve):
                    dve.wait_ge(norm_root, 1)
                    nc.vector.tensor_scalar(nrm[:, :], nrm[:, :], 1e-12, None, ALU.max).then_inc(norm_clip, 1)
                    dve.wait_ge(norm_clip, 1)
                    nc.vector.reciprocal(rnrm[:, :], nrm[:, :]).then_inc(norm_inv, 1)

                    def unit_q(u):
                        b, e = divmod(u, ET)
                        dve.wait_ge(inv_ps, u + 1)
                        dve.wait_ge(q_copy, u + 1)
                        nc.vector.tensor_tensor(qk[:, e, b, 1:1 + T], qk[:, e, b, 1:1 + T], c.bank[:, u % 4, :],
                                                ALU.mult).then_inc(q_normed, 1)

                    def unit_v(u):
                        dve.wait_ge(v_ps, u + 1)
                        dve.wait_ge(phase_sum, u + 1)
                        if u >= 2:
                            dve.wait_ge(gated, u - 1)
                        nc.vector.tensor_tensor(s2[:, u % 2, :], c.bank[:, 5 + u % 3, :], s1[:, u % 2, :],
                                                ALU.mult).then_inc(valued, 1)

                    def unit_scan(u):
                        b, e = divmod(u, ET)
                        dve.wait_ge(gated, u + 1)
                        nc.vector.tensor_tensor_scan(gate[:, e, b, :], s3[:, u % 2, :], s3[:, u % 2, :], 0.0,
                                                     ALU.add, ALU.bypass).then_inc(scanned, 1)

                    def unit_mix(u):
                        b, e = divmod(u, ET)
                        dve.wait_ge(scanned, u + 1)
                        dve.wait_ge(undecayed, u + 1)
                        nc.vector.tensor_tensor(gate[:, e, b, :], gate[:, e, b, :], w1[:, u % 2, :],
                                                ALU.mult).then_inc(mixed, 1)

                    for i in range(U + 2):
                        if i < U:
                            unit_q(i)
                        if 1 <= i <= U:
                            unit_v(i - 1)
                        if i >= 2:
                            unit_scan(i - 2)
                            unit_mix(i - 2)

                @block.gpsimd
                def _(pool):
                    nc.gpsimd.memset(qk[:, :, :, 0:1], 0.0).then_inc(q_zero, 1)
                    pool.wait_ge(q_zero, 1)

                    def unit_phase(u):
                        b, e = divmod(u, ET)
                        pool.wait_ge(q_normed, u + 1)
                        if u >= 2:
                            pool.wait_ge(valued, u - 1)
                        nc.gpsimd.tensor_tensor(s1[:, u % 2, :], cos[:, e, :], qk[:, e, b, 0:T],
                                                ALU.add).then_inc(phase_sum, 1)

                    def unit_gate(u):
                        b, e = divmod(u, ET)
                        pool.wait_ge(valued, u + 1)
                        if u >= 2:
                            pool.wait_ge(scanned, u - 1)
                        nc.gpsimd.tensor_tensor(s3[:, u % 2, :], s2[:, u % 2, :], gate[:, e, b, :],
                                                ALU.mult).then_inc(gated, 1)
                        if u >= 2:
                            pool.wait_ge(mixed, u - 1)
                        nc.gpsimd.tensor_tensor(w1[:, u % 2, :], qk[:, e, b, 1:1 + T], undecay[:, e, :],
                                                ALU.mult).then_inc(undecayed, 1)

                    for i in range(U + 1):
                        if i < U:
                            unit_phase(i)
                        if i >= 1:
                            unit_gate(i - 1)

        with ExitStack() as ctx2:
            parts = c.sb(ctx2, "a0_parts", [P, NT, 6])
            mom = c.sb(ctx2, "a0_mom", [P, NT, 2])
            sd = c.sb(ctx2, "a0_sd", [P, NT])
            rs = c.sb(ctx2, "a0_rs", [P, NT])
            y = c.sb(ctx2, "a0_y", [P, NT, D])
            out_ps = c.sem("a0_out_ps")
            parts_sem = c.sem("a0_parts_in")
            mom_sem = c.sem("a0_mom_in")
            std_sem = c.sem("a0_std")
            rstd_sem = c.sem("a0_rstd")
            y_sem = c.sem("a0_y_ready")
            gain_sem = c.sem("a0_gain")
            off_sem = c.sem("a0_offset")
            added = c.sem("a0_added")

            def out(t):
                return c.bank[:, t % 8, 0:D]

            with nc.Block() as block:
                @block.tensor
                def _(pe):
                    for t in range(NT):
                        b, i = divmod(t, TB)
                        if t >= 8:
                            pe.wait_ge(y_sem, t - 7)
                        for e in range(ET):
                            mm = nc.tensor.matmul(out(t), gate[:, e, b, i * P:(i + 1) * P], wo[:, e, :],
                                                  start=(e == 0), stop=(e == ET - 1))
                        mm.then_inc(out_ps, 1)

                @block.scalar
                def _(act):
                    for b in range(B):
                        act.wait_ge(mom_sem, TB * (b + 1))
                        nc.scalar.activation(sd[:, TB * b:TB * b + TB], mom[:, TB * b:TB * b + TB, 1], ACT.Sqrt,
                                             bias=c.eps[:, 0:1]).then_inc(std_sem, 1)

                @block.vector
                def _(dve):
                    for b in range(B):
                        ts = range(TB * b, TB * b + TB)
                        for t in ts:
                            dve.wait_ge(out_ps, t + 1)
                            nc.vector.bn_stats(parts[:, t, :], out(t)).then_inc(parts_sem, 1)
                        for t in ts:
                            dve.wait_ge(parts_sem, t + 1)
                            nc.vector.bn_aggr(mom[:, t, :], parts[:, t, :]).then_inc(mom_sem, 1)
                        dve.wait_ge(std_sem, b + 1)
                        nc.vector.reciprocal(rs[:, TB * b:TB * b + TB],
                                             sd[:, TB * b:TB * b + TB]).then_inc(rstd_sem, 1)
                        dve.wait_ge(rstd_sem, b + 1)
                        for t in ts:
                            nc.vector.tensor_scalar(y[:, t, :], out(t), mom[:, t, 0:1], rs[:, t:t + 1],
                                                    ALU.subtract, ALU.mult).then_inc(y_sem, 1)

                @block.gpsimd
                def _(pool):
                    for t in range(NT):
                        nc.gpsimd.tensor_tensor(c.X[:, t, :], c.X[:, t, :], c.row("ln_b"),
                                                ALU.add).then_inc(off_sem, 1)
                    for t in range(NT):
                        pool.wait_ge(y_sem, t + 1)
                        nc.gpsimd.tensor_tensor(y[:, t, :], y[:, t, :], c.row("ln_g"),
                                                ALU.mult).then_inc(gain_sem, 1)
                        pool.wait_ge(gain_sem, t + 1)
                        pool.wait_ge(off_sem, t + 1)
                        nc.gpsimd.tensor_tensor(c.X[:, t, :], c.X[:, t, :], y[:, t, :],
                                                ALU.add).then_inc(added, 1)


HG = 4
STACKS = 3
LAG = HX + 3
SPLIT_Q = (0, 0, 1, 0, 2, 1)
SPLIT_K = (0, 1, 0, 2, 0, 1)
NS = len(SPLIT_Q)
KS = NS * DX
RM = KS


def cross_attention_blocks(c):
    nc, dram = c.nc, c.dram
    norm_block(c, "n1")
    with ExitStack() as ctx:
        values = c.sb(ctx, "x_values", [P, NT, HX, 32])
        O = c.xn
        with ExitStack() as ctx2:
            wq = c.sb(ctx2, "x_wq", [P, KD, D])
            wk = c.sb(ctx2, "x_wk", [CK, 2, D])
            wv = c.sb(ctx2, "x_wv", [CK, 2, D])
            ctx_f = c.sb(ctx2, "x_ctx", [CK, 2, N])
            full = c.sb(ctx2, "x_full", [P, 4, T])
            rest = c.sb(ctx2, "x_rest", [P, 4, T])
            parts = c.sb(ctx2, "x_split", [P, 2, 3, KD, N], BF16)
            bq4 = c.sb(ctx2, "x_bq4", [P, KD])
            weights = c.sem("x_weights")
            ones_set = c.sem("x_ones_set")
            bq_sem = c.sem("x_bq4_ready")
            proj_ps = c.sem("x_proj_ps")
            full_sem = c.sem("x_full_ready")
            high = c.sem("x_high")
            rest1 = c.sem("x_rest_ready")
            mid = c.sem("x_mid")
            low = c.sem("x_low")
            v_ps = c.sem("x_v_ps")
            v_sem = c.sem("x_v_ready")
            spilled = c.sem("x_spilled")
            U = 2 * B * KD

            def place(u):
                b, r = divmod(u, 2 * KD)
                w, m = divmod(r, KD)
                return b, w, m

            with nc.Block() as block:
                @block.sync
                def _(sp):
                    for dst, name in ((wq, "x_wq"), (wk, "x_wk"), (wv, "x_wv"), (ctx_f, "ctx_f")):
                        sp.dma_start(dst[:, :, :], dram[name]).then_inc(weights, 16)
                    for b in range(B):
                        sp.wait_ge(low, 2 * KD * (b + 1))
                        sp.wait_ge(mid, 2 * KD * (b + 1))
                        sp.wait_ge(high, 2 * KD * (b + 1))
                        for w in range(2):
                            for s in range(3):
                                for m in range(KD):
                                    sp.dma_start(dram["split"][w, s, m * P:(m + 1) * P, b * T:(b + 1) * T],
                                                 parts[:, w, s, m, b * T:(b + 1) * T]).then_inc(spilled, 16)
                    sp.wait_ge(spilled, 16 * 6 * KD * B)

                @block.tensor
                def _(pe):
                    pe.wait_ge(weights, 64)
                    for u in range(U):
                        b, w, m = place(u)
                        if u >= 4:
                            pe.wait_ge(high, u - 3)
                        for k in range(2):
                            lhs = (wq, wk)[w][:, k, m * P:(m + 1) * P]
                            rhs = (c.xn_f, ctx_f)[w][:, k, b * T:(b + 1) * T]
                            mm = nc.tensor.matmul(c.bank[:, u % 4, :], lhs, rhs, start=(k == 0), stop=(k == 1))
                        mm.then_inc(proj_ps, 1)
                        t = u
                        if t >= 4:
                            pe.wait_ge(v_sem, t - 3)
                        for k in range(2):
                            mm = nc.tensor.matmul(c.bank[:, 4 + t % 4, 0:D], ctx_f[:, k, t * P:(t + 1) * P],
                                                  wv[:, k, :], start=(k == 0), stop=(k == 1))
                        mm.then_inc(v_ps, 1)

                @block.scalar
                def _(act):
                    act.wait_ge(bq_sem, 1)
                    for u in range(U):
                        b, w, m = place(u)
                        act.wait_ge(proj_ps, u + 1)
                        if u >= 4:
                            act.wait_ge(rest1, u - 3)
                        bias = bq4[:, m:m + 1] if w == 0 else c.col("bk", m)
                        scale = float(DX) ** -0.5 if w == 0 else 1.0
                        nc.scalar.activation(full[:, u % 4, :], c.bank[:, u % 4, :], ACT.Identity, bias=bias,
                                             scale=scale).then_inc(full_sem, 1)
                        nc.scalar.activation(parts[:, w, 0, m, b * T:(b + 1) * T], c.bank[:, u % 4, :],
                                             ACT.Identity, bias=bias, scale=scale).then_inc(high, 1)
                        act.wait_ge(v_ps, u + 1)
                        nc.scalar.activation(values[:, u, :, 0:DX],
                                             c.bank[:, 4 + u % 4, 0:D].rearrange("p (h d) -> p h d", h=HX),
                                             ACT.Copy).then_inc(v_sem, 1)

                @block.vector
                def _(dve):
                    nc.vector.tensor_scalar(bq4[:, :], c.col("bq", 0, KD), float(DX) ** -0.5, None,
                                            ALU.mult).then_inc(bq_sem, 1)
                    for u in range(U):
                        b, w, m = place(u)
                        cols = slice(b * T, (b + 1) * T)
                        dve.wait_ge(full_sem, u + 1)
                        dve.wait_ge(high, u + 1)
                        if u >= 4:
                            dve.wait_ge(low, u - 3)
                        nc.vector.tensor_tensor(rest[:, u % 4, :], full[:, u % 4, :], parts[:, w, 0, m, cols],
                                                ALU.subtract).then_inc(rest1, 1)
                        dve.wait_ge(rest1, u + 1)
                        nc.vector.tensor_copy(parts[:, w, 1, m, cols], rest[:, u % 4, :]).then_inc(mid, 1)
                        dve.wait_ge(mid, u + 1)
                        nc.vector.tensor_tensor(parts[:, w, 2, m, cols], rest[:, u % 4, :],
                                                parts[:, w, 1, m, cols], ALU.subtract).then_inc(low, 1)

                @block.gpsimd
                def _(pool):
                    nc.gpsimd.memset(values[:, :, :, DX:32], 1.0).then_inc(ones_set, 1)

        with ExitStack() as ctx2:
            qst = c.sb(ctx2, "x_qst", [P, STACKS, HX, T], BF16)
            kst = c.sb(ctx2, "x_kst", [P, STACKS, HX, T], BF16)
            mx = c.sb(ctx2, "x_mx", [P, 2, HX * TB])
            mcl = c.sb(ctx2, "x_mcl", [P, 2, HX * TB])
            neg = c.sb(ctx2, "x_neg", [HX * TB, 2, P])
            nparts = c.sb(ctx2, "x_nparts", [HX * TB, 2, 3, P], BF16)
            scratch = c.xn_f[:, :, :].rearrange("p k (a t) -> p (k a) t", t=T)
            floor, shifted, raw = scratch[:, 0:2, :], scratch[:, 2:6, :], scratch[:, 6:8, :]
            probs = c.sb(ctx2, "x_probs", [P, 4, 2, T])
            rsum = c.sb(ctx2, "x_rsum", [P, 2, TB * HG])
            neg_clamp = c.sb(ctx2, "x_neg_clamp", [P, 1])
            const_set = c.sem("x_const_set")
            q_in = [c.sem(f"x_q_in{i}") for i in range(STACKS)]
            k_in = [c.sem(f"x_k_in{i}") for i in range(STACKS)]
            score_ps = c.sem("x_score_ps")
            max_sem = c.sem("x_max")
            clip_sem = c.sem("x_clip")
            turn_ps = c.sem("x_turn_ps")
            neg_sem = c.sem("x_neg_ready")
            nhigh = c.sem("x_nhigh")
            nrest = c.sem("x_nrest")
            nmid = c.sem("x_nmid")
            nlow = c.sem("x_nlow")
            neg_out = c.sem("x_neg_out")
            neg_in = c.sem("x_neg_in")
            floor_ps = c.sem("x_floor_ps")
            floor_sem = c.sem("x_floor_ready")
            keyed_ps = c.sem("x_keyed_ps")
            shift_sem = c.sem("x_shift")
            exp_sem = c.sem("x_exp")
            pv_ps = c.sem("x_pv_ps")
            raw_sem = c.sem("x_raw")
            raw_turned = c.sem("x_raw_turned")
            rsum_sem = c.sem("x_rsum_ready")
            out_sem = c.sem("x_out")
            NH = B * HX

            def s_bank(half):
                return c.bank[:, 0:2, :]

            def t_bank(j):
                return c.bank[:, 2 + 2 * (j % 2):4 + 2 * (j % 2), :]

            FB, PVB = 6, 7
            NG = NH // HG

            with nc.Block() as block:
                @block.sync
                def _(sp):
                    def stacks(b):
                        s = b % STACKS
                        if b >= STACKS:
                            sp.wait_ge(keyed_ps, 2 * HX * (b - STACKS + 1))
                        for j in range(NS):
                            for w, dst, order, sem in ((0, qst, SPLIT_Q, q_in), (1, kst, SPLIT_K, k_in)):
                                src = dram["split"][w, order[j], :, b * T:(b + 1) * T]
                                sp.dma_start(dst[j * DX:(j + 1) * DX, s, :, :],
                                             src.rearrange("(h d) t -> d h t", d=DX)).then_inc(sem[s], 16)

                    def maxima(b):
                        sp.wait_ge(nhigh, b + 1)
                        sp.wait_ge(nmid, b + 1)
                        sp.wait_ge(nlow, b + 1)
                        sp.dma_start(dram["negmax"][b].rearrange("s r q -> r s q"),
                                     nparts[:, b % 2, :, :]).then_inc(neg_out, 16)
                        sp.wait_ge(neg_out, 16 * (b + 1))
                        sp.dma_start(qst[RM:RM + 3, b % STACKS, :, :],
                                     dram["negmax"][b].rearrange("s (h i) q -> s h (i q)", i=TB)).then_inc(neg_in, 16)

                    for b in range(STACKS):
                        stacks(b)
                    for b in range(B):
                        maxima(b)
                        if b >= 1 and b + STACKS - 1 < B:
                            stacks(b + STACKS - 1)

                STEPS = 2 * (NH + LAG) + 5
                BATCH_STEPS = 2 * HX

                def group_at(k):
                    q = (k - 2) // (2 * HG) - 1
                    return q if (k - 2) % (2 * HG) == 0 and 0 <= q < NG else None

                def turns_at(j):
                    b = j // BATCH_STEPS - 1
                    return b if j % BATCH_STEPS == 0 and 0 <= b < B else None

                @block.tensor
                def _(pe):
                    def scores(j):
                        b, h = divmod(j // 2, HX)
                        if j % BATCH_STEPS == 0:
                            pe.wait_ge(q_in[b % STACKS], 16 * NS * (b // STACKS + 1))
                            pe.wait_ge(k_in[b % STACKS], 16 * NS * (b // STACKS + 1))
                        if j >= 1:
                            pe.wait_ge(max_sem, j)
                        for i in range(2):
                            q0 = (2 * (j % 2) + i) * P
                            mm = nc.tensor.matmul(c.bank[:, i, :], qst[0:KS, b % STACKS, h, q0:q0 + P],
                                                  kst[0:KS, b % STACKS, h, :], start=True, stop=True)
                        mm.then_inc(score_ps, 1)

                    in_fb = {"floor": 0, "turn": 0, "group": 0}

                    def fb_free(use):
                        for sem, n in ((floor_sem, in_fb["floor"]), (neg_sem, in_fb["turn"]),
                                       (out_sem, in_fb["group"])):
                            if n:
                                pe.wait_ge(sem, n)
                        in_fb[use] += 1

                    def turn(b):
                        pe.wait_ge(clip_sem, b + 1)
                        fb_free("turn")
                        nc.tensor.transpose(c.bank[0:HX * TB, FB, 0:P], mcl[:, b % 2, :],
                                            c.ident[:, :]).then_inc(turn_ps, 1)

                    def floor_of(g):
                        b, h = divmod(g, HX)
                        if h == 0:
                            pe.wait_ge(neg_in, 16 * (b + 1))
                        if g == 0:
                            pe.wait_ge(const_set, 1 + STACKS)
                        fb_free("floor")
                        nc.tensor.matmul(c.bank[:, FB, :], kst[RM:RM + 3, b % STACKS, h, 0:P],
                                         qst[RM:RM + 3, b % STACKS, h, :], start=True,
                                         stop=True).then_inc(floor_ps, 1)

                    def turn_raw(q):
                        pe.wait_ge(raw_sem, q + 1)
                        fb_free("group")
                        for i in range(TB):
                            tr = nc.tensor.transpose(c.bank[:, FB, i * P:(i + 1) * P],
                                                     raw[:, q % 2, i * P:(i + 1) * P], c.ident[:, :])
                        tr.then_inc(raw_turned, 1)

                    def keyed(k):
                        b, h = divmod(k // 2, HX)
                        if k >= 2:
                            pe.wait_ge(shift_sem, k - 1)
                        for i in range(2):
                            k0 = (2 * (k % 2) + i) * P
                            mm = nc.tensor.matmul(t_bank(k)[:, i, :], kst[0:RM + 3, b % STACKS, h, k0:k0 + P],
                                                  qst[0:RM + 3, b % STACKS, h, :], start=True, stop=True)
                        mm.then_inc(keyed_ps, 1)

                    def apply(k):
                        g, half = divmod(k, 2)
                        b, h = divmod(g, HX)
                        pe.wait_ge(exp_sem, k + 1)
                        if h % HG == 0 and half == 0 and g >= HG:
                            pe.wait_ge(raw_sem, g // HG)
                        r0 = 32 * (h % HG)
                        for i in range(2):
                            mm = nc.tensor.matmul(c.bank[r0:r0 + 32, PVB, :],
                                                  values[:, TB * b + 2 * half + i, h, :], probs[:, k % 4, i, :],
                                                  start=(half == 0 and i == 0), stop=(half == 1 and i == 1))
                        mm.then_inc(pv_ps, 1)

                    for j in range(STEPS):
                        k = j - 2 * LAG
                        if j < 2 * NH:
                            scores(j)
                        if turns_at(j) is not None:
                            turn(turns_at(j))
                        if 0 <= k < 2 * NH:
                            keyed(k)
                        if k % 2 == 1 and 0 <= (k + 1) // 2 < NH:
                            floor_of((k + 1) // 2)
                        if group_at(k - 2) is not None:
                            turn_raw(group_at(k - 2))
                        if 0 <= k - 2 < 2 * NH:
                            apply(k - 2)

                @block.scalar
                def _(act):
                    def negate(b):
                        act.wait_ge(turn_ps, b + 1)
                        nc.scalar.activation(neg[:, b % 2, :], c.bank[0:HX * TB, FB, 0:P], ACT.Copy,
                                             scale=-1.0).then_inc(neg_sem, 1)

                    def floor_of(g):
                        act.wait_ge(floor_ps, g + 1)
                        if g >= 2:
                            act.wait_ge(shift_sem, 2 * g - 2)
                        nc.scalar.activation(floor[:, g % 2, :], c.bank[:, FB, :], ACT.Identity,
                                             bias=neg_clamp[:, 0:1]).then_inc(floor_sem, 1)

                    def weights_of(k):
                        act.wait_ge(shift_sem, k + 1)
                        if k >= 4:
                            act.wait_ge(pv_ps, k - 3)
                        nc.scalar.activation(probs[:, k % 4, :, :], shifted[:, 2 * (k % 2):2 * (k % 2) + 2, :],
                                             ACT.Exp).then_inc(exp_sem, 1)

                    def take_raw(q):
                        act.wait_ge(pv_ps, 2 * HG * (q + 1))
                        if q >= 2:
                            act.wait_ge(raw_turned, q - 1)
                        nc.scalar.activation(raw[:, q % 2, :], c.bank[:, PVB, :], ACT.Copy).then_inc(raw_sem, 1)

                    act.wait_ge(const_set, 1)
                    for j in range(STEPS):
                        k = j - 2 * LAG
                        if turns_at(j) is not None:
                            negate(turns_at(j))
                        if k % 2 == 1 and 0 <= (k + 1) // 2 < NH:
                            floor_of((k + 1) // 2)
                        if group_at(k + 1) is not None:
                            take_raw(group_at(k + 1))
                        if 0 <= k < 2 * NH:
                            weights_of(k)

                @block.vector
                def _(dve):
                    def maxima(j):
                        b, h = divmod(j // 2, HX)
                        dve.wait_ge(score_ps, j + 1)
                        if b >= 2 and h == 0 and j % 2 == 0:
                            dve.wait_ge(clip_sem, b - 1)
                        at = TB * h + 2 * (j % 2)
                        nc.vector.tensor_reduce(mx[:, b % 2, at:at + 2], c.bank[:, 0:2, :], AX.X,
                                                ALU.max).then_inc(max_sem, 1)

                    def clip(b):
                        dve.wait_ge(max_sem, 2 * HX * (b + 1))
                        nc.vector.tensor_scalar(mcl[:, b % 2, :], mx[:, b % 2, :], CLAMP, -CLAMP, ALU.min,
                                                ALU.max).then_inc(clip_sem, 1)

                    def split(b):
                        dve.wait_ge(neg_sem, b + 1)
                        if b >= 2:
                            dve.wait_ge(neg_out, 16 * (b - 1))
                        nc.vector.tensor_copy(nparts[:, b % 2, 0, :], neg[:, b % 2, :]).then_inc(nhigh, 1)
                        dve.wait_ge(nhigh, b + 1)
                        nc.vector.tensor_tensor(neg[:, b % 2, :], neg[:, b % 2, :], nparts[:, b % 2, 0, :],
                                                ALU.subtract).then_inc(nrest, 1)
                        dve.wait_ge(nrest, b + 1)
                        nc.vector.tensor_copy(nparts[:, b % 2, 1, :], neg[:, b % 2, :]).then_inc(nmid, 1)
                        dve.wait_ge(nmid, b + 1)
                        nc.vector.tensor_tensor(nparts[:, b % 2, 2, :], neg[:, b % 2, :], nparts[:, b % 2, 1, :],
                                                ALU.subtract).then_inc(nlow, 1)

                    def shift(k):
                        g = k // 2
                        dve.wait_ge(floor_sem, g + 1)
                        dve.wait_ge(keyed_ps, k + 1)
                        if k >= 2:
                            dve.wait_ge(exp_sem, k - 1)
                        nc.vector.scalar_tensor_tensor(
                            out=shifted[:, 2 * (k % 2):2 * (k % 2) + 2, :], in0=t_bank(k), scalar=0.0,
                            in1=floor[:, g % 2:g % 2 + 1, :].to_broadcast([P, 2, T]),
                            op0=ALU.min, op1=ALU.max).then_inc(shift_sem, 1)

                    def finish(q):
                        b, h0 = divmod(HG * q, HX)
                        turned = c.bank[:, FB, :].rearrange("p (i h d) -> p i h d", i=TB, h=HG)
                        dve.wait_ge(raw_turned, q + 1)
                        inv = rsum[:, q % 2, :].rearrange("p (i h) -> p i h", i=TB)
                        nc.vector.reciprocal(inv, turned[:, :, :, DX]).then_inc(rsum_sem, 1)
                        dve.wait_ge(rsum_sem, q + 1)
                        nc.vector.tensor_tensor(
                            O[:, TB * b:TB * b + TB, h0 * DX:(h0 + HG) * DX].rearrange("p i (h d) -> p i h d", h=HG),
                            turned[:, :, :, 0:DX], inv.unsqueeze(3).to_broadcast([P, TB, HG, DX]),
                            ALU.mult).then_inc(out_sem, 1)

                    for j in range(STEPS):
                        k = j - 2 * LAG
                        if j < 2 * NH:
                            maxima(j)
                        if j % BATCH_STEPS == BATCH_STEPS - 1 and j < 2 * NH:
                            clip(j // BATCH_STEPS)
                        if turns_at(j - 1) is not None:
                            split(turns_at(j - 1))
                        if 0 <= k < 2 * NH:
                            shift(k)
                        if group_at(k - 2) is not None:
                            finish(group_at(k - 2))

                @block.gpsimd
                def _(pool):
                    nc.gpsimd.memset(neg_clamp[:, :], -CLAMP).then_inc(const_set, 1)
                    for s in range(STACKS):
                        pool.wait_ge(const_set, 1 + s)
                        nc.gpsimd.memset(kst[RM:P, s, :, :], 1.0).then_inc(const_set, 1)

        with ExitStack() as ctx2:
            wo = c.sb(ctx2, "x_wo", [P, KD, D])
            weights = c.sem("x_wo_in")
            turned = c.sem("x_o_turned")
            stored = c.sem("x_o_stored")
            out_ps = c.sem("x_out_ps")
            off_sem = c.sem("x_offset")
            added = c.sem("x_added")
            with nc.Block() as block:
                @block.sync
                def _(sp):
                    sp.dma_start(wo[:, :, :], dram["x_wo"]).then_inc(weights, 16)

                @block.tensor
                def _(pe):
                    def turn(b):
                        for k in range(KD):
                            if b >= 2:
                                pe.wait_ge(stored, KD * (b - 2) + k + 1)
                            for i in range(TB):
                                tr = nc.tensor.transpose(c.bank[:, KD * (b % 2) + k, i * P:(i + 1) * P],
                                                         O[:, TB * b + i, k * P:(k + 1) * P], c.ident[:, :])
                            tr.then_inc(turned, 1)

                    turn(0)
                    pe.wait_ge(weights, 16)
                    for b in range(B):
                        if b + 1 < B:
                            turn(b + 1)
                        pe.wait_ge(stored, KD * (b + 1))
                        for t in range(TB * b, TB * b + TB):
                            if t >= 4:
                                pe.wait_ge(added, t - 3)
                            for k in range(KD):
                                mm = nc.tensor.matmul(c.bank[:, 4 + t % 4, 0:D], c.xn_f[:, k, t * P:(t + 1) * P],
                                                      wo[:, k, :], start=(k == 0), stop=(k == KD - 1))
                            mm.then_inc(out_ps, 1)

                @block.scalar
                def _(act):
                    for b in range(B):
                        for k in range(KD):
                            act.wait_ge(turned, KD * b + k + 1)
                            nc.scalar.activation(c.xn_f[:, k, b * T:(b + 1) * T], c.bank[:, KD * (b % 2) + k, :],
                                                 ACT.Identity, bias=c.col("bv", k)).then_inc(stored, 1)

                @block.gpsimd
                def _(pool):
                    for t in range(NT):
                        nc.gpsimd.tensor_tensor(c.X[:, t, :], c.X[:, t, :], c.row("bo"),
                                                ALU.add).then_inc(off_sem, 1)

                @block.vector
                def _(dve):
                    for t in range(NT):
                        dve.wait_ge(out_ps, t + 1)
                        dve.wait_ge(off_sem, t + 1)
                        nc.vector.tensor_tensor(c.X[:, t, :], c.X[:, t, :], c.bank[:, 4 + t % 4, 0:D],
                                                ALU.add).then_inc(added, 1)


def route_block(c, ctx, tag, n_all, w_name, bias):
    nc, dram = c.nc, c.dram
    gates = c.sb(ctx, tag + "_gates", [P, NT, n_all])
    with ExitStack() as ctx2:
        wg = c.sb(ctx2, tag + "_wg", [P, KD, n_all])
        lg = c.sb(ctx2, tag + "_lg", [P, NT, n_all])
        rest = c.sb(ctx2, tag + "_rest", [P, NT, n_all])
        cand = c.sb(ctx2, tag + "_cand", [P, NT, n_all])
        pick = c.sb(ctx2, tag + "_pick", [P, 2, NT, n_all])
        top = c.sb(ctx2, tag + "_top", [P, 2, NT])
        at = c.sb(ctx2, tag + "_at", [P, 2, NT])
        ex = c.sb(ctx2, tag + "_ex", [P, NT])
        den = c.sb(ctx2, tag + "_den", [P, NT])
        share = c.sb(ctx2, tag + "_share", [P, 2, NT])
        weights, weights0 = c.tally("route_wg_in", 16)
        logits, logits0 = c.tally("route_logits", 1)
        step, step0 = c.tally("route_step", 18)
        gap, gap0 = c.tally("route_gap", 1)
        exp_sem, exp_sem0 = c.tally("route_exp", 1)

        def wide(ap):
            return ap.unsqueeze(2).to_broadcast([P, NT, n_all])

        index = c.row("expert_index")[:, 0:n_all].unsqueeze(1).to_broadcast([P, NT, n_all])
        with nc.Block() as block:
            @block.sync
            def _(sp):
                sp.dma_start(wg[:, :, :], dram[w_name]).then_inc(weights, 16)

            @block.tensor
            def _(pe):
                pe.wait_ge(weights, weights0 + 16)
                for t in range(NT):
                    for k in range(KD):
                        mm = nc.tensor.matmul(c.bank[:, 0, t * n_all:(t + 1) * n_all],
                                              c.xn_f[:, k, t * P:(t + 1) * P], wg[:, k, :],
                                              start=(k == 0), stop=(k == KD - 1))
                mm.then_inc(logits, 1)

            @block.vector
            def _(dve):
                done = [0]

                def then(ins):
                    done[0] += 1
                    ins.then_inc(step, 1)
                    dve.wait_ge(step, step0 + done[0])

                dve.wait_ge(logits, logits0 + 1)
                ps = c.bank[:, 0, 0:NT * n_all].rearrange("p (t e) -> p t e", t=NT)
                if bias:
                    then(nc.vector.tensor_tensor(lg[:, :, :], ps,
                                                 c.row("expert_bias").unsqueeze(1).to_broadcast([P, NT, n_all]),
                                                 ALU.add))
                else:
                    then(nc.vector.tensor_copy(lg[:, :, :], ps))
                left = lg
                for r in range(2):
                    then(nc.vector.tensor_reduce(top[:, r, :], left[:, :, :], AX.X, ALU.max))
                    then(nc.vector.tensor_tensor(cand[:, :, :], left[:, :, :], wide(top[:, r, :]), ALU.is_lt))
                    then(nc.vector.scalar_tensor_tensor(out=cand[:, :, :], in0=cand[:, :, :], scalar=float(n_all),
                                                        in1=index, op0=ALU.mult, op1=ALU.add))
                    then(nc.vector.tensor_reduce(at[:, r, :], cand[:, :, :], AX.X, ALU.min))
                    then(nc.vector.tensor_tensor(pick[:, r], cand[:, :, :], wide(at[:, r, :]), ALU.is_equal))
                    if r == 0:
                        then(nc.vector.scalar_tensor_tensor(out=rest[:, :, :], in0=pick[:, 0], scalar=-3.0e38,
                                                            in1=lg[:, :, :], op0=ALU.mult, op1=ALU.add))
                        left = rest
                nc.vector.tensor_tensor(ex[:, :], top[:, 1, :], top[:, 0, :], ALU.subtract).then_inc(gap, 1)
                dve.wait_ge(exp_sem, exp_sem0 + 1)
                then(nc.vector.tensor_scalar(den[:, :], ex[:, :], 1.0, None, ALU.add))
                then(nc.vector.reciprocal(share[:, 0, :], den[:, :]))
                then(nc.vector.tensor_tensor(share[:, 1, :], share[:, 0, :], ex[:, :], ALU.mult))
                then(nc.vector.tensor_tensor(pick[:, 0], pick[:, 0], wide(share[:, 0, :]), ALU.mult))
                then(nc.vector.tensor_tensor(pick[:, 1], pick[:, 1], wide(share[:, 1, :]), ALU.mult))
                then(nc.vector.tensor_tensor(gates[:, :, :], pick[:, 0], pick[:, 1], ALU.add))
                assert done[0] == 18

            @block.scalar
            def _(act):
                act.wait_ge(gap, gap0 + 1)
                nc.scalar.activation(ex[:, :], ex[:, :], ACT.Exp).then_inc(exp_sem, 1)
    return gates


TERMS = ((0, 0), (0, 1), (1, 0))


def split_input_block(c, ctx, tag):
    nc = c.nc
    halves = [c.sb(ctx, f"{tag}_x{i}", [P, KD, N], F32R) for i in range(2)]
    high, _high = c.tally("split_high", KD)
    low, _low = c.tally("split_low", KD)
    with nc.Block() as block:
        @block.scalar
        def _(act):
            for k in range(KD):
                nc.scalar.activation(halves[0][:, k, :], c.xn_f[:, k, :], ACT.Copy).then_inc(high, 1)

        @block.vector
        def _(dve):
            for k in range(KD):
                dve.wait_ge(high, _high + k + 1)
                nc.vector.tensor_tensor(halves[1][:, k, :], c.xn_f[:, k, :], halves[0][:, k, :].bitcast(F32),
                                        ALU.subtract).then_inc(low, 1)
    return halves


def experts_blocks(c):
    nc, dram = c.nc, c.dram
    norm_block(c, "n2")
    FT = FF0 // P
    with ExitStack() as ctx:
        gates = route_block(c, ctx, "r0", NE_ALL, "e0_gate", True)
        xs = split_input_block(c, ctx, "e0")
        w_full = [c.sb(ctx, "e0_w1", [P, 2, KD, FF0]), c.sb(ctx, "e0_w2", [P, 2, FT, D])]
        w1 = [c.sb(ctx, f"e0_w1_{i}", [P, 2, KD, FF0], F32R) for i in range(2)]
        w2 = [c.sb(ctx, f"e0_w2_{i}", [P, 2, FT, D], F32R) for i in range(2)]
        full = c.sb(ctx, "e0_hid", [P, 4, T])
        hid = [c.sb(ctx, f"e0_hid{i}", [P, 2, FT, T], F32R) for i in range(2)]
        zero_w = c.sb(ctx, "e0_zero_w", [P, NT])
        w1_in = [c.sem(f"e0_w1_in{i}") for i in range(2)]
        w2_in = [c.sem(f"e0_w2_in{i}") for i in range(2)]
        w_high = c.sem("e0_w_high")
        w_low = c.sem("e0_w_low")
        hid_ps = c.sem("e0_hid_ps")
        hid_full = c.sem("e0_hid_full")
        hid_high = c.sem("e0_hid_high")
        hid_low = c.sem("e0_hid_low")
        out_ps = c.sem("e0_out_ps")
        added = c.sem("e0_added")
        zero_sem = c.sem("e0_zero")
        U = NE * B
        with nc.Block() as block:
            @block.sync
            def _(sp):
                for e in range(NE):
                    if e >= 2:
                        sp.wait_ge(w_low, 2 * (e - 1))
                    sp.dma_start(w_full[0][:, e % 2], dram["e0_w1"][e]).then_inc(w1_in[e % 2], 16)
                    sp.dma_start(w_full[1][:, e % 2], dram["e0_w2"][e]).then_inc(w2_in[e % 2], 16)

            @block.gpsimd
            def _(pool):
                for e in range(NE):
                    for i, (w, w_in) in enumerate(((w1, w1_in), (w2, w2_in))):
                        pool.wait_ge(w_in[e % 2], 16 * (e // 2 + 1))
                        if e >= 2:
                            pool.wait_ge(out_ps, NT * (e - 1))
                        nc.gpsimd.tensor_copy(w[0][:, e % 2], w_full[i][:, e % 2]).then_inc(w_high, 1)
                        pool.wait_ge(w_high, 2 * e + i + 1)
                        nc.gpsimd.tensor_tensor(w[1][:, e % 2], w_full[i][:, e % 2],
                                                w[0][:, e % 2].bitcast(F32), ALU.subtract).then_inc(w_low, 1)

            @block.tensor
            def _(pe):
                def hidden(u):
                    e, b = divmod(u, B)
                    if b == 0:
                        pe.wait_ge(w_low, 2 * e + 1)
                    for f in range(FT):
                        n = FT * u + f
                        if n >= 4:
                            pe.wait_ge(hid_high, n - 3)
                        for k in range(KD):
                            for i, (wi, xi) in enumerate(TERMS):
                                mm = nc.tensor.matmul(c.bank[:, n % 4, :], w1[wi][:, e % 2, k, f * P:(f + 1) * P],
                                                      xs[xi][:, k, b * T:(b + 1) * T], start=(k == 0 and i == 0),
                                                      stop=(k == KD - 1 and i == 2))
                        mm.then_inc(hid_ps, 1)

                def output(u):
                    e, b = divmod(u, B)
                    if b == 0:
                        pe.wait_ge(w_low, 2 * e + 2)
                    pe.wait_ge(hid_low, FT * (u + 1))
                    for i in range(TB):
                        n = TB * u + i
                        if n >= 4:
                            pe.wait_ge(added, n - 3)
                        for f in range(FT):
                            for j, (hi, wi) in enumerate(TERMS):
                                mm = nc.tensor.matmul(c.bank[:, 4 + n % 4, 0:D],
                                                      hid[hi][:, u % 2, f, i * P:(i + 1) * P],
                                                      w2[wi][:, e % 2, f, :], start=(f == 0 and j == 0),
                                                      stop=(f == FT - 1 and j == 2))
                        mm.then_inc(out_ps, 1)

                hidden(0)
                for u in range(U):
                    if u + 1 < U:
                        hidden(u + 1)
                    output(u)

            @block.scalar
            def _(act):
                for n in range(FT * U):
                    u, f = divmod(n, FT)
                    act.wait_ge(hid_ps, n + 1)
                    if n >= 4:
                        act.wait_ge(hid_low, n - 3)
                    nc.scalar.activation(full[:, n % 4, :], c.bank[:, n % 4, :], ACT.Silu).then_inc(hid_full, 1)
                    if u >= 2:
                        act.wait_ge(out_ps, TB * (u - 1))
                    nc.scalar.activation(hid[0][:, u % 2, f, :], c.bank[:, n % 4, :],
                                         ACT.Silu).then_inc(hid_high, 1)

            @block.vector
            def _(dve):
                nc.vector.tensor_reduce(zero_w[:, :], gates[:, :, NE:NE_ALL], AX.X, ALU.add).then_inc(zero_sem, 1)
                dve.wait_ge(zero_sem, 1)
                for t in range(NT):
                    nc.vector.scalar_tensor_tensor(out=c.X[:, t, :], in0=c.xn[:, t, :], scalar=zero_w[:, t:t + 1],
                                                   in1=c.X[:, t, :], op0=ALU.mult,
                                                   op1=ALU.add).then_inc(zero_sem, 1)

                def lows(u):
                    for n in range(FT * u, FT * u + FT):
                        dve.wait_ge(hid_full, n + 1)
                        dve.wait_ge(hid_high, n + 1)
                        if u >= 2:
                            dve.wait_ge(out_ps, TB * (u - 1))
                        nc.vector.tensor_tensor(hid[1][:, u % 2, n % FT, :], full[:, n % 4, :],
                                                hid[0][:, u % 2, n % FT, :].bitcast(F32),
                                                ALU.subtract).then_inc(hid_low, 1)

                def adds(u):
                    e, b = divmod(u, B)
                    for i in range(TB):
                        n, t = TB * u + i, TB * b + i
                        dve.wait_ge(out_ps, n + 1)
                        if e == 0:
                            dve.wait_ge(zero_sem, t + 2)
                        else:
                            dve.wait_ge(added, NT * (e - 1) + t + 1)
                        nc.vector.scalar_tensor_tensor(out=c.X[:, t, :], in0=c.bank[:, 4 + n % 4, 0:D],
                                                       scalar=gates[:, t, e:e + 1], in1=c.X[:, t, :],
                                                       op0=ALU.mult, op1=ALU.add).then_inc(added, 1)

                lows(0)
                for u in range(U):
                    if u + 1 < U:
                        lows(u + 1)
                    adds(u)


def gru_blocks(c):
    nc, dram = c.nc, c.dram
    norm_block(c, "n3")
    with ExitStack() as ctx:
        wf = c.sb(ctx, "g_wf", [P, KD, 2 * EG])
        wd = c.sb(ctx, "g_wd", [P, GT, D])
        state = c.sb(ctx, "g_state", [P, GT, B, T])
        z = c.sb(ctx, "g_z", [P, 2, T])
        keep = c.sb(ctx, "g_keep", [P, 4, T])
        soft = c.sb(ctx, "g_soft", [P, 2, T])
        lin = c.sb(ctx, "g_lin", [P, 2, T])
        cand = c.sb(ctx, "g_cand", [P, 2, T])
        val = c.sb(ctx, "g_val", [P, 2, T])
        neg_b = c.sb(ctx, "g_neg_b", [P, GT])
        weights = c.sem("g_weights")
        neg_sem = c.sem("g_neg_b_ready")
        kz_ps = c.sem("g_kz_ps")
        hx_ps = c.sem("g_hx_ps")
        z_sem = c.sem("g_z_ready")
        keep_sem = c.sem("g_keep_ready")
        soft_sem = c.sem("g_soft_ready")
        lin_sem = c.sem("g_lin_ready")
        cand_sem = c.sem("g_cand_ready")
        val_sem = c.sem("g_val_ready")
        scanned = c.sem("g_scanned")
        out_ps = c.sem("g_out_ps")
        added = c.sem("g_added")
        U = B * GT
        with nc.Block() as block:
            @block.sync
            def _(sp):
                sp.dma_start(wf[:, :, :], dram["g_wf"]).then_inc(weights, 16)
                sp.dma_start(wd[:, :, :], dram["g_wd"]).then_inc(weights, 16)

            @block.tensor
            def _(pe):
                pe.wait_ge(weights, 32)
                for u in range(U):
                    b, m = divmod(u, GT)
                    for bank, off, sem, used in ((0, 0, kz_ps, keep_sem), (2, EG, hx_ps, lin_sem)):
                        if u >= 2:
                            pe.wait_ge(used, u - 1)
                            if off:
                                pe.wait_ge(soft_sem, u - 1)
                        for k in range(KD):
                            mm = nc.tensor.matmul(c.bank[:, bank + u % 2, :],
                                                  wf[:, k, off + m * P:off + (m + 1) * P],
                                                  c.xn_f[:, k, b * T:(b + 1) * T], start=(k == 0),
                                                  stop=(k == KD - 1))
                        mm.then_inc(sem, 1)
                for t in range(NT):
                    b, i = divmod(t, TB)
                    pe.wait_ge(scanned, GT * (b + 1))
                    if t >= 4:
                        pe.wait_ge(added, t - 3)
                    for m in range(GT):
                        mm = nc.tensor.matmul(c.bank[:, 4 + t % 4, 0:D], state[:, m, b, i * P:(i + 1) * P],
                                              wd[:, m, :], start=(m == 0), stop=(m == GT - 1))
                    mm.then_inc(out_ps, 1)

            @block.scalar
            def _(act):
                act.wait_ge(neg_sem, 1)
                for u in range(U):
                    b, m = divmod(u, GT)
                    act.wait_ge(kz_ps, u + 1)
                    if u >= 2:
                        act.wait_ge(val_sem, u - 1)
                    nc.scalar.activation(z[:, u % 2, :], c.bank[:, u % 2, :], ACT.Sigmoid,
                                         bias=c.col("b_f", m)).then_inc(z_sem, 1)
                    if u >= 4:
                        act.wait_ge(scanned, u - 3)
                    nc.scalar.activation(keep[:, u % 4, :], c.bank[:, u % 2, :], ACT.Sigmoid,
                                         bias=neg_b[:, m:m + 1], scale=-1.0).then_inc(keep_sem, 1)
                    act.wait_ge(lin_sem, u + 1)
                    if u >= 2:
                        act.wait_ge(cand_sem, u - 1)
                    nc.scalar.activation(soft[:, u % 2, :], c.bank[:, 2 + u % 2, :], ACT.Sigmoid,
                                         bias=c.col("b_f", GT + m)).then_inc(soft_sem, 1)

            @block.vector
            def _(dve):
                nc.vector.tensor_scalar(neg_b[:, :], c.col("b_f", 0, GT), -1.0, None,
                                        ALU.mult).then_inc(neg_sem, 1)

                def candidate(u):
                    b, m = divmod(u, GT)
                    dve.wait_ge(hx_ps, u + 1)
                    if u >= 2:
                        dve.wait_ge(cand_sem, u - 1)
                    nc.vector.tensor_scalar(lin[:, u % 2, :], c.bank[:, 2 + u % 2, :], c.col("b_f", GT + m), 0.0,
                                            ALU.add, ALU.max).then_inc(lin_sem, 1)
                    dve.wait_ge(lin_sem, u + 1)
                    dve.wait_ge(soft_sem, u + 1)
                    if u >= 2:
                        dve.wait_ge(val_sem, u - 1)
                    nc.vector.scalar_tensor_tensor(out=cand[:, u % 2, :], in0=soft[:, u % 2, :], scalar=0.5,
                                                   in1=lin[:, u % 2, :], op0=ALU.min,
                                                   op1=ALU.add).then_inc(cand_sem, 1)

                def scan(u):
                    b, m = divmod(u, GT)
                    dve.wait_ge(val_sem, u + 1)
                    dve.wait_ge(keep_sem, u + 1)
                    nc.vector.tensor_tensor_scan(state[:, m, b, :], keep[:, u % 4, :], val[:, u % 2, :], 0.5,
                                                 ALU.mult, ALU.add).then_inc(scanned, 1)

                for u in range(U + 1):
                    if u < U:
                        candidate(u)
                    if u >= 1:
                        scan(u - 1)
                for t in range(NT):
                    dve.wait_ge(out_ps, t + 1)
                    nc.vector.tensor_tensor(c.X[:, t, :], c.X[:, t, :], c.bank[:, 4 + t % 4, 0:D],
                                            ALU.add).then_inc(added, 1)

            @block.gpsimd
            def _(pool):
                for u in range(U):
                    pool.wait_ge(cand_sem, u + 1)
                    pool.wait_ge(z_sem, u + 1)
                    if u >= 2:
                        pool.wait_ge(scanned, u - 1)
                    nc.gpsimd.tensor_tensor(val[:, u % 2, :], cand[:, u % 2, :], z[:, u % 2, :],
                                            ALU.mult).then_inc(val_sem, 1)


TERNARY = (("t_d2v", CK, 2, D), ("t_img", P, KD, D), ("t_txt", P, KD, D), ("t_att0", P, KD, P),
           ("t_att1", P, KD, P), ("t_f1", P, 2 * KD, FX), ("t_f2", P, FX // P, D))
W_D2V, W_IMG, W_TXT, W_ATT0, W_ATT1, W_F1, W_F2 = range(len(TERNARY))


def ternary_weights_block(c, ctx):
    nc, dram = c.nc, c.dram
    n = len(TERNARY)
    tern = [c.sb(ctx, name + "_q", [p, k, w], BF16) for name, p, k, w in TERNARY]
    scale = c.sb(ctx, "t_scale", [P, n])
    with ExitStack() as ctx2:
        full = [c.sb(ctx2, name, [p, k, w]) for name, p, k, w in TERNARY]
        below = [c.sb(ctx2, name + "_b", [p, k, w], BF16) for name, p, k, w in TERNARY]
        sums = c.sb(ctx2, "t_sums", [P, n])
        total = c.sb(ctx2, "t_total", [P, n])
        half = c.sb(ctx2, "t_half", [P, 2, n])
        loaded = [c.sem(f"t_loaded{i}") for i in range(n)]
        zero_sem = c.sem("t_zero")
        sum_sem = c.sem("t_sum")
        total_sem = c.sem("t_total_ready")
        HT = FF1 // P
        w_in = c.sb(ctx2, "e1_w_in", [P, 2, HT, D])
        w_out = c.sb(ctx2, "e1_w_out", [P, 2, HT, D])
        in_in = [c.sem(f"e1_in_in{i}") for i in range(2)]
        out_in = [c.sem(f"e1_out_in{i}") for i in range(2)]
        comb_ps = c.sem("e1_comb_ps")
        comb_sem = c.sem("e1_comb_ready")
        scale_sem = c.sem("t_scale_ready")
        half_sem = c.sem("t_half_ready")
        below_sem = c.sem("t_below")
        tern_sem = c.sem("t_tern")
        with nc.Block() as block:
            @block.sync
            def _(sp):
                for i, (name, p, k, w) in enumerate(TERNARY):
                    sp.dma_start(full[i][:, :, :], dram[name]).then_inc(loaded[i], 16)
                for e in range(NE):
                    if e >= 2:
                        sp.wait_ge(comb_ps, KD * (e - 1))
                    sp.dma_start(w_in[:, e % 2], dram["e1_w_in"][e]).then_inc(in_in[e % 2], 16)
                    sp.dma_start(w_out[:, e % 2], dram["e1_w_out"][e]).then_inc(out_in[e % 2], 16)

            @block.tensor
            def _(pe):
                for e in range(NE):
                    pe.wait_ge(in_in[e % 2], 16 * (e // 2 + 1))
                    pe.wait_ge(out_in[e % 2], 16 * (e // 2 + 1))
                    for k in range(KD):
                        u = KD * e + k
                        if u >= 8:
                            pe.wait_ge(comb_sem, u - 7)
                        for h in range(HT):
                            mm = nc.tensor.matmul(c.bank[:, u % 8, 0:D], w_in[:, e % 2, h, k * P:(k + 1) * P],
                                                  w_out[:, e % 2, h, :], start=(h == 0), stop=(h == HT - 1))
                        mm.then_inc(comb_ps, 1)

            @block.scalar
            def _(act):
                for u in range(KD * NE):
                    e, k = divmod(u, KD)
                    act.wait_ge(comb_ps, u + 1)
                    nc.scalar.activation(c.comb[:, k, e, :], c.bank[:, u % 8, 0:D], ACT.Copy).then_inc(comb_sem, 1)

            @block.gpsimd
            def _(pool):
                pool.wait_ge(sum_sem, n)
                nc.gpsimd.partition_all_reduce(total[:, :], sums[:, :], P, RED.add).then_inc(total_sem, 1)

            @block.vector
            def _(dve):
                nc.vector.memset(sums[:, :], 0.0).then_inc(zero_sem, 1)
                dve.wait_ge(zero_sem, 1)
                for i, (name, p, k, w) in enumerate(TERNARY):
                    dve.wait_ge(loaded[i], 16)
                    nc.vector.tensor_reduce(sums[0:p, i:i + 1], full[i][:, :, :], AX.XY, ALU.add,
                                            apply_absolute_value=True).then_inc(sum_sem, 1)
                dve.wait_ge(total_sem, 1)
                for i, (name, p, k, w) in enumerate(TERNARY):
                    nc.vector.tensor_scalar(scale[:, i:i + 1], total[:, i:i + 1], 1.0 / (p * k * w), 1e-5,
                                            ALU.mult, ALU.max).then_inc(scale_sem, 1)
                dve.wait_ge(scale_sem, n)
                nc.vector.tensor_scalar(half[:, 0, :], scale[:, :], 0.5, None, ALU.mult).then_inc(half_sem, 1)
                nc.vector.tensor_scalar(half[:, 1, :], scale[:, :], -0.5, None, ALU.mult).then_inc(half_sem, 1)
                dve.wait_ge(half_sem, 2)
                for i, (name, p, k, w) in enumerate(TERNARY):
                    nc.vector.tensor_scalar(below[i][:, :, :], full[i][:, :, :], half[0:p, 1, i:i + 1], None,
                                            ALU.is_lt).then_inc(below_sem, 1)
                for i, (name, p, k, w) in enumerate(TERNARY):
                    dve.wait_ge(below_sem, i + 1)
                    nc.vector.scalar_tensor_tensor(
                        out=tern[i][:, :, :].rearrange("p k w -> p (k w)"),
                        in0=full[i][:, :, :].rearrange("p k w -> p (k w)"), scalar=half[0:p, 0, i:i + 1],
                        in1=below[i][:, :, :].rearrange("p k w -> p (k w)"), op0=ALU.is_gt,
                        op1=ALU.subtract).then_inc(tern_sem, 1)
    return tern, scale


def quantise_block(c, tag, sources, scale, i_w, scratch):
    nc = c.nc
    peak, top, step, inv, out_scale, magic = scratch
    n = len(sources)
    peak_zero, peak_zero0 = c.tally("quant_peak_zero", 1)
    peak_sem, peak_sem0 = c.tally("quant_peak", n)
    peak1_sem, peak1_sem0 = c.tally("quant_peak1", 1)
    top_sem, top_sem0 = c.tally("quant_top", 1)
    step_sem, step_sem0 = c.tally("quant_step", 1)
    inv_sem, inv_sem0 = c.tally("quant_inv", 1)
    scale_sem, scale_sem0 = c.tally("quant_scale", 1)
    up_sem, up_sem0 = c.tally("quant_up", n)
    clip_sem, clip_sem0 = c.tally("quant_clip", n)
    down_sem, down_sem0 = c.tally("quant_down", n)
    with nc.Block() as block:
        @block.vector
        def _(dve):
            nc.vector.memset(peak[:, :], 0.0).then_inc(peak_zero, 1)
            dve.wait_ge(peak_zero, peak_zero0 + 1)
            for i, (src, dst) in enumerate(sources):
                axis = AX.X if len(src.shape) == 2 else AX.XY
                nc.vector.tensor_reduce(peak[0:src.shape[0], i:i + 1], src, axis, ALU.max,
                                        apply_absolute_value=True).then_inc(peak_sem, 1)
            dve.wait_ge(peak_sem, peak_sem0 + n)
            nc.vector.tensor_reduce(top[:, 0:1], peak[:, 0:n], AX.X, ALU.max).then_inc(peak1_sem, 1)
            dve.wait_ge(top_sem, top_sem0 + 1)
            nc.vector.tensor_scalar(step[:, 0:1], top[:, 1:2], 1e-8, 1.0 / 127.0, ALU.max,
                                    ALU.mult).then_inc(step_sem, 1)
            dve.wait_ge(step_sem, step_sem0 + 1)
            nc.vector.reciprocal(inv[:, 0:1], step[:, 0:1]).then_inc(inv_sem, 1)
            nc.vector.tensor_tensor(out_scale[:, 0:1], step[:, 0:1], scale[:, i_w:i_w + 1],
                                    ALU.mult).then_inc(scale_sem, 1)
            for i, (src, dst) in enumerate(sources):
                dve.wait_ge(up_sem, up_sem0 + i + 1)
                nc.vector.tensor_scalar(src, src, MAGIC - 128.0, MAGIC + 127.0, ALU.max,
                                        ALU.min).then_inc(clip_sem, 1)

        @block.gpsimd
        def _(pool):
            pool.wait_ge(peak1_sem, peak1_sem0 + 1)
            nc.gpsimd.partition_all_reduce(top[:, 1:2], top[:, 0:1], P, RED.max).then_inc(top_sem, 1)
            for i, (src, dst) in enumerate(sources):
                pool.wait_ge(clip_sem, clip_sem0 + i + 1)
                nc.gpsimd.tensor_scalar(dst, src, 1.0, -MAGIC, ALU.mult, ALU.add).then_inc(down_sem, 1)

        @block.scalar
        def _(act):
            act.wait_ge(inv_sem, inv_sem0 + 1)
            for i, (src, dst) in enumerate(sources):
                p = src.shape[0]
                nc.scalar.activation(src, src, ACT.Identity, bias=magic[0:p, 0:1],
                                     scale=inv[0:p, 0:1]).then_inc(up_sem, 1)


def product_block(c, tag, units, out_scale, func=ACT.Identity):
    nc = c.nc
    ps, ps0 = c.tally("product_ps", len(units))
    done, done0 = c.tally("product_done", len(units))
    with nc.Block() as block:
        @block.tensor
        def _(pe):
            for u, (pairs, out, bias) in enumerate(units):
                if u >= 8:
                    pe.wait_ge(done, done0 + u - 7)
                for k, (lhs, rhs) in enumerate(pairs):
                    mm = nc.tensor.matmul(c.bank[:, u % 8, :], lhs, rhs, start=(k == 0),
                                          stop=(k == len(pairs) - 1))
                mm.then_inc(ps, 1)

        @block.scalar
        def _(act):
            for u, (pairs, out, bias) in enumerate(units):
                act.wait_ge(ps, ps0 + u + 1)
                nc.scalar.activation(out, c.bank[:, u % 8, :], func, bias=bias,
                                     scale=out_scale[:, 0:1]).then_inc(done, 1)


def ternary_cross_blocks(c):
    nc, dram = c.nc, c.dram
    norm_block(c, "n4")
    with ExitStack() as ctx:
        tern, scale = ternary_weights_block(c, ctx)
        peak = c.sb(ctx, "t_peak", [P, 32])
        top = c.sb(ctx, "t_top", [P, 2])
        step = c.sb(ctx, "t_step", [P, 1])
        inv = c.sb(ctx, "t_inv", [P, 1])
        magic = c.sb(ctx, "t_magic", [P, 1])
        out_scale = c.sb(ctx, "t_out_scale", [P, 1])
        scratch = (peak, top, step, inv, out_scale, magic)
        fused = c.sb(ctx, "t_fused", [P, KD, N])
        mean_img = c.sb(ctx, "t_mean_img", [P, KD, B])
        keys_ctx = ExitStack()
        keys_f = c.sb(keys_ctx, "t_keys_f", [P, 2, N])
        keys_t = c.sb(keys_ctx, "t_keys_t", [P, 2, NT, P])

        def cut(ap, b):
            return ap[:, b * T:(b + 1) * T]

        with ExitStack() as ctx2:
            cf = c.sb(ctx2, "t_ctx", [CK, 2, N])
            qb = c.sb(ctx2, "t_q", [P, KD, N], BF16)
            img = c.sb(ctx2, "t_img_f", [P, KD, N])
            ctx_in = c.sem("t_ctx_in")
            magic_set = c.sem("t_magic_set")
            mean_sum = c.sem("t_mean_sum")
            mean_sem = c.sem("t_mean")
            turned = c.sem("t_keys_turned")
            turned_out = c.sem("t_keys_stored")
            with nc.Block() as block:
                @block.sync
                def _(sp):
                    sp.dma_start(cf[:, :, :], dram["ctx_f"]).then_inc(ctx_in, 16)
                    sp.wait_ge(ctx_in, 16)

                @block.gpsimd
                def _(pool):
                    nc.gpsimd.memset(magic[:, :], MAGIC).then_inc(magic_set, 1)

            def project(tag, src, rows, i_w, i_b, dst, halves=KD):
                quantise_block(c, tag + "q", [(cut(src[:, k, :], b), cut(qb[0:rows, k, :], b))
                                              for k in range(2) for b in range(B)], scale, i_w, scratch)
                product_block(c, tag, [([(tern[i_w][:, k, m * P:(m + 1) * P], cut(qb[0:rows, k, :], b))
                                         for k in range(2)], cut(dst[:, m, :], b), c.col(i_b, m))
                                       for b in range(B) for m in range(halves)], out_scale)

            project("td", cf, CK, W_D2V, "b_d2v", fused)
            project("ti", fused, P, W_IMG, "b_img", img)
            with nc.Block() as block:
                @block.vector
                def _(dve):
                    nc.vector.tensor_reduce(mean_img[:, :, :], img[:, :, :].rearrange("p k (b t) -> p k b t", b=B),
                                            AX.X, ALU.add).then_inc(mean_sum, 1)
                    dve.wait_ge(mean_sum, 1)
                    nc.vector.tensor_scalar(mean_img[:, :, :], mean_img[:, :, :], 1.0 / T, None,
                                            ALU.mult).then_inc(mean_sem, 1)
            quantise_block(c, "tkq", [(cut(img[:, k, :], b), cut(qb[:, k, :], b))
                                      for k in range(2) for b in range(B)], scale, W_ATT0, scratch)
            product_block(c, "tk0", [([(tern[W_ATT0][:, k, :], cut(qb[:, k, :], b)) for k in range(2)],
                                      cut(keys_f[:, 0, :], b), c.col("b_att0")) for b in range(B)], out_scale)
            scale1 = c.sem("t_scale1")
            with nc.Block() as block:
                @block.vector
                def _(dve):
                    nc.vector.tensor_tensor(out_scale[:, 0:1], step[:, 0:1], scale[:, W_ATT1:W_ATT1 + 1],
                                            ALU.mult).then_inc(scale1, 1)
            product_block(c, "tk1", [([(tern[W_ATT1][:, k, :], cut(qb[:, k, :], b)) for k in range(2)],
                                      cut(keys_f[:, 1, :], b), c.col("b_att1")) for b in range(B)], out_scale)
            with nc.Block() as block:
                @block.tensor
                def _(pe):
                    for j in range(2 * B):
                        r, b = divmod(j, B)
                        for i in range(TB):
                            tr = nc.tensor.transpose(c.bank[:, j, i * P:(i + 1) * P],
                                                     keys_f[:, r, b * T + i * P:b * T + (i + 1) * P],
                                                     c.ident[:, :])
                        tr.then_inc(turned, 1)

                @block.scalar
                def _(act):
                    for j in range(2 * B):
                        r, b = divmod(j, B)
                        act.wait_ge(turned, j + 1)
                        nc.scalar.activation(keys_t[:, r, TB * b:TB * b + TB, :],
                                             c.bank[:, j, :].rearrange("p (i d) -> p i d", i=TB),
                                             ACT.Copy).then_inc(turned_out, 1)
            project("tt", c.xn_f, P, W_TXT, "b_txt", fused)

        with ExitStack() as ctx2:
            qsum = c.sb(ctx2, "t_qsum", [P, 2, T])
            mx = c.sb(ctx2, "t_mx", [P, 2 * NT])
            neg = c.sb(ctx2, "t_neg", [P, 2 * NT])
            ex = c.sb(ctx2, "t_ex", [P, 4, T])
            rsum = c.sb(ctx2, "t_rsum", [P, 2 * NT])
            rinv = c.sb(ctx2, "t_rinv", [P, 2 * NT])
            probs = c.sb(ctx2, "t_probs", [P, 2, T])
            probs_f = c.sb(ctx2, "t_probs_f", [P, 2, TB, T])
            qsum_sem = c.sem("t_qsum_ready")
            score_ps = c.sem("t_score_ps")
            max_sem = c.sem("t_max")
            neg_sem = c.sem("t_neg_ready")
            exp_sem = c.sem("t_exp")
            inv_sem = c.sem("t_rinv_ready")
            prob_sem = c.sem("t_prob")
            turn_ps = c.sem("t_turn_ps")
            turn_out = c.sem("t_turn_out")
            att_ps = c.sem("t_att_ps")
            add_sem = c.sem("t_add")
            inv_sqrt = 1.0 / float(np.sqrt(D))
            AHEAD = 2
            with nc.Block() as block:
                @block.tensor
                def _(pe):
                    def score(u):
                        r, b, i = u // NT, (u // TB) % B, u % TB
                        g = u // TB
                        pe.wait_ge(qsum_sem, g + 1)
                        if u >= 4:
                            pe.wait_ge(exp_sem, u - 3)
                        nc.tensor.matmul(c.bank[:, u % 4, :], qsum[:, g % 2, i * P:(i + 1) * P],
                                         cut(keys_f[:, r, :], b), start=True, stop=True).then_inc(score_ps, 1)

                    def turn(u):
                        pe.wait_ge(prob_sem, u + 1)
                        if u >= 2:
                            pe.wait_ge(turn_out, u - 1)
                        for k in range(TB):
                            tr = nc.tensor.transpose(c.bank[:, 4 + u % 2, k * P:(k + 1) * P],
                                                     probs[:, u % 2, k * P:(k + 1) * P], c.ident[:, :])
                        tr.then_inc(turn_ps, 1)

                    def apply(g):
                        r, b = divmod(g, B)
                        pe.wait_ge(turn_out, TB * (g + 1))
                        if g >= 2:
                            pe.wait_ge(add_sem, KD * (g - 1))
                        for k in range(TB):
                            mm = nc.tensor.matmul(c.bank[:, 6 + g % 2, :], keys_t[:, r, TB * b + k, :],
                                                  probs_f[:, g % 2, k, :], start=(k == 0), stop=(k == TB - 1))
                        mm.then_inc(att_ps, 1)

                    for u in range(AHEAD):
                        score(u)
                    for u in range(2 * NT):
                        if u + AHEAD < 2 * NT:
                            score(u + AHEAD)
                        turn(u)
                        if u % TB == TB - 1:
                            apply(u // TB)

                @block.vector
                def _(dve):
                    def sum_q(g):
                        r, b = divmod(g, B)
                        if g >= 2:
                            dve.wait_ge(score_ps, TB * (g - 1))
                        if r:
                            dve.wait_ge(add_sem, KD * (b + 1))
                        nc.vector.tensor_tensor(qsum[:, g % 2, :], cut(fused[:, 0, :], b), cut(fused[:, 1, :], b),
                                                ALU.add).then_inc(qsum_sem, 1)

                    def top_of(u):
                        dve.wait_ge(score_ps, u + 1)
                        nc.vector.tensor_reduce(mx[:, u:u + 1], c.bank[:, u % 4, :], AX.X,
                                                ALU.max).then_inc(max_sem, 1)
                        dve.wait_ge(max_sem, u + 1)
                        nc.vector.tensor_scalar(neg[:, u:u + 1], mx[:, u:u + 1], -inv_sqrt, None,
                                                ALU.mult).then_inc(neg_sem, 1)

                    def divide(u):
                        dve.wait_ge(exp_sem, u + 1)
                        nc.vector.reciprocal(rinv[:, u:u + 1], rsum[:, u:u + 1]).then_inc(inv_sem, 1)
                        dve.wait_ge(inv_sem, u + 1)
                        if u >= 2:
                            dve.wait_ge(turn_ps, u - 1)
                        nc.vector.tensor_scalar(probs[:, u % 2, :], ex[:, u % 4, :], rinv[:, u:u + 1], 0.1,
                                                ALU.mult, ALU.mult).then_inc(prob_sem, 1)

                    def add(g):
                        r, b = divmod(g, B)
                        dve.wait_ge(att_ps, g + 1)
                        for k in range(KD):
                            nc.vector.tensor_tensor(cut(fused[:, k, :], b), cut(fused[:, k, :], b),
                                                    c.bank[:, 6 + g % 2, :], ALU.add).then_inc(add_sem, 1)

                    sum_q(0)
                    for u in range(AHEAD):
                        top_of(u)
                    for u in range(2 * NT):
                        g = u // TB
                        if u % TB == 0 and g + 1 < 2 * B:
                            sum_q(g + 1)
                        if u + AHEAD < 2 * NT:
                            top_of(u + AHEAD)
                        divide(u)
                        if u % TB == 1 and g >= 1:
                            add(g - 1)
                    add(2 * B - 1)

                @block.scalar
                def _(act):
                    def weigh(u):
                        act.wait_ge(neg_sem, u + 1)
                        if u >= 4:
                            act.wait_ge(prob_sem, u - 3)
                        nc.scalar.activation(ex[:, u % 4, :], c.bank[:, u % 4, :], ACT.Exp, bias=neg[:, u:u + 1],
                                             scale=inv_sqrt, accum_out=rsum[:, u:u + 1]).then_inc(exp_sem, 1)

                    def store(u):
                        g, i = divmod(u, TB)
                        act.wait_ge(turn_ps, u + 1)
                        if g >= 2:
                            act.wait_ge(att_ps, g - 1)
                        nc.scalar.activation(probs_f[:, g % 2, :, i * P:(i + 1) * P],
                                             c.bank[:, 4 + u % 2, :].rearrange("p (k q) -> p k q", k=TB),
                                             ACT.Copy).then_inc(turn_out, 1)

                    for u in range(2 * NT + AHEAD):
                        if u < 2 * NT:
                            weigh(u)
                        if u >= AHEAD:
                            store(u - AHEAD)

        keys_ctx.close()
        with ExitStack() as ctx2:
            hid = c.sb(ctx2, "t_hid", [P, FX // P, N])
            qh = c.sb(ctx2, "t_qh", [P, FX // P, N], BF16)
            qf = c.xn[:, :, :].bitcast(BF16).rearrange("p t d -> p (t d)")[:, 0:KD * N].rearrange(
                "p (k n) -> p k n", k=KD)
            qm = c.sb(ctx2, "t_qm", [P, KD * B], BF16)
            mb = c.sb(ctx2, "t_mb", [P, FX // P, B])
            MF = FX // P
            quantise_block(c, "tfq", [(cut(fused[:, k, :], b), cut(qf[:, k, :], b))
                                      for k in range(KD) for b in range(B)]
                           + [(mean_img[:, :, :].rearrange("p k b -> p (k b)"), qm[:, :])], scale, W_F1, scratch)
            mean_ps = c.sem("t_mean_ps")
            mean_bias = c.sem("t_mean_bias")
            with nc.Block() as block:
                @block.tensor
                def _(pe):
                    for m in range(MF):
                        for k in range(KD):
                            mm = nc.tensor.matmul(c.bank[:, m, 0:B], tern[W_F1][:, KD + k, m * P:(m + 1) * P],
                                                  qm[:, k * B:(k + 1) * B], start=(k == 0), stop=(k == KD - 1))
                        mm.then_inc(mean_ps, 1)

                @block.scalar
                def _(act):
                    for m in range(MF):
                        act.wait_ge(mean_ps, m + 1)
                        nc.scalar.activation(mb[:, m, :], c.bank[:, m, 0:B], ACT.Identity, bias=c.col("b_f1", m),
                                             scale=out_scale[:, 0:1]).then_inc(mean_bias, 1)

            product_block(c, "tf1", [([(tern[W_F1][:, k, m * P:(m + 1) * P], cut(qf[:, k, :], b))
                                       for k in range(KD)], cut(hid[:, m, :], b), mb[:, m, b:b + 1])
                                     for b in range(B) for m in range(MF)], out_scale, ACT.Relu)
            quantise_block(c, "thq", [(hid[:, m, :], qh[:, m, :]) for m in range(MF)], scale, W_F2, scratch)
            out_ps = c.sem("t_out_ps")
            off_sem = c.sem("t_offset")
            added = c.sem("t_added")
            with nc.Block() as block:
                @block.tensor
                def _(pe):
                    for t in range(NT):
                        if t >= 8:
                            pe.wait_ge(added, t - 7)
                        for m in range(MF):
                            mm = nc.tensor.matmul(c.bank[:, t % 8, 0:D], qh[:, m, t * P:(t + 1) * P],
                                                  tern[W_F2][:, m, :], start=(m == 0), stop=(m == MF - 1))
                        mm.then_inc(out_ps, 1)

                @block.gpsimd
                def _(pool):
                    for t in range(NT):
                        nc.gpsimd.tensor_tensor(c.X[:, t, :], c.X[:, t, :], c.row("b_f2"),
                                                ALU.add).then_inc(off_sem, 1)

                @block.vector
                def _(dve):
                    for t in range(NT):
                        dve.wait_ge(out_ps, t + 1)
                        dve.wait_ge(off_sem, t + 1)
                        nc.vector.scalar_tensor_tensor(out=c.X[:, t, :], in0=c.bank[:, t % 8, 0:D],
                                                       scalar=out_scale[:, 0:1], in1=c.X[:, t, :],
                                                       op0=ALU.mult, op1=ALU.add).then_inc(added, 1)


def linear_experts_blocks(c):
    nc, dram = c.nc, c.dram
    norm_block(c, "n5")
    with ExitStack() as ctx:
        gates = route_block(c, ctx, "r1", NE, "e1_gate", False)
        xs = split_input_block(c, ctx, "e1")
        comb = [c.sb(ctx, f"e1_comb{i}", [P, KD, NE, D], F32R) for i in range(2)]
        comb_high = c.sem("e1_comb_high")
        comb_low = c.sem("e1_comb_low")
        out_ps = c.sem("e1_out_ps")
        added = c.sem("e1_added")
        NP = NE // 2
        with nc.Block() as block:
            @block.sync
            def _(sp):
                for t in range(NT):
                    sp.wait_ge(added, NE * (t + 1))
                    sp.dma_start(dram["out"][t * P:(t + 1) * P, :], c.X[:, t, :]).then_inc(c.saved, 16)
                sp.wait_ge(c.saved, 16 * NT)

            @block.scalar
            def _(act):
                for p in range(NP):
                    nc.scalar.activation(comb[0][:, :, 2 * p:2 * p + 2, :], c.comb[:, :, 2 * p:2 * p + 2, :],
                                         ACT.Copy).then_inc(comb_high, 1)

            @block.tensor
            def _(pe):
                for t in range(NT):
                    for p in range(NP):
                        n = NP * t + p
                        if t == 0:
                            pe.wait_ge(comb_low, p + 1)
                        if n >= 8:
                            pe.wait_ge(added, 2 * (n - 7))
                        for k in range(KD):
                            for i, (xi, wi) in enumerate(TERMS):
                                mm = nc.tensor.matmul(c.bank[:, n % 8, :], xs[xi][:, k, t * P:(t + 1) * P],
                                                      comb[wi][:, k, 2 * p:2 * p + 2, :],
                                                      start=(k == 0 and i == 0), stop=(k == KD - 1 and i == 2))
                        mm.then_inc(out_ps, 1)

            @block.vector
            def _(dve):
                for p in range(NP):
                    dve.wait_ge(comb_high, p + 1)
                    nc.vector.tensor_tensor(comb[1][:, :, 2 * p:2 * p + 2, :], c.comb[:, :, 2 * p:2 * p + 2, :],
                                            comb[0][:, :, 2 * p:2 * p + 2, :].bitcast(F32),
                                            ALU.subtract).then_inc(comb_low, 1)
                for t in range(NT):
                    for e in range(NE):
                        n = NP * t + e // 2
                        dve.wait_ge(out_ps, n + 1)
                        if e:
                            dve.wait_ge(added, NE * t + e)
                        nc.vector.scalar_tensor_tensor(out=c.X[:, t, :],
                                                       in0=c.bank[:, n % 8, (e % 2) * D:(e % 2) * D + D],
                                                       scalar=gates[:, t, e:e + 1], in1=c.X[:, t, :],
                                                       op0=ALU.mult, op1=ALU.add).then_inc(added, 1)


def decoder_kernel(nc, dram):
    with ExitStack() as ctx:
        c = Core(nc, ctx, dram)
        load_block(c)
        attention_blocks(c)
        c.end_section()
        cross_attention_blocks(c)
        c.end_section()
        experts_blocks(c)
        c.end_section()
        gru_blocks(c)
        c.end_section()
        c.comb = c.sb(ctx, "comb", [P, KD, NE, D])
        ternary_cross_blocks(c)
        c.end_section()
        linear_experts_blocks(c)


def _tiles(w, p=P):
    return w.reshape(w.shape[0] // p, p, *w.shape[1:]).swapaxes(0, 1)


def _layout(i):
    a = {k: np.asarray(v) for k, v in i.items()}
    f = np.float32
    cols = np.zeros((P, N_COLS), f)

    def put(name, v):
        lo, hi = COLS[name]
        cols[:v.shape[0], lo:hi] = v

    put("conv_w", a["L0_attn_conv_w"].reshape(KD, P, 4).swapaxes(0, 1).reshape(P, KD * 4))
    for name, key in (("conv_b", "L0_attn_conv_b"), ("g_b", "L0_attn_g_b"), ("bq", "L0_xattn_bq"),
                      ("bk", "L0_xattn_bk"), ("bv", "L0_xattn_bv"), ("b_f", "L1_attn_b_f"),
                      ("b_d2v", "L1_xattn_b_d2v"), ("b_img", "L1_xattn_b_img"), ("b_txt", "L1_xattn_b_txt"),
                      ("b_att0", "L1_xattn_b_att0"), ("b_att1", "L1_xattn_b_att1"), ("b_f1", "L1_xattn_b_f1")):
        put(name, a[key].reshape(-1, P).T)
    put("freqs", a["L0_attn_freqs"].reshape(-1, P).T)
    put("gamma", a["L0_attn_gamma"].reshape(H0, 1))
    rows = np.zeros((P, N_ROWS), f)
    for name, v in (("ln_g", a["L0_attn_ln_g"]), ("ln_b", a["L0_attn_ln_b"]), ("bo", a["L0_xattn_bo"]),
                    ("b_f2", a["L1_xattn_b_f2"]), ("expert_bias", a["L0_ffn_expert_bias"]),
                    ("steps", np.arange(T, dtype=f)), ("expert_index", np.arange(NE_ALL, dtype=f))):
        lo, hi = ROWS[name]
        rows[:, lo:hi] = np.broadcast_to(v, (P, hi - lo))
    head_in = np.zeros((P, ET, 32), f)
    head_out = np.zeros((P, ET, P), f)
    per = E0 // H0
    for e in range(ET):
        for p in range(P):
            h = (e * P + p) // per
            head_in[p, e, h] = 1.0
            for g in range(P // 32):
                head_out[32 * g + h, e, p] = 1.0
    return {
        "x": a["x"].reshape(N, D),
        "columns": cols,
        "rows": rows,
        "ident": np.eye(P, dtype=f),
        "head_in": head_in,
        "head_out": head_out,
        "a0_wq": _tiles(a["L0_attn_qk_w"].T),
        "a0_wv": _tiles(a["L0_attn_v_w"].T),
        "a0_wg": _tiles(a["L0_attn_g_w"].T),
        "a0_wo": _tiles(a["L0_attn_o_w"].T),
        "ctx_f": _tiles(a["ctx_768"].reshape(N, CTX).T, CK),
        "x_wq": _tiles(a["L0_xattn_Wq"]),
        "x_wk": _tiles(a["L0_xattn_Wk"], CK),
        "x_wv": _tiles(a["L0_xattn_Wv"], CK),
        "x_wo": _tiles(a["L0_xattn_Wo"]),
        "e0_gate": _tiles(a["L0_ffn_gate_w"].T),
        "e0_w1": np.stack([_tiles(w.T) for w in a["L0_ffn_w1"]]),
        "e0_w2": np.stack([_tiles(w.T) for w in a["L0_ffn_w2"]]),
        "g_wf": _tiles(a["L1_attn_W_f"].T),
        "g_wd": _tiles(a["L1_attn_W_down"].T),
        "t_d2v": _tiles(a["L1_xattn_W_d2v"].T, CK),
        "t_img": _tiles(a["L1_xattn_W_img"].T),
        "t_txt": _tiles(a["L1_xattn_W_txt"].T),
        "t_att0": _tiles(a["L1_xattn_W_att0"].T),
        "t_att1": _tiles(a["L1_xattn_W_att1"].T),
        "t_f1": _tiles(a["L1_xattn_W_f1"].T),
        "t_f2": _tiles(a["L1_xattn_W_f2"].T),
        "e1_gate": _tiles(a["L1_ffn_w_gate"].T),
        "e1_w_in": np.stack([_tiles(w) for w in a["L1_ffn_w_in"]]),
        "e1_w_out": np.stack([_tiles(w.T) for w in a["L1_ffn_w_out"]]),
    }


def kernel(**inputs):
    import concourse.bacc as _bacc
    from concourse.bass_utils import run_bass_kernel_spmd as _run

    nc = _bacc.Bacc("TRN2", target_bir_lowering=False, num_devices=1)
    arrays, dram = {}, {}
    for name, v in _layout(inputs).items():
        v = np.ascontiguousarray(v)
        arrays[f"in_{name}_dram"] = v
        dram[name] = nc.dram_tensor(f"in_{name}_dram", v.shape, mybir.dt.from_np(v.dtype), kind="ExternalInput").ap()
    dram["out"] = nc.dram_tensor("out_dram", (N, D), F32, kind="ExternalOutput").ap()
    dram["split"] = nc.dram_tensor("split_scratch", (2, 3, D, N), BF16, kind="Internal").ap()
    dram["negmax"] = nc.dram_tensor("negmax_scratch", (B, 3, HX * TB, P), BF16, kind="Internal").ap()
    decoder_kernel(nc, dram)
    r = _run(nc, [arrays], core_ids=[0])
    return r.results[0]["out_dram"].reshape(B, T, D)
```

```python
from contextlib import ExitStack

import numpy as np
import concourse.bass as bass
from concourse import mybir

F32 = mybir.dt.float32
BF16 = mybir.dt.bfloat16
F32R = mybir.dt.float32r
ALU = mybir.AluOpType
ACT = mybir.ActivationFunctionType
AX = mybir.AxisListType
RED = bass.bass_isa.ReduceOp

P = 128
B = 4
T = 512
N = B * T
NT = N // P
TB = T // P
D = 256
KD = D // P
E0 = 512
ET = E0 // P
H0 = 16
HX = 16
DX = D // HX
CTX = 192
CK = CTX // 2
NE = 8
NE_ALL = 12
FF0 = 512
FF1 = 1024
EG = 384
GT = EG // P
FX = 1024
CLAMP = 10000.0
MAGIC = 12582912.0
TWO_PI_HI = 6.28125
TWO_PI_MID = 0.0019350051879882812
TWO_PI_LO = 2.0 * np.pi - TWO_PI_HI - TWO_PI_MID
EPS = 1e-5

COLS = {}
_at = 0
for _name, _n in (("conv_w", KD * 4), ("conv_b", KD), ("g_b", ET), ("freqs", ET), ("bq", KD), ("bk", KD),
                  ("bv", KD), ("b_f", 2 * GT), ("b_d2v", KD), ("b_img", KD), ("b_txt", KD), ("b_att0", 1),
                  ("b_att1", 1), ("b_f1", FX // P), ("gamma", 1)):
    COLS[_name] = (_at, _at + _n)
    _at += _n
N_COLS = _at
ROWS = {}
_at = 0
for _name, _n in (("ln_g", D), ("ln_b", D), ("bo", D), ("b_f2", D), ("expert_bias", NE_ALL),
                  ("steps", T), ("expert_index", NE_ALL)):
    ROWS[_name] = (_at, _at + _n)
    _at += _n
N_ROWS = _at


class Core:

    def __init__(self, nc, ctx, dram):
        self.nc, self.ctx, self.dram = nc, ctx, dram
        self.tallies = {}
        self.section_sems = []
        self.saved = nc.alloc_semaphore(name="saved")
        self.bank = ctx.enter_context(nc.psum_tensor("bank", [P, 8, 512], F32))
        self.X = self.sb(ctx, "X", [P, NT, D])
        self.xn = self.sb(ctx, "xn", [P, NT, D])
        self.xn_f = self.sb(ctx, "xn_f", [P, KD, N])
        self.ident = self.sb(ctx, "ident", [P, P])
        self.cols = self.sb(ctx, "cols", [P, N_COLS])
        self.rows = self.sb(ctx, "rows", [P, N_ROWS])
        self.eps = self.sb(ctx, "eps", [P, 1])

    def sb(self, ctx, name, shape, dt=F32):
        return ctx.enter_context(self.nc.sbuf_tensor(name, shape, dt))

    def sem(self, name):
        handle = self.nc.alloc_semaphore(name=name)
        self.section_sems.append(handle)
        return handle

    def end_section(self):
        self.nc.clear_and_free_semaphores(self.section_sems)
        self.section_sems = []
        self.nc.all_engine_barrier()

    def tally(self, name, total):
        if name not in self.tallies:
            self.tallies[name] = [self.nc.alloc_semaphore(name=name), 0]
        sem, before = self.tallies[name]
        self.tallies[name][1] += total
        return sem, before

    def col(self, name, i=0, n=1, p=P):
        a = COLS[name][0] + i
        return self.cols[0:p, a:a + n]

    def row(self, name):
        a, b = ROWS[name]
        return self.rows[:, a:b]


def load_block(c):
    nc = c.nc
    loaded = c.sem("loaded")
    eps_set = c.sem("eps_set")
    with nc.Block() as block:
        @block.sync
        def _(sp):
            sp.dma_start(c.X[:, :, :], c.dram["x"].rearrange("(t p) d -> p t d", p=P)).then_inc(loaded, 16)
            sp.dma_start(c.ident[:, :], c.dram["ident"]).then_inc(loaded, 16)
            sp.dma_start(c.cols[:, :], c.dram["columns"]).then_inc(loaded, 16)
            sp.dma_start(c.rows[:, :], c.dram["rows"]).then_inc(loaded, 16)
            sp.wait_ge(loaded, 64)

        @block.vector
        def _(dve):
            nc.vector.memset(c.eps[:, :], EPS).then_inc(eps_set, 1)


def norm_block(c, tag, put=None, load_ahead=None, split_weights=None):
    nc = c.nc
    if put is None:
        def put(k, b):
            return c.xn_f[:, k, b * T:(b + 1) * T]
    moments_in, moments_in0 = c.tally("norm_moments_in", NT)
    moments, moments0 = c.tally("norm_moments", NT)
    std, std0 = c.tally("norm_std", B)
    rstd, rstd0 = c.tally("norm_rstd", B)
    normed, normed0 = c.tally("norm_normed", NT)
    turned, turned0 = c.tally("norm_turned", KD * B)
    stored, stored0 = c.tally("norm_stored", KD * B)
    with ExitStack() as ctx:
        parts = c.sb(ctx, tag + "_parts", [P, NT, 6])
        mom = c.sb(ctx, tag + "_mom", [P, NT, 2])
        sd = c.sb(ctx, tag + "_sd", [P, NT])
        rs = c.sb(ctx, tag + "_rs", [P, NT])
        with nc.Block() as block:
            if load_ahead is not None:
                @block.sync
                def _(sp):
                    load_ahead(sp)

            if split_weights is not None:
                @block.gpsimd
                def _(pool):
                    split_weights(pool)

            @block.vector
            def _(dve):
                def stats(b):
                    for t in range(TB * b, TB * b + TB):
                        nc.vector.bn_stats(parts[:, t, :], c.X[:, t, :]).then_inc(moments_in, 1)
                    for t in range(TB * b, TB * b + TB):
                        dve.wait_ge(moments_in, moments_in0 + t + 1)
                        nc.vector.bn_aggr(mom[:, t, :], parts[:, t, :]).then_inc(moments, 1)

                def scale(b):
                    dve.wait_ge(std, std0 + b + 1)
                    nc.vector.reciprocal(rs[:, TB * b:TB * b + TB], sd[:, TB * b:TB * b + TB]).then_inc(rstd, 1)
                    dve.wait_ge(rstd, rstd0 + b + 1)
                    for t in range(TB * b, TB * b + TB):
                        nc.vector.tensor_scalar(c.xn[:, t, :], c.X[:, t, :], mom[:, t, 0:1], rs[:, t:t + 1],
                                                ALU.subtract, ALU.mult).then_inc(normed, 1)

                stats(0)
                for b in range(B):
                    if b + 1 < B:
                        stats(b + 1)
                    scale(b)

            @block.scalar
            def _(act):
                def root(b):
                    act.wait_ge(moments, moments0 + TB * (b + 1))
                    nc.scalar.activation(sd[:, TB * b:TB * b + TB], mom[:, TB * b:TB * b + TB, 1], ACT.Sqrt,
                                         bias=c.eps[:, 0:1]).then_inc(std, 1)

                root(0)
                for b in range(B):
                    if b + 1 < B:
                        root(b + 1)
                    for k in range(KD):
                        act.wait_ge(turned, turned0 + KD * b + k + 1)
                        src = c.bank[:, KD * b + k, :]
                        if len(put(k, b).shape) == 3:
                            src = src.rearrange("p (a t) -> p a t", a=1)
                        nc.scalar.activation(put(k, b), src, ACT.Copy).then_inc(stored, 1)

            @block.tensor
            def _(pe):
                for b in range(B):
                    pe.wait_ge(normed, normed0 + TB * (b + 1))
                    for k in range(KD):
                        for i in range(TB):
                            tr = nc.tensor.transpose(c.bank[:, KD * b + k, i * P:(i + 1) * P],
                                                     c.xn[:, TB * b + i, k * P:(k + 1) * P], c.ident[:, :])
                        tr.then_inc(turned, 1)


def attention_blocks(c):
    nc, dram = c.nc, c.dram
    with ExitStack() as ctx:
        wo = c.sb(ctx, "a0_wo", [P, ET, D])
        wq = c.sb(ctx, "a0_wq", [P, KD, E0])
        wv = c.sb(ctx, "a0_wv", [P, KD, E0])
        wg = c.sb(ctx, "a0_wg", [P, KD, E0])
        head_in = c.sb(ctx, "a0_head_in", [P, ET, 32])
        head_out = c.sb(ctx, "a0_head_out", [P, ET, P])
        xc = c.sb(ctx, "a0_xc", [P, KD, B, T])
        cos = c.sb(ctx, "a0_cos", [P, ET, T])
        decay = c.sb(ctx, "a0_decay", [P, ET, T])
        undecay = c.sb(ctx, "a0_undecay", [P, ET, T])
        gate = c.sb(ctx, "a0_gate", [P, ET, B, T])
        half_pi = c.sb(ctx, "a0_half_pi", [P, 1])
        with ExitStack() as ctx2:
            xpad = c.sb(ctx2, "a0_xpad", [P, KD, B, 3 + T])
            pad_set = c.sem("a0_pad_set")
            with nc.Block() as block:
                @block.gpsimd
                def _(pool):
                    nc.gpsimd.memset(xpad[:, :, :, 0:3], 0.0).then_inc(pad_set, 1)
            gate_weights = c.sem("a0_gate_weights")
            weights = c.sem("a0_weights")

            def load_ahead(sp):
                for dst, name in ((wg, "a0_wg"), (head_out, "head_out")):
                    sp.dma_start(dst[:, :, :], dram[name]).then_inc(gate_weights, 16)
                for dst, name in ((wq, "a0_wq"), (head_in, "head_in"), (wv, "a0_wv"), (wo, "a0_wo")):
                    sp.dma_start(dst[:, :, :], dram[name]).then_inc(weights, 16)

            norm_block(c, "n0", lambda k, b: xpad[:, k, b:b + 1, 3:3 + T], load_ahead)

            conv_sem = c.sem("a0_conv")
            angle_sem = c.sem("a0_angle")
            abs_sem = c.sem("a0_angle_abs")
            cos_sem = c.sem("a0_cos_ready")
            decay_rows = c.sem("a0_decay_rows")
            bank_full = c.sem("a0_bank_full")
            bank_read = c.sem("a0_bank_read")
            decayed = c.sem("a0_gate_decayed")
            off_sem = c.sem("a0_offset")
            ang = c.sb(ctx2, "a0_ang", [P, ET, T])
            turns = c.sb(ctx2, "a0_turns", [P, ET, T])
            gam = c.sb(ctx2, "a0_gam", [32, T])
            dec = c.sb(ctx2, "a0_dec", [32, 2, T])
            dece = c.sb(ctx2, "a0_dece", [32, T])
            zero = c.sb(ctx2, "a0_zero", [32, T])
            with nc.Block() as block:
                @block.sync
                def _(sp):
                    sp.wait_ge(weights, 64)

                order = ([("gate", u) for u in range(ET)] + [("spread", s) for s in range(2 * ET)]
                         + [("gate", u) for u in range(ET, B * ET)])

                @block.vector
                def _(dve):
                    def convolve(b):
                        for k in range(KD):
                            nc.vector.tensor_scalar(xc[:, k, b], xpad[:, k, b, 3:3 + T], c.col("conv_w", 4 * k + 3),
                                                    c.col("conv_b", k), ALU.mult, ALU.add).then_inc(conv_sem, 1)
                        for j in range(3):
                            for k in range(KD):
                                dve.wait_ge(conv_sem, KD * (4 * b + j) + k + 1)
                                nc.vector.scalar_tensor_tensor(out=xc[:, k, b], in0=xpad[:, k, b, j:j + T],
                                                               scalar=c.col("conv_w", 4 * k + j), in1=xc[:, k, b],
                                                               op0=ALU.mult, op1=ALU.add).then_inc(conv_sem, 1)

                    convolve(0)
                    nc.vector.memset(zero[:, :], 0.0).then_inc(decay_rows, 1)
                    nc.vector.memset(dec[:, 0, 0:1], 1.0).then_inc(decay_rows, 1)
                    nc.vector.memset(half_pi[:, :], float(np.pi / 2)).then_inc(decay_rows, 1)
                    dve.wait_ge(decay_rows, 3)
                    nc.vector.tensor_scalar(gam[:, :], zero[:, :], c.col("gamma", p=32), None,
                                            ALU.add).then_inc(decay_rows, 1)
                    dve.wait_ge(decay_rows, 4)
                    nc.vector.tensor_tensor_scan(dec[:, 0, 1:T], gam[:, 1:T], zero[:, 1:T], 1.0,
                                                 ALU.mult, ALU.add).then_inc(decay_rows, 1)
                    dve.wait_ge(decay_rows, 5)
                    nc.vector.tensor_scalar(dece[:, :], dec[:, 0, :], 1e-6, None, ALU.add).then_inc(decay_rows, 1)
                    dve.wait_ge(decay_rows, 6)
                    nc.vector.reciprocal(dec[:, 1, :], dece[:, :]).then_inc(decay_rows, 1)
                    for b in range(1, B):
                        convolve(b)
                    for e in range(ET):
                        nc.vector.tensor_scalar(ang[:, e, :], c.row("steps"), c.col("freqs", e), None,
                                                ALU.mult).then_inc(angle_sem, 1)
                    dve.wait_ge(angle_sem, ET)
                    nc.vector.tensor_scalar(turns[:, :, :], ang[:, :, :], float(0.5 / np.pi), MAGIC,
                                            ALU.mult, ALU.add).then_inc(angle_sem, 1)
                    dve.wait_ge(angle_sem, ET + 1)
                    nc.vector.tensor_scalar(turns[:, :, :], turns[:, :, :], MAGIC, None,
                                            ALU.subtract).then_inc(angle_sem, 1)
                    for i, part in enumerate((TWO_PI_HI, TWO_PI_MID, TWO_PI_LO)):
                        dve.wait_ge(angle_sem, ET + 2 + i)
                        nc.vector.scalar_tensor_tensor(out=ang[:, :, :], in0=turns[:, :, :], scalar=-float(part),
                                                       in1=ang[:, :, :], op0=ALU.mult,
                                                       op1=ALU.add).then_inc(angle_sem, 1)
                @block.tensor
                def _(pe):
                    pe.wait_ge(gate_weights, 32)
                    for n, (what, u) in enumerate(order):
                        if n >= 8:
                            pe.wait_ge(bank_read, n - 7)
                        if what == "gate":
                            b, e = divmod(u, ET)
                            pe.wait_ge(conv_sem, 4 * KD * (b + 1))
                            for k in range(KD):
                                mm = nc.tensor.matmul(c.bank[:, n % 8, :], wg[:, k, e * P:(e + 1) * P], xc[:, k, b, :],
                                                      start=(k == 0), stop=(k == KD - 1))
                        else:
                            w, e = divmod(u, ET)
                            pe.wait_ge(decay_rows, 7)
                            mm = nc.tensor.matmul(c.bank[:, n % 8, :], head_out[0:32, e, :], dec[:, w, :],
                                                  start=True, stop=True)
                        mm.then_inc(bank_full, 1)

                @block.scalar
                def _(act):
                    def cosines():
                        act.wait_ge(angle_sem, ET + 5)
                        nc.scalar.activation(turns[:, :, :], ang[:, :, :], ACT.Abs).then_inc(abs_sem, 1)
                        act.wait_ge(abs_sem, 1)
                        nc.scalar.activation(cos[:, :, :], turns[:, :, :], ACT.Sin, bias=half_pi[:, 0:1],
                                             scale=-1.0).then_inc(cos_sem, 1)

                    for n, (what, u) in enumerate(order):
                        if n == len(order) - 4:
                            cosines()
                        act.wait_ge(bank_full, n + 1)
                        if what == "gate":
                            b, e = divmod(u, ET)
                            nc.scalar.activation(gate[:, e, b, :], c.bank[:, n % 8, :], ACT.Sigmoid,
                                                 bias=c.col("g_b", e)).then_inc(bank_read, 1)
                        else:
                            w, e = divmod(u, ET)
                            nc.scalar.activation((decay, undecay)[w][:, e, :], c.bank[:, n % 8, :],
                                                 ACT.Copy).then_inc(bank_read, 1)

                @block.gpsimd
                def _(pool):
                    for t in range(NT):
                        nc.gpsimd.tensor_tensor(c.X[:, t, :], c.X[:, t, :], c.row("ln_b"),
                                                ALU.add).then_inc(off_sem, 1)
                    for u in range(B * ET):
                        b, e = divmod(u, ET)
                        pool.wait_ge(bank_read, order.index(("gate", u)) + 1)
                        pool.wait_ge(bank_read, order.index(("spread", e)) + 1)
                        nc.gpsimd.tensor_tensor(gate[:, e, b, :], gate[:, e, b, :], decay[:, e, :],
                                                ALU.mult).then_inc(decayed, 1)

        with ExitStack() as ctx2:
            qk = c.sb(ctx2, "a0_qk", [P, ET, B, 1 + T])
            sq = c.xn_f[:, :, :].rearrange("p k (e t) -> p k e t", e=ET)
            nrm = c.sb(ctx2, "a0_nrm", [P, T])
            rnrm = c.sb(ctx2, "a0_rnrm", [P, T])
            s1, s2, s3, w1 = (c.xn[:, 4 * i:4 * i + 4, :].rearrange("p (s a) d -> p s (a d)", s=2)
                              for i in range(4))
            q_ps = c.sem("a0_q_ps")
            q_zero = c.sem("a0_q_zero")
            q_copy = c.sem("a0_q_copy")
            q_square = c.sem("a0_q_square")
            norm_ps = c.sem("a0_norm_ps")
            norm_root = c.sem("a0_norm_root")
            norm_clip = c.sem("a0_norm_clip")
            norm_inv = c.sem("a0_norm_inv")
            inv_ps = c.sem("a0_inv_ps")
            q_normed = c.sem("a0_q_normed")
            v_ps = c.sem("a0_v_ps")
            phase_sum = c.sem("a0_phase_sum")
            valued = c.sem("a0_valued")
            gated = c.sem("a0_gated")
            scanned = c.sem("a0_scanned")
            undecayed = c.sem("a0_undecayed")
            mixed = c.sem("a0_mixed")
            U = B * ET
            HB = B // 2

            def half_rows(half):
                return slice(32 * HB * half, 32 * HB * (half + 1))

            with nc.Block() as block:
                @block.tensor
                def _(pe):
                    def queries(u):
                        b, e = divmod(u, ET)
                        if u >= 2:
                            pe.wait_ge(q_square, u - 1)
                            pe.wait_ge(q_copy, u - 1)
                        for k in range(KD):
                            mm = nc.tensor.matmul(c.bank[:, u % 2, :], wq[:, k, e * P:(e + 1) * P],
                                                  xc[:, k, b, :], start=(k == 0), stop=(k == KD - 1))
                        mm.then_inc(q_ps, 1)

                    def squares(b):
                        for e in range(ET):
                            pe.wait_ge(q_square, ET * b + e + 1)
                            mm = nc.tensor.matmul(c.bank[32 * b:32 * b + 32, 4, :], head_in[:, e, :],
                                                  sq[:, b % 2, e, :], start=(e == 0), stop=(e == ET - 1))
                        mm.then_inc(norm_ps, 1)

                    def inverse_and_value(u):
                        b, e = divmod(u, ET)
                        pe.wait_ge(norm_inv, b // HB + 1)
                        if u >= 2:
                            pe.wait_ge(q_normed, u - 1)
                        nc.tensor.matmul(c.bank[:, 2 + u % 2, :], head_out[32 * b:32 * b + 32, e, :],
                                         rnrm[32 * b:32 * b + 32, :], start=True, stop=True).then_inc(inv_ps, 1)
                        if u >= 3:
                            pe.wait_ge(valued, u - 2)
                        for k in range(KD):
                            mm = nc.tensor.matmul(c.bank[:, 5 + u % 3, :], wv[:, k, e * P:(e + 1) * P],
                                                  xc[:, k, b, :], start=(k == 0), stop=(k == KD - 1))
                        mm.then_inc(v_ps, 1)

                    for b in range(HB):
                        for e in range(ET):
                            queries(ET * b + e)
                        squares(b)
                    queries(HB * ET)
                    for i in range(HB * ET):
                        if i + 1 < HB * ET:
                            queries(HB * ET + i + 1)
                        if i % ET == ET - 1:
                            squares(HB + i // ET)
                        inverse_and_value(i)
                    for u in range(HB * ET, U):
                        inverse_and_value(u)

                @block.scalar
                def _(act):
                    for b in range(B):
                        for e in range(ET):
                            u = ET * b + e
                            act.wait_ge(q_ps, u + 1)
                            nc.scalar.activation(qk[:, e, b, 1:1 + T], c.bank[:, u % 2, :],
                                                 ACT.Copy).then_inc(q_copy, 1)
                            if b >= 2:
                                act.wait_ge(norm_ps, b - 1)
                            nc.scalar.activation(sq[:, b % 2, e, :], c.bank[:, u % 2, :],
                                                 ACT.Square).then_inc(q_square, 1)
                        if b % HB == HB - 1:
                            rows = half_rows(b // HB)
                            act.wait_ge(norm_ps, b + 1)
                            nc.scalar.activation(nrm[rows, :], c.bank[rows, 4, :], ACT.Sqrt).then_inc(norm_root, 1)

                @block.vector
                def _(dve):
                    def invert(half):
                        rows = half_rows(half)
                        dve.wait_ge(norm_root, half + 1)
                        nc.vector.tensor_scalar(nrm[rows, :], nrm[rows, :], 1e-12, None,
                                                ALU.max).then_inc(norm_clip, 1)
                        dve.wait_ge(norm_clip, half + 1)
                        nc.vector.reciprocal(rnrm[rows, :], nrm[rows, :]).then_inc(norm_inv, 1)

                    def unit_q(u):
                        b, e = divmod(u, ET)
                        dve.wait_ge(inv_ps, u + 1)
                        dve.wait_ge(q_copy, u + 1)
                        nc.vector.tensor_tensor(qk[:, e, b, 1:1 + T], qk[:, e, b, 1:1 + T], c.bank[:, 2 + u % 2, :],
                                                ALU.mult).then_inc(q_normed, 1)

                    def unit_v(u):
                        dve.wait_ge(v_ps, u + 1)
                        dve.wait_ge(phase_sum, u + 1)
                        if u >= 2:
                            dve.wait_ge(gated, u - 1)
                        nc.vector.tensor_tensor(s2[:, u % 2, :], c.bank[:, 5 + u % 3, :], s1[:, u % 2, :],
                                                ALU.mult).then_inc(valued, 1)

                    def unit_scan(u):
                        b, e = divmod(u, ET)
                        if u >= 2:
                            dve.wait_ge(mixed, u - 1)
                        nc.vector.tensor_tensor(w1[:, u % 2, :], qk[:, e, b, 1:1 + T], undecay[:, e, :],
                                                ALU.mult).then_inc(undecayed, 1)
                        dve.wait_ge(gated, u + 1)
                        nc.vector.tensor_tensor_scan(gate[:, e, b, :], s3[:, u % 2, :], s3[:, u % 2, :], 0.0,
                                                     ALU.add, ALU.bypass).then_inc(scanned, 1)

                    def unit_mix(u):
                        b, e = divmod(u, ET)
                        dve.wait_ge(scanned, u + 1)
                        dve.wait_ge(undecayed, u + 1)
                        nc.vector.tensor_tensor(gate[:, e, b, :], gate[:, e, b, :], w1[:, u % 2, :],
                                                ALU.mult).then_inc(mixed, 1)

                    for i in range(U + 2):
                        if i == 0:
                            invert(0)
                        if i == HB * ET:
                            invert(1)
                        if i < U:
                            unit_q(i)
                        if 1 <= i <= U:
                            unit_v(i - 1)
                        if i >= 2:
                            unit_scan(i - 2)
                            unit_mix(i - 2)

                @block.gpsimd
                def _(pool):
                    nc.gpsimd.memset(qk[:, :, :, 0:1], 0.0).then_inc(q_zero, 1)
                    pool.wait_ge(q_zero, 1)

                    def unit_phase(u):
                        b, e = divmod(u, ET)
                        pool.wait_ge(q_normed, u + 1)
                        if u >= 2:
                            pool.wait_ge(valued, u - 1)
                        nc.gpsimd.tensor_tensor(s1[:, u % 2, :], cos[:, e, :], qk[:, e, b, 0:T],
                                                ALU.add).then_inc(phase_sum, 1)

                    def unit_gate(u):
                        b, e = divmod(u, ET)
                        pool.wait_ge(valued, u + 1)
                        if u >= 2:
                            pool.wait_ge(scanned, u - 1)
                        nc.gpsimd.tensor_tensor(s3[:, u % 2, :], s2[:, u % 2, :], gate[:, e, b, :],
                                                ALU.mult).then_inc(gated, 1)

                    for i in range(U + 1):
                        if i < U:
                            unit_phase(i)
                        if i >= 1:
                            unit_gate(i - 1)

        with ExitStack() as ctx2:
            parts = c.sb(ctx2, "a0_parts", [P, NT, 6])
            mom = c.sb(ctx2, "a0_mom", [P, NT, 2])
            sd = c.sb(ctx2, "a0_sd", [P, NT])
            rs = c.sb(ctx2, "a0_rs", [P, NT])
            y = c.sb(ctx2, "a0_y", [P, NT, D])
            out_ps = c.sem("a0_out_ps")
            parts_sem = c.sem("a0_parts_in")
            mom_sem = c.sem("a0_mom_in")
            std_sem = c.sem("a0_std")
            rstd_sem = c.sem("a0_rstd")
            y_sem = c.sem("a0_y_ready")
            gain_sem = c.sem("a0_gain")
            added = c.sem("a0_added")

            def out(t):
                return c.bank[:, t % 8, 0:D]

            with nc.Block() as block:
                @block.tensor
                def _(pe):
                    for t in range(NT):
                        b, i = divmod(t, TB)
                        if t >= 8:
                            pe.wait_ge(y_sem, t - 7)
                        for e in range(ET):
                            mm = nc.tensor.matmul(out(t), gate[:, e, b, i * P:(i + 1) * P], wo[:, e, :],
                                                  start=(e == 0), stop=(e == ET - 1))
                        mm.then_inc(out_ps, 1)

                @block.scalar
                def _(act):
                    for b in range(B):
                        act.wait_ge(mom_sem, TB * (b + 1))
                        nc.scalar.activation(sd[:, TB * b:TB * b + TB], mom[:, TB * b:TB * b + TB, 1], ACT.Sqrt,
                                             bias=c.eps[:, 0:1]).then_inc(std_sem, 1)

                @block.vector
                def _(dve):
                    def add(b):
                        for t in range(TB * b, TB * b + TB):
                            dve.wait_ge(gain_sem, t + 1)
                            nc.vector.tensor_tensor(c.X[:, t, :], c.X[:, t, :], y[:, t, :],
                                                    ALU.add).then_inc(added, 1)

                    for b in range(B):
                        ts = range(TB * b, TB * b + TB)
                        for t in ts:
                            dve.wait_ge(out_ps, t + 1)
                            nc.vector.bn_stats(parts[:, t, :], out(t)).then_inc(parts_sem, 1)
                        for t in ts:
                            dve.wait_ge(parts_sem, t + 1)
                            nc.vector.bn_aggr(mom[:, t, :], parts[:, t, :]).then_inc(mom_sem, 1)
                        dve.wait_ge(std_sem, b + 1)
                        nc.vector.reciprocal(rs[:, TB * b:TB * b + TB],
                                             sd[:, TB * b:TB * b + TB]).then_inc(rstd_sem, 1)
                        dve.wait_ge(rstd_sem, b + 1)
                        for t in ts:
                            nc.vector.tensor_scalar(y[:, t, :], out(t), mom[:, t, 0:1], rs[:, t:t + 1],
                                                    ALU.subtract, ALU.mult).then_inc(y_sem, 1)
                        if b:
                            add(b - 1)
                    add(B - 1)

                @block.gpsimd
                def _(pool):
                    for t in range(NT):
                        pool.wait_ge(y_sem, t + 1)
                        nc.gpsimd.tensor_tensor(y[:, t, :], y[:, t, :], c.row("ln_g"),
                                                ALU.mult).then_inc(gain_sem, 1)


HG = 4
MG = HG
STACKS = 2
LAG = 2 * MG
SPLIT_Q = (0, 0, 1, 0, 2, 1)
SPLIT_K = (0, 1, 0, 2, 0, 1)
NS = len(SPLIT_Q)
KS = NS * DX
RM = KS


def cross_attention_blocks(c):
    nc, dram = c.nc, c.dram
    PLAIN, CLIPPED, UNIFORM = 0, 1, 2
    U = 2 * B * KD

    def place(u):
        b, r = divmod(u, 2 * KD)
        w, m = divmod(r, KD)
        return b, w, m

    with ExitStack() as ctx:
        case = c.sb(ctx, "x_case", [P, 1], mybir.dt.int32)
        case_sem = c.sem("x_case_step")
        CASE_STEPS = 8
        qst = [c.sb(ctx, "x_qst0", [P, HX, T], BF16)]
        kst = [c.sb(ctx, "x_kst0", [P, HX, T], BF16)]
        q_in = [c.sem(f"x_q_in{i}") for i in range(STACKS)]
        k_in = [c.sem(f"x_k_in{i}") for i in range(STACKS)]

        def load_stacks(sp, b):
            s = b % STACKS
            for j in range(NS):
                for w, dst, order, sem in ((0, qst, SPLIT_Q, q_in), (1, kst, SPLIT_K, k_in)):
                    src = dram["split"][w, order[j], :, b * T:(b + 1) * T]
                    sp.dma_start(dst[s][j * DX:(j + 1) * DX, :, :],
                                 src.rearrange("(h d) t -> d h t", d=DX)).then_inc(sem[s], 16)

        values = c.sb(ctx, "x_values", [P, NT, HX, 32])
        O = c.xn
        with ExitStack() as ctx2:
            wq = c.sb(ctx2, "x_wq", [P, KD, D])
            wk = c.sb(ctx2, "x_wk", [CK, 2, D])
            wv = c.sb(ctx2, "x_wv", [CK, 2, D])
            ctx_f = c.sb(ctx2, "x_ctx", [CK, 2, N])
            full = c.sb(ctx2, "x_full", [P, 4, T])
            rest = c.sb(ctx2, "x_rest", [P, 4, T])
            parts = c.sb(ctx2, "x_split", [P, 2, 3, KD, N], BF16)
            bq4 = c.sb(ctx2, "x_bq4", [P, KD])
            weights = c.sem("x_weights")
            ones_set = c.sem("x_ones_set")
            bq_sem = c.sem("x_bq4_ready")
            proj_ps = c.sem("x_proj_ps")
            full_sem = c.sem("x_full_ready")
            high = c.sem("x_high")
            rest1 = c.sem("x_rest_ready")
            mid = c.sem("x_mid")
            low = c.sem("x_low")
            v_ps = c.sem("x_v_ps")
            v_sem = c.sem("x_v_ready")
            spilled = [c.sem(f"x_spilled{b}") for b in range(B)]
            unit_sum = c.sb(ctx2, "x_unit_sum", [P, U])
            unit_top = c.sb(ctx2, "x_unit_top", [P, 2, B * KD])
            finite = c.sb(ctx2, "x_finite", [P, U])
            limits = c.sb(ctx2, "x_limits", [P, 2, 3])
            bound = c.sb(ctx2, "x_bound", [P, 1])
            limits_sem = c.sem("x_limits_ready")
            top_sem = c.sem("x_unit_top_ready")

            def load_ahead(sp):
                for dst, name in ((wq, "x_wq"), (wk, "x_wk"), (wv, "x_wv"), (ctx_f, "ctx_f")):
                    sp.dma_start(dst[:, :, :], dram[name]).then_inc(weights, 16)

            norm_block(c, "n1", load_ahead=load_ahead)
            with nc.Block() as block:
                @block.sync
                def _(sp):
                    for b in range(B):
                        sp.wait_ge(low, 2 * KD * (b + 1))
                        sp.wait_ge(mid, 2 * KD * (b + 1))
                        sp.wait_ge(high, 2 * KD * (b + 1))
                        for w in range(2):
                            for s in range(3):
                                for m in range(KD):
                                    sp.dma_start(dram["split"][w, s, m * P:(m + 1) * P, b * T:(b + 1) * T],
                                                 parts[:, w, s, m, b * T:(b + 1) * T]).then_inc(spilled[b], 16)
                        if b == 1:
                            sp.wait_ge(spilled[0], 16 * 6 * KD)
                            sp.wait_ge(ones_set, 2)
                            load_stacks(sp, 0)
                    for b in range(1, B):
                        sp.wait_ge(spilled[b], 16 * 6 * KD)
                    sp.wait_ge(q_in[0], 16 * NS)
                    sp.wait_ge(k_in[0], 16 * NS)

                @block.tensor
                def _(pe):
                    pe.wait_ge(weights, 64)
                    for u in range(U):
                        b, w, m = place(u)
                        if u >= 4:
                            pe.wait_ge(high, u - 3)
                        for k in range(2):
                            lhs = (wq, wk)[w][:, k, m * P:(m + 1) * P]
                            rhs = (c.xn_f, ctx_f)[w][:, k, b * T:(b + 1) * T]
                            mm = nc.tensor.matmul(c.bank[:, u % 4, :], lhs, rhs, start=(k == 0), stop=(k == 1))
                        mm.then_inc(proj_ps, 1)
                        t = u
                        if t >= 4:
                            pe.wait_ge(v_sem, t - 3)
                        for k in range(2):
                            mm = nc.tensor.matmul(c.bank[:, 4 + t % 4, 0:D], ctx_f[:, k, t * P:(t + 1) * P],
                                                  wv[:, k, :], start=(k == 0), stop=(k == 1))
                        mm.then_inc(v_ps, 1)

                @block.scalar
                def _(act):
                    act.wait_ge(bq_sem, 1)
                    for u in range(U):
                        b, w, m = place(u)
                        act.wait_ge(proj_ps, u + 1)
                        if u >= 4:
                            act.wait_ge(rest1, u - 3)
                            act.wait_ge(top_sem, u - 3)
                        bias = bq4[:, m:m + 1] if w == 0 else c.col("bk", m)
                        scale = float(DX) ** -0.5 if w == 0 else 1.0
                        nc.scalar.activation(full[:, u % 4, :], c.bank[:, u % 4, :], ACT.Identity, bias=bias,
                                             scale=scale, accum_out=unit_sum[:, u:u + 1]).then_inc(full_sem, 1)
                        nc.scalar.activation(parts[:, w, 0, m, b * T:(b + 1) * T], c.bank[:, u % 4, :],
                                             ACT.Identity, bias=bias, scale=scale).then_inc(high, 1)
                        act.wait_ge(v_ps, u + 1)
                        nc.scalar.activation(values[:, u, :, 0:DX],
                                             c.bank[:, 4 + u % 4, 0:D].rearrange("p (h d) -> p h d", h=HX),
                                             ACT.Copy).then_inc(v_sem, 1)

                @block.vector
                def _(dve):
                    nc.vector.tensor_scalar(bq4[:, :], c.col("bq", 0, KD), float(DX) ** -0.5, None,
                                            ALU.mult).then_inc(bq_sem, 1)
                    for u in range(U):
                        b, w, m = place(u)
                        cols = slice(b * T, (b + 1) * T)
                        dve.wait_ge(full_sem, u + 1)
                        nc.vector.tensor_reduce(unit_top[:, w, KD * b + m:KD * b + m + 1], full[:, u % 4, :], AX.X,
                                                ALU.max, apply_absolute_value=True).then_inc(top_sem, 1)
                        dve.wait_ge(high, u + 1)
                        if u >= 4:
                            dve.wait_ge(low, u - 3)
                        nc.vector.tensor_tensor(rest[:, u % 4, :], full[:, u % 4, :], parts[:, w, 0, m, cols],
                                                ALU.subtract).then_inc(rest1, 1)
                        dve.wait_ge(rest1, u + 1)
                        nc.vector.tensor_copy(parts[:, w, 1, m, cols], rest[:, u % 4, :]).then_inc(mid, 1)
                        dve.wait_ge(mid, u + 1)
                        nc.vector.tensor_tensor(parts[:, w, 2, m, cols], rest[:, u % 4, :],
                                                parts[:, w, 1, m, cols], ALU.subtract).then_inc(low, 1)

                    dve.wait_ge(top_sem, U)
                    nc.vector.tensor_scalar(finite[:, :], unit_sum[:, :], 0.0, 0.0, ALU.mult,
                                            ALU.is_equal).then_inc(case_sem, 1)
                    nc.vector.tensor_reduce(limits[:, 0, 0:2], unit_top[:, :, :], AX.X, ALU.max).then_inc(case_sem, 1)
                    dve.wait_ge(case_sem, 2)
                    nc.vector.tensor_reduce(bound[:, :], finite[:, :], AX.X, ALU.min).then_inc(case_sem, 1)
                    dve.wait_ge(case_sem, 3)
                    nc.vector.tensor_scalar(limits[:, 0, 2:3], bound[:, :], -1.0, 1.0, ALU.mult,
                                            ALU.add).then_inc(case_sem, 1)
                    dve.wait_ge(limits_sem, 1)
                    nc.vector.tensor_tensor(bound[:, :], limits[:, 1, 0:1], limits[:, 1, 1:2],
                                            ALU.mult).then_inc(case_sem, 1)
                    dve.wait_ge(case_sem, 5)
                    nc.vector.tensor_scalar(bound[:, :], bound[:, :], (CLAMP - 200.0) / DX, None,
                                            ALU.is_gt).then_inc(case_sem, 1)
                    nc.vector.tensor_scalar(limits[:, 1, 2:3], limits[:, 1, 2:3], float(UNIFORM), None,
                                            ALU.mult).then_inc(case_sem, 1)
                    dve.wait_ge(case_sem, 7)
                    nc.vector.tensor_tensor(case[:, :], bound[:, :], limits[:, 1, 2:3],
                                            ALU.max).then_inc(case_sem, 1)

                @block.gpsimd
                def _(pool):
                    nc.gpsimd.memset(kst[0][RM:P, :, :], 1.0).then_inc(ones_set, 1)
                    pool.wait_ge(ones_set, 1)
                    nc.gpsimd.memset(values[:, :, :, DX:32], 1.0).then_inc(ones_set, 1)
                    pool.wait_ge(ones_set, 2)
                    pool.wait_ge(case_sem, 4)
                    nc.gpsimd.partition_all_reduce(limits[:, 1, :], limits[:, 0, :], P,
                                                   RED.max).then_inc(limits_sem, 1)

        with ExitStack() as ctx2:
            qst.append(c.sb(ctx2, "x_qst1", [P, HX, T], BF16))
            kst.append(c.sb(ctx2, "x_kst1", [P, HX, T], BF16))
            mx = c.sb(ctx2, "x_mx", [P, 2, MG * TB])
            mcl = c.sb(ctx2, "x_mcl", [P, 2, MG * TB])
            neg = c.sb(ctx2, "x_neg", [MG * TB, 2, P])
            nparts = c.sb(ctx2, "x_nparts", [MG * TB, 2, 3, P], BF16)
            scratch = c.xn_f[:, :, :].rearrange("p k (a t) -> p (k a) t", t=T)
            floor, shifted, raw = scratch[:, 0:2, :], scratch[:, 2:6, :], scratch[:, 6:8, :]
            SLOTS = 27
            probs = c.sb(ctx2, "x_probs", [P, SLOTS, T])
            rsum = c.sb(ctx2, "x_rsum", [P, 2, TB * HG])
            neg_clamp = c.sb(ctx2, "x_neg_clamp", [P, 1])
            mean_w = raw[:, 0, 0:P]
            mean_ps = c.sem("x_mean_ps")
            mean_out = c.sem("x_mean_out")
            const_set = c.sem("x_const_set")
            score_ps = c.sem("x_score_ps")
            max_sem = c.sem("x_max")
            clip_sem = c.sem("x_clip")
            turn_ps = c.sem("x_turn_ps")
            neg_sem = c.sem("x_neg_ready")
            nhigh = c.sem("x_nhigh")
            nrest = c.sem("x_nrest")
            nmid = c.sem("x_nmid")
            nlow = c.sem("x_nlow")
            neg_out = c.sem("x_neg_out")
            neg_in = c.sem("x_neg_in")
            floor_ps = c.sem("x_floor_ps")
            floor_sem = c.sem("x_floor_ready")
            keyed_ps = c.sem("x_keyed_ps")
            shift_sem = c.sem("x_shift")
            exp_sem = c.sem("x_exp")
            pv_ps = c.sem("x_pv_ps")
            raw_sem = c.sem("x_raw")
            raw_turned = c.sem("x_raw_turned")
            rsum_sem = c.sem("x_rsum_ready")
            out_sem = c.sem("x_out")
            NH = B * HX
            NM = NH // MG

            RING = 3

            def score_ring(clips):
                return RING - 1 if clips else RING

            def s_bank(n, clips):
                return c.bank[:, n % score_ring(clips), :]

            def t_bank(n):
                return c.bank[:, RING + n % RING, :]

            FB = RING - 1

            def out_bank(q):
                return c.bank[:, 6 + q % 2, :]

            def turn_bank(m):
                return c.bank[0:MG * TB, 6 + (m + 1) % 2, 0:P]

            NG = NH // HG

            def read_case(engine):
                engine.wait_ge(case_sem, CASE_STEPS)
                return engine.value_load(case[0:1, 0:1], min_val=0, max_val=UNIFORM)

            with nc.Block() as block:
                @block.sync
                def _(sp):
                    def stacks(b):
                        if b >= STACKS:
                            sp.wait_ge(keyed_ps, TB * HX * (b - STACKS + 1))
                        load_stacks(sp, b)

                    def maxima(m):
                        b, i = divmod(m, NM // B)
                        rows = dram["negmax"][b, :, i * MG * TB:(i + 1) * MG * TB, :]
                        sp.wait_ge(nhigh, m + 1)
                        sp.wait_ge(nmid, m + 1)
                        sp.wait_ge(nlow, m + 1)
                        sp.dma_start(rows.rearrange("s r q -> r s q"), nparts[:, m % 2, :, :]).then_inc(neg_out, 16)
                        sp.wait_ge(neg_out, 16 * (m + 1))
                        sp.dma_start(qst[b % STACKS][RM:RM + 3, i * MG:(i + 1) * MG, :],
                                     rows.rearrange("s (h i) q -> s h (i q)", i=TB)).then_inc(neg_in, 16)

                    for b in range(1, STACKS):
                        stacks(b)
                    case_of = read_case(sp)
                    with sp.If(case_of < UNIFORM):
                        for m in range(NM):
                            b, i = divmod(m, NM // B)
                            if i == 1 and 1 <= b and b + 1 < B:
                                stacks(b + 1)
                            maxima(m)
                    for s in range(STACKS):
                        for sem in (q_in[s], k_in[s]):
                            sp.wait_ge(sem, 16 * NS)

                STEPS = 2 * (NH + LAG + HG) + 2

                def row_at(k):
                    q = k // (2 * HG) - 1
                    return (q, k % (2 * HG) // 2) if k % 2 == 0 and 0 <= q < NG else None

                def done_at(k):
                    q = k // (2 * HG) - 2
                    return q if k % (2 * HG) == 0 and 0 <= q < NG else None

                def turns_at(j):
                    m = (j - 2) // (2 * MG) - 1
                    return m if (j - 2) % (2 * MG) == 0 and 0 <= m < NM else None

                @block.tensor
                def _(pe):
                    def score(n, clips):
                        b, h = divmod(n // TB, HX)
                        if n % (TB * HX) == 0:
                            pe.wait_ge(q_in[b % STACKS], 16 * NS * (b // STACKS + 1))
                            pe.wait_ge(k_in[b % STACKS], 16 * NS * (b // STACKS + 1))
                        if n >= score_ring(clips):
                            pe.wait_ge(max_sem, n - score_ring(clips) + 1)
                        q0 = (n % TB) * P
                        nc.tensor.matmul(s_bank(n, clips), qst[b % STACKS][0:KS, h, q0:q0 + P],
                                         kst[b % STACKS][0:KS, h, :], start=True, stop=True).then_inc(score_ps, 1)

                    def turn(m):
                        pe.wait_ge(clip_sem, m + 1)
                        if m >= 3:
                            pe.wait_ge(out_sem, m - 2)
                        nc.tensor.transpose(turn_bank(m), mcl[:, m % 2, :], c.ident[:, :]).then_inc(turn_ps, 1)

                    def floor_of(g):
                        b, h = divmod(g, HX)
                        if h % MG == 0:
                            pe.wait_ge(neg_in, 16 * (g // MG + 1))
                        if g:
                            pe.wait_ge(floor_sem, g)
                        nc.tensor.matmul(c.bank[:, FB, :], kst[b % STACKS][RM:RM + 3, h, 0:P],
                                         qst[b % STACKS][RM:RM + 3, h, :], start=True,
                                         stop=True).then_inc(floor_ps, 1)

                    def turn_raw(q):
                        pe.wait_ge(raw_sem, q + 1)
                        for i in range(TB):
                            tr = nc.tensor.transpose(out_bank(q)[:, i * P:(i + 1) * P],
                                                     raw[:, q % 2, i * P:(i + 1) * P], c.ident[:, :])
                        tr.then_inc(raw_turned, 1)

                    def keyed(n, clips):
                        b, h = divmod(n // TB, HX)
                        if n >= RING:
                            pe.wait_ge(shift_sem if clips else exp_sem, n - RING + 1)
                        k0 = (n % TB) * P
                        nc.tensor.matmul(t_bank(n), kst[b % STACKS][0:RM + 3, h, k0:k0 + P],
                                         qst[b % STACKS][0:RM + 3, h, :], start=True,
                                         stop=True).then_inc(keyed_ps, 1)

                    def apply(q, i):
                        if i == 0:
                            pe.wait_ge(neg_sem, min(q + 2, NM))
                            if q >= 2:
                                pe.wait_ge(out_sem, q - 1)
                        pe.wait_ge(exp_sem, TB * (HG * (q + 1) - 1) + i + 1)
                        for a in range(HG):
                            b, h = divmod(HG * q + a, HX)
                            n = TB * (HG * q + a) + i
                            mm = nc.tensor.matmul(out_bank(q)[32 * a:32 * a + 32, :], values[:, TB * b + i, h, :],
                                                  probs[:, n % SLOTS, :], start=(i == 0), stop=(i == TB - 1))
                        mm.then_inc(pv_ps, 1)

                    def products(clips):
                        for j in range(STEPS):
                            k = j - 2 * LAG
                            if k == 0:
                                pe.wait_ge(const_set, STACKS)
                            if not clips and 0 <= k < 2 * NH and k % (2 * MG) == 0:
                                pe.wait_ge(neg_in, 16 * (k // (2 * MG) + 1))
                            for i in range(2):
                                if j < 2 * NH:
                                    score(2 * j + i, clips)
                                if i == 0 and turns_at(j) is not None:
                                    turn(turns_at(j))
                                if 0 <= k < 2 * NH:
                                    keyed(2 * k + i, clips)
                                if i == 0 and done_at(k) is not None:
                                    turn_raw(done_at(k))
                                if i == 0 and row_at(k) is not None:
                                    apply(*row_at(k))
                            if clips and k % 2 == 1 and 0 <= (k + 1) // 2 < NH:
                                floor_of((k + 1) // 2)

                    case_of = read_case(pe)
                    with pe.If(case_of == PLAIN):
                        products(False)
                    with pe.If(case_of == CLIPPED):
                        products(True)
                    with pe.If(case_of == UNIFORM):
                        pe.wait_ge(const_set, 1 + STACKS)
                        for b in range(B):
                            for t in range(TB):
                                mm = nc.tensor.matmul(c.bank[:, b, 0:D], mean_w, values[:, TB * b + t, :, 0:DX],
                                                      start=(t == 0), stop=(t == TB - 1))
                            mm.then_inc(mean_ps, 1)

                @block.scalar
                def _(act):
                    def negate(m):
                        act.wait_ge(turn_ps, m + 1)
                        if m >= 2:
                            act.wait_ge(nlow, m - 1)
                        nc.scalar.activation(neg[:, m % 2, :], turn_bank(m), ACT.Copy,
                                             scale=-1.0).then_inc(neg_sem, 1)

                    def floor_of(g):
                        act.wait_ge(floor_ps, g + 1)
                        if g >= 2:
                            act.wait_ge(shift_sem, TB * (g - 1))
                        nc.scalar.activation(floor[:, g % 2, :], c.bank[:, FB, :], ACT.Identity,
                                             bias=neg_clamp[:, 0:1]).then_inc(floor_sem, 1)

                    def weights_of(n, clips):
                        act.wait_ge(shift_sem if clips else keyed_ps, n + 1)
                        if n >= SLOTS:
                            last = n - SLOTS
                            act.wait_ge(pv_ps, TB * (last // (TB * HG)) + last % TB + 1)
                        src = shifted[:, n % 4, :] if clips else t_bank(n)
                        nc.scalar.activation(probs[:, n % SLOTS, :], src, ACT.Exp).then_inc(exp_sem, 1)

                    def take_raw(q):
                        act.wait_ge(pv_ps, TB * (q + 1))
                        if q >= 2:
                            act.wait_ge(raw_turned, q - 1)
                        nc.scalar.activation(raw[:, q % 2, :], out_bank(q), ACT.Copy).then_inc(raw_sem, 1)

                    def weigh(clips):
                        for j in range(STEPS):
                            k = j - 2 * LAG
                            if turns_at(j) is not None:
                                negate(turns_at(j))
                            if clips and k % 2 == 1 and 0 <= (k + 1) // 2 < NH:
                                floor_of((k + 1) // 2)
                            if done_at(k + 1) is not None:
                                take_raw(done_at(k + 1))
                            if 0 <= k < 2 * NH:
                                weights_of(2 * k, clips)
                                weights_of(2 * k + 1, clips)

                    act.wait_ge(const_set, 1)
                    case_of = read_case(act)
                    with act.If(case_of == PLAIN):
                        weigh(False)
                    with act.If(case_of == CLIPPED):
                        weigh(True)
                    with act.If(case_of == UNIFORM):
                        for b in range(B):
                            act.wait_ge(mean_ps, b + 1)
                            for t in range(TB * b, TB * b + TB):
                                nc.scalar.activation(O[:, t, :], c.bank[:, b, 0:D], ACT.Copy).then_inc(mean_out, 1)

                @block.vector
                def _(dve):
                    def maximum(n, clips):
                        m, i = divmod(n, TB * MG)
                        dve.wait_ge(score_ps, n + 1)
                        if m >= 2 and i == 0:
                            dve.wait_ge(clip_sem, m - 1)
                        nc.vector.tensor_reduce(mx[:, m % 2, i:i + 1], s_bank(n, clips), AX.X,
                                                ALU.max).then_inc(max_sem, 1)

                    def clip(m):
                        dve.wait_ge(max_sem, TB * MG * (m + 1))
                        if m >= 2:
                            dve.wait_ge(turn_ps, m - 1)
                        nc.vector.tensor_scalar(mcl[:, m % 2, :], mx[:, m % 2, :], CLAMP, -CLAMP, ALU.min,
                                                ALU.max).then_inc(clip_sem, 1)

                    def shift(n):
                        g = n // TB
                        dve.wait_ge(floor_sem, g + 1)
                        dve.wait_ge(keyed_ps, n + 1)
                        if n >= 4:
                            dve.wait_ge(exp_sem, n - 3)
                        nc.vector.scalar_tensor_tensor(
                            out=shifted[:, n % 4, :], in0=t_bank(n), scalar=0.0,
                            in1=floor[:, g % 2, :], op0=ALU.min, op1=ALU.max).then_inc(shift_sem, 1)

                    def finish(q):
                        b, h0 = divmod(HG * q, HX)
                        turned = out_bank(q).rearrange("p (i h d) -> p i h d", i=TB, h=HG)
                        dve.wait_ge(raw_turned, q + 1)
                        inv = rsum[:, q % 2, :].rearrange("p (i h) -> p i h", i=TB)
                        nc.vector.reciprocal(inv, turned[:, :, :, DX]).then_inc(rsum_sem, 1)
                        dve.wait_ge(rsum_sem, q + 1)
                        nc.vector.tensor_tensor(
                            O[:, TB * b:TB * b + TB, h0 * DX:(h0 + HG) * DX].rearrange("p i (h d) -> p i h d", h=HG),
                            turned[:, :, :, 0:DX], inv.unsqueeze(3).to_broadcast([P, TB, HG, DX]),
                            ALU.mult).then_inc(out_sem, 1)

                    def reduce_and_divide(clips):
                        for j in range(STEPS):
                            k = j - 2 * LAG
                            if j < 2 * NH:
                                maximum(2 * j, clips)
                            if done_at(k) is not None:
                                finish(done_at(k))
                            if j < 2 * NH:
                                maximum(2 * j + 1, clips)
                            if turns_at(j + 3) is not None:
                                clip(turns_at(j + 3))
                            if clips and 0 <= k < 2 * NH:
                                shift(2 * k)
                                shift(2 * k + 1)

                    case_of = read_case(dve)
                    with dve.If(case_of == PLAIN):
                        reduce_and_divide(False)
                    with dve.If(case_of == CLIPPED):
                        reduce_and_divide(True)

                @block.gpsimd
                def _(pool):
                    nc.gpsimd.memset(neg_clamp[:, :], -CLAMP).then_inc(const_set, 1)
                    for s in range(1, STACKS):
                        pool.wait_ge(const_set, s)
                        nc.gpsimd.memset(kst[s][RM:P, :, :], 1.0).then_inc(const_set, 1)

                    case_of = read_case(pool)
                    with pool.If(case_of == UNIFORM):
                        pool.wait_ge(const_set, STACKS)
                        nc.gpsimd.memset(mean_w, 1.0 / T).then_inc(const_set, 1)
                    with pool.If(case_of < UNIFORM):
                        for m in range(NM):
                            pool.wait_ge(neg_sem, m + 1)
                            if m >= 2:
                                pool.wait_ge(neg_out, 16 * (m - 1))
                            nc.gpsimd.tensor_copy(nparts[:, m % 2, 0, :], neg[:, m % 2, :]).then_inc(nhigh, 1)
                            pool.wait_ge(nhigh, m + 1)
                            nc.gpsimd.tensor_tensor(neg[:, m % 2, :], neg[:, m % 2, :], nparts[:, m % 2, 0, :],
                                                    ALU.subtract).then_inc(nrest, 1)
                            pool.wait_ge(nrest, m + 1)
                            nc.gpsimd.tensor_copy(nparts[:, m % 2, 1, :], neg[:, m % 2, :]).then_inc(nmid, 1)
                            pool.wait_ge(nmid, m + 1)
                            nc.gpsimd.tensor_tensor(nparts[:, m % 2, 2, :], neg[:, m % 2, :],
                                                    nparts[:, m % 2, 1, :], ALU.subtract).then_inc(nlow, 1)

        with ExitStack() as ctx2:
            wo = c.sb(ctx2, "x_wo", [P, KD, D])
            weights = c.sem("x_wo_in")
            turned = c.sem("x_o_turned")
            stored = c.sem("x_o_stored")
            out_ps = c.sem("x_out_ps")
            off_sem = c.sem("x_offset")
            added = c.sem("x_added")
            with nc.Block() as block:
                @block.sync
                def _(sp):
                    sp.dma_start(wo[:, :, :], dram["x_wo"]).then_inc(weights, 16)

                @block.tensor
                def _(pe):
                    def turn(b):
                        for k in range(KD):
                            if b >= 2:
                                pe.wait_ge(stored, KD * (b - 2) + k + 1)
                            for i in range(TB):
                                tr = nc.tensor.transpose(c.bank[:, KD * (b % 2) + k, i * P:(i + 1) * P],
                                                         O[:, TB * b + i, k * P:(k + 1) * P], c.ident[:, :])
                            tr.then_inc(turned, 1)

                    turn(0)
                    pe.wait_ge(weights, 16)
                    for b in range(B):
                        if b + 1 < B:
                            turn(b + 1)
                        pe.wait_ge(stored, KD * (b + 1))
                        for t in range(TB * b, TB * b + TB):
                            if t >= 4:
                                pe.wait_ge(added, t - 3)
                            for k in range(KD):
                                mm = nc.tensor.matmul(c.bank[:, 4 + t % 4, 0:D], c.xn_f[:, k, t * P:(t + 1) * P],
                                                      wo[:, k, :], start=(k == 0), stop=(k == KD - 1))
                            mm.then_inc(out_ps, 1)

                @block.scalar
                def _(act):
                    for b in range(B):
                        for k in range(KD):
                            act.wait_ge(turned, KD * b + k + 1)
                            nc.scalar.activation(c.xn_f[:, k, b * T:(b + 1) * T], c.bank[:, KD * (b % 2) + k, :],
                                                 ACT.Identity, bias=c.col("bv", k)).then_inc(stored, 1)

                @block.gpsimd
                def _(pool):
                    for t in range(NT):
                        nc.gpsimd.tensor_tensor(c.X[:, t, :], c.X[:, t, :], c.row("bo"),
                                                ALU.add).then_inc(off_sem, 1)

                @block.vector
                def _(dve):
                    for t in range(NT):
                        dve.wait_ge(out_ps, t + 1)
                        dve.wait_ge(off_sem, t + 1)
                        nc.vector.tensor_tensor(c.X[:, t, :], c.X[:, t, :], c.bank[:, 4 + t % 4, 0:D],
                                                ALU.add).then_inc(added, 1)


def route_block(c, tag, n_all, wg, wg_in, bias, gates, xs, split_weights, round_weights=None):
    nc = c.nc
    with ExitStack() as ctx2:
        lg = c.sb(ctx2, tag + "_lg", [P, NT, n_all])
        rest = c.sb(ctx2, tag + "_rest", [P, NT, n_all])
        cand = c.sb(ctx2, tag + "_cand", [P, NT, n_all])
        pick = c.sb(ctx2, tag + "_pick", [P, 2, NT, n_all])
        top = c.sb(ctx2, tag + "_top", [P, 2, NT])
        at = c.sb(ctx2, tag + "_at", [P, 2, NT])
        ex = c.sb(ctx2, tag + "_ex", [P, NT])
        den = c.sb(ctx2, tag + "_den", [P, NT])
        share = c.sb(ctx2, tag + "_share", [P, 2, NT])
        high, _high = c.tally("split_high", KD)
        low, _low = c.tally("split_low", KD)
        logits, logits0 = c.tally("route_logits", 1)
        step, step0 = c.tally("route_step", 18)
        gap, gap0 = c.tally("route_gap", 1)
        exp_sem, exp_sem0 = c.tally("route_exp", 1)

        def wide(ap):
            return ap.unsqueeze(2).to_broadcast([P, NT, n_all])

        index = c.row("expert_index")[:, 0:n_all].unsqueeze(1).to_broadcast([P, NT, n_all])
        with nc.Block() as block:
            @block.gpsimd
            def _(pool):
                split_weights(pool)

            @block.tensor
            def _(pe):
                pe.wait_ge(wg_in, 16)
                for t in range(NT):
                    for k in range(KD):
                        mm = nc.tensor.matmul(c.bank[:, 0, t * n_all:(t + 1) * n_all],
                                              c.xn_f[:, k, t * P:(t + 1) * P], wg[:, k, :],
                                              start=(k == 0), stop=(k == KD - 1))
                mm.then_inc(logits, 1)

            @block.vector
            def _(dve):
                done = [0]

                def then(ins):
                    done[0] += 1
                    ins.then_inc(step, 1)
                    dve.wait_ge(step, step0 + done[0])

                for k in range(KD):
                    dve.wait_ge(high, _high + k + 1)
                    nc.vector.tensor_tensor(xs[1][:, k, :], c.xn_f[:, k, :], xs[0][:, k, :].bitcast(F32),
                                            ALU.subtract).then_inc(low, 1)
                dve.wait_ge(logits, logits0 + 1)
                ps = c.bank[:, 0, 0:NT * n_all].rearrange("p (t e) -> p t e", t=NT)
                if bias:
                    then(nc.vector.tensor_tensor(lg[:, :, :], ps,
                                                 c.row("expert_bias").unsqueeze(1).to_broadcast([P, NT, n_all]),
                                                 ALU.add))
                else:
                    then(nc.vector.tensor_copy(lg[:, :, :], ps))
                left = lg
                for r in range(2):
                    then(nc.vector.tensor_reduce(top[:, r, :], left[:, :, :], AX.X, ALU.max))
                    then(nc.vector.tensor_tensor(cand[:, :, :], left[:, :, :], wide(top[:, r, :]), ALU.is_lt))
                    then(nc.vector.scalar_tensor_tensor(out=cand[:, :, :], in0=cand[:, :, :], scalar=float(n_all),
                                                        in1=index, op0=ALU.mult, op1=ALU.add))
                    then(nc.vector.tensor_reduce(at[:, r, :], cand[:, :, :], AX.X, ALU.min))
                    then(nc.vector.tensor_tensor(pick[:, r], cand[:, :, :], wide(at[:, r, :]), ALU.is_equal))
                    if r == 0:
                        then(nc.vector.scalar_tensor_tensor(out=rest[:, :, :], in0=pick[:, 0], scalar=-3.0e38,
                                                            in1=lg[:, :, :], op0=ALU.mult, op1=ALU.add))
                        left = rest
                nc.vector.tensor_tensor(ex[:, :], top[:, 1, :], top[:, 0, :], ALU.subtract).then_inc(gap, 1)
                dve.wait_ge(exp_sem, exp_sem0 + 1)
                then(nc.vector.tensor_scalar(den[:, :], ex[:, :], 1.0, None, ALU.add))
                then(nc.vector.reciprocal(share[:, 0, :], den[:, :]))
                then(nc.vector.tensor_tensor(share[:, 1, :], share[:, 0, :], ex[:, :], ALU.mult))
                then(nc.vector.tensor_tensor(pick[:, 0], pick[:, 0], wide(share[:, 0, :]), ALU.mult))
                then(nc.vector.tensor_tensor(pick[:, 1], pick[:, 1], wide(share[:, 1, :]), ALU.mult))
                then(nc.vector.tensor_tensor(gates[:, :, :], pick[:, 0], pick[:, 1], ALU.add))
                assert done[0] == 18

            @block.scalar
            def _(act):
                for k in range(KD):
                    nc.scalar.activation(xs[0][:, k, :], c.xn_f[:, k, :], ACT.Copy).then_inc(high, 1)
                if round_weights is not None:
                    round_weights(act)
                act.wait_ge(gap, gap0 + 1)
                nc.scalar.activation(ex[:, :], ex[:, :], ACT.Exp).then_inc(exp_sem, 1)


TERMS = ((0, 0), (0, 1), (1, 0))


def experts_blocks(c):
    nc, dram = c.nc, c.dram
    FT = FF0 // P
    with ExitStack() as ctx:
        wg = c.sb(ctx, "r0_wg", [P, KD, NE_ALL])
        gates = c.sb(ctx, "r0_gates", [P, NT, NE_ALL])
        xs = [c.sb(ctx, f"e0_x{i}", [P, KD, N], F32R) for i in range(2)]
        w_full = [c.sb(ctx, "e0_w1", [P, 2, KD, FF0]), c.sb(ctx, "e0_w2", [P, 2, FT, D])]
        w1 = [c.sb(ctx, f"e0_w1_{i}", [P, 2, KD, FF0], F32R) for i in range(2)]
        w2 = [c.sb(ctx, f"e0_w2_{i}", [P, 2, FT, D], F32R) for i in range(2)]
        full = c.sb(ctx, "e0_hid", [P, 4, T])
        hid = [c.sb(ctx, f"e0_hid{i}", [P, 2, FT, T], F32R) for i in range(2)]
        zero_w = c.sb(ctx, "e0_zero_w", [P, NT])
        wg_in = c.sem("e0_wg_in")
        w1_in = [c.sem(f"e0_w1_in{i}") for i in range(2)]
        w2_in = [c.sem(f"e0_w2_in{i}") for i in range(2)]
        w_high = c.sem("e0_w_high")
        w_low = c.sem("e0_w_low")
        hid_ps = c.sem("e0_hid_ps")
        hid_full = c.sem("e0_hid_full")
        hid_high = c.sem("e0_hid_high")
        hid_low = c.sem("e0_hid_low")
        out_ps = c.sem("e0_out_ps")
        added = c.sem("e0_added")
        zero_sem = c.sem("e0_zero")
        U = NE * B

        def load_expert(sp, e):
            if e >= 2:
                sp.wait_ge(w_low, 2 * (e - 1))
            sp.dma_start(w_full[0][:, e % 2], dram["e0_w1"][e]).then_inc(w1_in[e % 2], 16)
            sp.dma_start(w_full[1][:, e % 2], dram["e0_w2"][e]).then_inc(w2_in[e % 2], 16)

        def split_expert(pool, e):
            for i, (w, w_in) in enumerate(((w1, w1_in), (w2, w2_in))):
                pool.wait_ge(w_in[e % 2], 16 * (e // 2 + 1))
                if e >= 2:
                    pool.wait_ge(out_ps, NT * (e - 1))
                nc.gpsimd.tensor_copy(w[0][:, e % 2], w_full[i][:, e % 2]).then_inc(w_high, 1)
                pool.wait_ge(w_high, 2 * e + i + 1)
                nc.gpsimd.tensor_tensor(w[1][:, e % 2], w_full[i][:, e % 2], w[0][:, e % 2].bitcast(F32),
                                        ALU.subtract).then_inc(w_low, 1)
                pool.wait_ge(w_low, 2 * e + i + 1)

        def load_ahead(sp):
            sp.dma_start(wg[:, :, :], dram["e0_gate"]).then_inc(wg_in, 16)
            load_expert(sp, 0)
            load_expert(sp, 1)

        norm_block(c, "n2", load_ahead=load_ahead)
        route_block(c, "r0", NE_ALL, wg, wg_in, True, gates, xs, lambda pool: split_expert(pool, 0))
        with nc.Block() as block:
            @block.sync
            def _(sp):
                for e in range(2, NE):
                    load_expert(sp, e)

            @block.gpsimd
            def _(pool):
                for e in range(1, NE):
                    split_expert(pool, e)

            @block.tensor
            def _(pe):
                def hidden(u):
                    e, b = divmod(u, B)
                    if b == 0:
                        pe.wait_ge(w_low, 2 * e + 1)
                    for f in range(FT):
                        n = FT * u + f
                        if n >= 4:
                            pe.wait_ge(hid_high, n - 3)
                        for k in range(KD):
                            for i, (wi, xi) in enumerate(TERMS):
                                mm = nc.tensor.matmul(c.bank[:, n % 4, :], w1[wi][:, e % 2, k, f * P:(f + 1) * P],
                                                      xs[xi][:, k, b * T:(b + 1) * T], start=(k == 0 and i == 0),
                                                      stop=(k == KD - 1 and i == 2))
                        mm.then_inc(hid_ps, 1)

                def output(u):
                    e, b = divmod(u, B)
                    if b == 0:
                        pe.wait_ge(w_low, 2 * e + 2)
                    pe.wait_ge(hid_low, FT * (u + 1))
                    for i in range(TB):
                        n = TB * u + i
                        if n >= 4:
                            pe.wait_ge(added, n - 3)
                        for f in range(FT):
                            for j, (hi, wi) in enumerate(TERMS):
                                mm = nc.tensor.matmul(c.bank[:, 4 + n % 4, 0:D],
                                                      hid[hi][:, u % 2, f, i * P:(i + 1) * P],
                                                      w2[wi][:, e % 2, f, :], start=(f == 0 and j == 0),
                                                      stop=(f == FT - 1 and j == 2))
                        mm.then_inc(out_ps, 1)

                hidden(0)
                for u in range(U):
                    if u + 1 < U:
                        hidden(u + 1)
                    output(u)

            @block.scalar
            def _(act):
                for n in range(FT * U):
                    u, f = divmod(n, FT)
                    act.wait_ge(hid_ps, n + 1)
                    if n >= 4:
                        act.wait_ge(hid_low, n - 3)
                    nc.scalar.activation(full[:, n % 4, :], c.bank[:, n % 4, :], ACT.Silu).then_inc(hid_full, 1)
                    if u >= 2:
                        act.wait_ge(out_ps, TB * (u - 1))
                    nc.scalar.activation(hid[0][:, u % 2, f, :], c.bank[:, n % 4, :],
                                         ACT.Silu).then_inc(hid_high, 1)

            @block.vector
            def _(dve):
                def add_inputs():
                    nc.vector.tensor_reduce(zero_w[:, :], gates[:, :, NE:NE_ALL], AX.X,
                                            ALU.add).then_inc(zero_sem, 1)
                    dve.wait_ge(zero_sem, 1)
                    for t in range(NT):
                        nc.vector.scalar_tensor_tensor(out=c.X[:, t, :], in0=c.xn[:, t, :],
                                                       scalar=zero_w[:, t:t + 1], in1=c.X[:, t, :], op0=ALU.mult,
                                                       op1=ALU.add).then_inc(zero_sem, 1)

                def lows(u):
                    for n in range(FT * u, FT * u + FT):
                        dve.wait_ge(hid_full, n + 1)
                        dve.wait_ge(hid_high, n + 1)
                        if u >= 2:
                            dve.wait_ge(out_ps, TB * (u - 1))
                        nc.vector.tensor_tensor(hid[1][:, u % 2, n % FT, :], full[:, n % 4, :],
                                                hid[0][:, u % 2, n % FT, :].bitcast(F32),
                                                ALU.subtract).then_inc(hid_low, 1)

                def adds(u):
                    e, b = divmod(u, B)
                    for i in range(TB):
                        n, t = TB * u + i, TB * b + i
                        dve.wait_ge(out_ps, n + 1)
                        if e == 0:
                            dve.wait_ge(zero_sem, t + 2)
                        else:
                            dve.wait_ge(added, NT * (e - 1) + t + 1)
                        nc.vector.scalar_tensor_tensor(out=c.X[:, t, :], in0=c.bank[:, 4 + n % 4, 0:D],
                                                       scalar=gates[:, t, e:e + 1], in1=c.X[:, t, :],
                                                       op0=ALU.mult, op1=ALU.add).then_inc(added, 1)

                lows(0)
                add_inputs()
                for u in range(U):
                    if u + 1 < U:
                        lows(u + 1)
                    adds(u)


def gru_blocks(c):
    nc, dram = c.nc, c.dram
    with ExitStack() as ctx:
        wf = c.sb(ctx, "g_wf", [P, KD, 2 * EG])
        wd = c.sb(ctx, "g_wd", [P, GT, D])
        wfs = [c.sb(ctx, f"g_wf{i}", [P, KD, 2 * EG], F32R) for i in range(2)]
        wds = [c.sb(ctx, f"g_wd{i}", [P, GT, D], F32R) for i in range(2)]
        xs = [c.sb(ctx, f"g_x{i}", [P, KD, N], F32R) for i in range(2)]
        state = c.sb(ctx, "g_state", [P, GT, B, T])
        states = [c.sb(ctx, f"g_state{i}", [P, 2, GT, T], F32R) for i in range(2)]
        z = c.sb(ctx, "g_z", [P, 2, T])
        keep = c.sb(ctx, "g_keep", [P, 4, T])
        soft = c.sb(ctx, "g_soft", [P, 2, T])
        lin = c.sb(ctx, "g_lin", [P, 2, T])
        cand = c.sb(ctx, "g_cand", [P, 2, T])
        val = c.sb(ctx, "g_val", [P, 2, T])
        neg_b = c.sb(ctx, "g_neg_b", [P, GT])
        weights = c.sem("g_weights")
        w_high = c.sem("g_w_high")
        w_low = c.sem("g_w_low")
        x_high = c.sem("g_x_high")
        x_low = c.sem("g_x_low")
        state_high = c.sem("g_state_high")
        state_low = c.sem("g_state_low")
        neg_sem = c.sem("g_neg_b_ready")
        kz_ps = c.sem("g_kz_ps")
        hx_ps = c.sem("g_hx_ps")
        z_sem = c.sem("g_z_ready")
        keep_sem = c.sem("g_keep_ready")
        soft_sem = c.sem("g_soft_ready")
        lin_sem = c.sem("g_lin_ready")
        cand_sem = c.sem("g_cand_ready")
        val_sem = c.sem("g_val_ready")
        scanned = c.sem("g_scanned")
        out_ps = c.sem("g_out_ps")
        added = c.sem("g_added")
        U = B * GT

        def load_ahead(sp):
            sp.dma_start(wf[:, :, :], dram["g_wf"]).then_inc(weights, 16)
            sp.dma_start(wd[:, :, :], dram["g_wd"]).then_inc(weights, 16)

        def split_weights(pool, i):
            full, halves = ((wf, wfs), (wd, wds))[i]
            pool.wait_ge(weights, 32)
            nc.gpsimd.tensor_copy(halves[0][:, :, :], full[:, :, :]).then_inc(w_high, 1)
            pool.wait_ge(w_high, i + 1)
            nc.gpsimd.tensor_tensor(halves[1][:, :, :], full[:, :, :], halves[0][:, :, :].bitcast(F32),
                                    ALU.subtract).then_inc(w_low, 1)
            pool.wait_ge(w_low, i + 1)

        norm_block(c, "n3", load_ahead=load_ahead, split_weights=lambda pool: split_weights(pool, 0))
        with nc.Block() as block:
            @block.tensor
            def _(pe):
                def hidden(u):
                    b, m = divmod(u, GT)
                    pe.wait_ge(x_low, KD * (b + 1))
                    for bank, off, sem, used in ((0, 0, kz_ps, keep_sem), (2, EG, hx_ps, lin_sem)):
                        if u >= 2:
                            pe.wait_ge(used, u - 1)
                            if off:
                                pe.wait_ge(soft_sem, u - 1)
                        for k in range(KD):
                            for i, (wi, xi) in enumerate(TERMS):
                                mm = nc.tensor.matmul(c.bank[:, bank + u % 2, :],
                                                      wfs[wi][:, k, off + m * P:off + (m + 1) * P],
                                                      xs[xi][:, k, b * T:(b + 1) * T], start=(k == 0 and i == 0),
                                                      stop=(k == KD - 1 and i == 2))
                        mm.then_inc(sem, 1)

                def outputs(b):
                    pe.wait_ge(w_low, 2)
                    pe.wait_ge(state_low, GT * (b + 1))
                    for i in range(TB):
                        t = TB * b + i
                        if t >= 4:
                            pe.wait_ge(added, t - 3)
                        for m in range(GT):
                            for j, (si, wi) in enumerate(TERMS):
                                mm = nc.tensor.matmul(c.bank[:, 4 + t % 4, 0:D],
                                                      states[si][:, b % 2, m, i * P:(i + 1) * P], wds[wi][:, m, :],
                                                      start=(m == 0 and j == 0), stop=(m == GT - 1 and j == 2))
                        mm.then_inc(out_ps, 1)

                for u in range(U):
                    hidden(u)
                    if u % GT == 0 and u >= 2 * GT:
                        outputs(u // GT - 2)
                outputs(B - 2)
                outputs(B - 1)

            @block.scalar
            def _(act):
                def input_high(b):
                    for k in range(KD):
                        nc.scalar.activation(xs[0][:, k, b * T:(b + 1) * T], c.xn_f[:, k, b * T:(b + 1) * T],
                                             ACT.Copy).then_inc(x_high, 1)

                def high_of(u):
                    b, m = divmod(u, GT)
                    act.wait_ge(scanned, u + 1)
                    if b >= 2:
                        act.wait_ge(out_ps, TB * (b - 1))
                    nc.scalar.activation(states[0][:, b % 2, m, :], state[:, m, b, :],
                                         ACT.Copy).then_inc(state_high, 1)

                input_high(0)
                act.wait_ge(neg_sem, 1)
                for u in range(U):
                    b, m = divmod(u, GT)
                    if m == 0 and b + 1 < B:
                        input_high(b + 1)
                    act.wait_ge(kz_ps, u + 1)
                    if u >= 2:
                        act.wait_ge(val_sem, u - 1)
                    nc.scalar.activation(z[:, u % 2, :], c.bank[:, u % 2, :], ACT.Sigmoid,
                                         bias=c.col("b_f", m)).then_inc(z_sem, 1)
                    if u >= 4:
                        act.wait_ge(scanned, u - 3)
                    nc.scalar.activation(keep[:, u % 4, :], c.bank[:, u % 2, :], ACT.Sigmoid,
                                         bias=neg_b[:, m:m + 1], scale=-1.0).then_inc(keep_sem, 1)
                    act.wait_ge(lin_sem, u + 1)
                    if u >= 2:
                        act.wait_ge(cand_sem, u - 1)
                    nc.scalar.activation(soft[:, u % 2, :], c.bank[:, 2 + u % 2, :], ACT.Sigmoid,
                                         bias=c.col("b_f", GT + m)).then_inc(soft_sem, 1)
                    if u >= 2:
                        high_of(u - 2)
                high_of(U - 2)
                high_of(U - 1)

            @block.vector
            def _(dve):
                nc.vector.tensor_scalar(neg_b[:, :], c.col("b_f", 0, GT), -1.0, None,
                                        ALU.mult).then_inc(neg_sem, 1)

                def candidate(u):
                    b, m = divmod(u, GT)
                    dve.wait_ge(hx_ps, u + 1)
                    if u >= 2:
                        dve.wait_ge(cand_sem, u - 1)
                    nc.vector.tensor_scalar(lin[:, u % 2, :], c.bank[:, 2 + u % 2, :], c.col("b_f", GT + m), 0.0,
                                            ALU.add, ALU.max).then_inc(lin_sem, 1)
                    dve.wait_ge(lin_sem, u + 1)
                    dve.wait_ge(soft_sem, u + 1)
                    if u >= 2:
                        dve.wait_ge(val_sem, u - 1)
                    nc.vector.scalar_tensor_tensor(out=cand[:, u % 2, :], in0=soft[:, u % 2, :], scalar=0.5,
                                                   in1=lin[:, u % 2, :], op0=ALU.min,
                                                   op1=ALU.add).then_inc(cand_sem, 1)

                def scan(u):
                    b, m = divmod(u, GT)
                    dve.wait_ge(val_sem, u + 1)
                    dve.wait_ge(keep_sem, u + 1)
                    nc.vector.tensor_tensor_scan(state[:, m, b, :], keep[:, u % 4, :], val[:, u % 2, :], 0.5,
                                                 ALU.mult, ALU.add).then_inc(scanned, 1)

                def input_low(b):
                    cols = slice(b * T, (b + 1) * T)
                    for k in range(KD):
                        dve.wait_ge(x_high, KD * b + k + 1)
                        nc.vector.tensor_tensor(xs[1][:, k, cols], c.xn_f[:, k, cols],
                                                xs[0][:, k, cols].bitcast(F32), ALU.subtract).then_inc(x_low, 1)

                def low_of(u):
                    b, m = divmod(u, GT)
                    dve.wait_ge(state_high, u + 1)
                    if b >= 2:
                        dve.wait_ge(out_ps, TB * (b - 1))
                    nc.vector.tensor_tensor(states[1][:, b % 2, m, :], state[:, m, b, :],
                                            states[0][:, b % 2, m, :].bitcast(F32),
                                            ALU.subtract).then_inc(state_low, 1)

                def add(b):
                    for t in range(TB * b, TB * b + TB):
                        dve.wait_ge(out_ps, t + 1)
                        nc.vector.tensor_tensor(c.X[:, t, :], c.X[:, t, :], c.bank[:, 4 + t % 4, 0:D],
                                                ALU.add).then_inc(added, 1)

                input_low(0)
                for u in range(U + 2):
                    if u % GT == 0 and u // GT + 1 < B:
                        input_low(u // GT + 1)
                    if u < U:
                        candidate(u)
                    if 1 <= u <= U:
                        scan(u - 1)
                    if u >= 2:
                        low_of(u - 2)
                    if u % GT == 1 and u >= 2 * GT:
                        add(u // GT - 2)
                add(B - 1)

            @block.gpsimd
            def _(pool):
                split_weights(pool, 1)
                for u in range(U):
                    pool.wait_ge(cand_sem, u + 1)
                    pool.wait_ge(z_sem, u + 1)
                    if u >= 2:
                        pool.wait_ge(scanned, u - 1)
                    nc.gpsimd.tensor_tensor(val[:, u % 2, :], cand[:, u % 2, :], z[:, u % 2, :],
                                            ALU.mult).then_inc(val_sem, 1)


TERNARY = (("t_d2v", CK, 2, D), ("t_img", P, KD, D), ("t_txt", P, KD, D), ("t_att0", P, KD, P),
           ("t_att1", P, KD, P), ("t_f1", P, 2 * KD, FX), ("t_f2", P, FX // P, D))
W_D2V, W_IMG, W_TXT, W_ATT0, W_ATT1, W_F1, W_F2 = range(len(TERNARY))


class CombineExperts:

    HT = FF1 // P

    def __init__(self, c, ctx):
        self.c = c
        self.w_in = c.sb(ctx, "e1_w_in", [P, 2, self.HT, D])
        self.w_out = c.sb(ctx, "e1_w_out", [P, 2, self.HT, D])
        self.in_in = [c.sem(f"e1_in_in{i}") for i in range(2)]
        self.out_in = [c.sem(f"e1_out_in{i}") for i in range(2)]
        self.product_ps = c.sem("e1_comb_ps")
        self.stored = c.sem("e1_comb_stored")

    def load(self, sp, experts):
        for e in experts:
            if e >= NE:
                continue
            if e >= 2:
                sp.wait_ge(self.product_ps, KD * (e - 1))
            sp.dma_start(self.w_in[:, e % 2], self.c.dram["e1_w_in"][e]).then_inc(self.in_in[e % 2], 16)
            sp.dma_start(self.w_out[:, e % 2], self.c.dram["e1_w_out"][e]).then_inc(self.out_in[e % 2], 16)

    def products(self, pe, experts):
        nc, c = self.c.nc, self.c
        for e in experts:
            pe.wait_ge(self.in_in[e % 2], 16 * (e // 2 + 1))
            pe.wait_ge(self.out_in[e % 2], 16 * (e // 2 + 1))
            for k in range(KD):
                u = KD * e + k
                if u >= 4:
                    pe.wait_ge(self.stored, u - 3)
                for h in range(self.HT):
                    mm = nc.tensor.matmul(c.bank[:, u % 4, 0:D], self.w_in[:, e % 2, h, k * P:(k + 1) * P],
                                          self.w_out[:, e % 2, h, :], start=(h == 0), stop=(h == self.HT - 1))
                mm.then_inc(self.product_ps, 1)

    def store(self, act, experts):
        nc, c = self.c.nc, self.c
        for e in experts:
            for k in range(KD):
                u = KD * e + k
                act.wait_ge(self.product_ps, u + 1)
                nc.scalar.activation(c.comb[:, k, e, :], c.bank[:, u % 4, 0:D], ACT.Copy).then_inc(self.stored, 1)


def ternary_weights_block(c, tern, full, loaded, scale, magic, ctx_in, combine, experts):
    nc = c.nc
    n = len(TERNARY)
    with ExitStack() as ctx2:
        below = [c.sb(ctx2, name + "_b", [p, k, w], BF16) for name, p, k, w in TERNARY]
        sums = c.sb(ctx2, "t_sums", [P, n])
        total = c.sb(ctx2, "t_total", [P, n])
        half = c.sb(ctx2, "t_half", [P, 2, n])
        zero_sem = c.sem("t_zero")
        sum_sem = c.sem("t_sum")
        total_sem = c.sem("t_total_ready")
        scale_sem = c.sem("t_scale_ready")
        half_sem = c.sem("t_half_ready")
        below_sem = c.sem("t_below")
        tern_sem = c.sem("t_tern")
        with nc.Block() as block:
            @block.sync
            def _(sp):
                combine.load(sp, [e + 2 for e in experts])
                sp.wait_ge(ctx_in, 16)

            @block.tensor
            def _(pe):
                combine.products(pe, experts)

            @block.scalar
            def _(act):
                act.wait_ge(zero_sem, 2)
                for i in (W_F1, W_F2):
                    _name, p, _k, _w = TERNARY[i]
                    act.wait_ge(loaded[i], 16)
                    nc.scalar.activation(below[i][:, :, :], full[i][:, :, :], ACT.Abs,
                                         accum_out=sums[0:p, i:i + 1]).then_inc(sum_sem, 1)
                combine.store(act, experts)

            @block.gpsimd
            def _(pool):
                pool.wait_ge(sum_sem, n)
                nc.gpsimd.partition_all_reduce(total[:, :], sums[:, :], P, RED.add).then_inc(total_sem, 1)

            @block.vector
            def _(dve):
                nc.vector.memset(magic[:, :], MAGIC).then_inc(zero_sem, 1)
                nc.vector.memset(sums[:, :], 0.0).then_inc(zero_sem, 1)
                dve.wait_ge(zero_sem, 2)
                for i, (name, p, k, w) in enumerate(TERNARY):
                    if i in (W_F1, W_F2):
                        continue
                    dve.wait_ge(loaded[i], 16)
                    nc.vector.tensor_reduce(sums[0:p, i:i + 1], full[i][:, :, :], AX.XY, ALU.add,
                                            apply_absolute_value=True).then_inc(sum_sem, 1)
                dve.wait_ge(total_sem, 1)
                for i, (name, p, k, w) in enumerate(TERNARY):
                    nc.vector.tensor_scalar(scale[:, i:i + 1], total[:, i:i + 1], 1.0 / (p * k * w), 1e-5,
                                            ALU.mult, ALU.max).then_inc(scale_sem, 1)
                dve.wait_ge(scale_sem, n)
                nc.vector.tensor_scalar(half[:, 0, :], scale[:, :], 0.5, None, ALU.mult).then_inc(half_sem, 1)
                nc.vector.tensor_scalar(half[:, 1, :], scale[:, :], -0.5, None, ALU.mult).then_inc(half_sem, 1)
                dve.wait_ge(half_sem, 2)
                for i, (name, p, k, w) in enumerate(TERNARY):
                    nc.vector.tensor_scalar(below[i][:, :, :], full[i][:, :, :], half[0:p, 1, i:i + 1], None,
                                            ALU.is_lt).then_inc(below_sem, 1)
                for i, (name, p, k, w) in enumerate(TERNARY):
                    dve.wait_ge(below_sem, i + 1)
                    nc.vector.scalar_tensor_tensor(
                        out=tern[i][:, :, :].rearrange("p k w -> p (k w)"),
                        in0=full[i][:, :, :].rearrange("p k w -> p (k w)"), scalar=half[0:p, 0, i:i + 1],
                        in1=below[i][:, :, :].rearrange("p k w -> p (k w)"), op0=ALU.is_gt,
                        op1=ALU.subtract).then_inc(tern_sem, 1)


def quantise_block(c, tag, sources, scale, i_w, scratch, combine=None, experts=(),
                   peaks=0):
    nc = c.nc
    peak, top, step, inv, out_scale, magic = scratch
    n = len(sources)
    peak_zero, peak_zero0 = c.tally("quant_peak_zero", 0 if peaks else 1)
    peak_sem, peak_sem0 = c.tally("quant_peak", 0 if peaks else n)
    peak1_sem, peak1_sem0 = c.tally("quant_peak1", 1)
    top_sem, top_sem0 = c.tally("quant_top", 1)
    step_sem, step_sem0 = c.tally("quant_step", 1)
    inv_sem, inv_sem0 = c.tally("quant_inv", 1)
    scale_sem, scale_sem0 = c.tally("quant_scale", 1)
    up_sem, up_sem0 = c.tally("quant_up", n)
    clip_sem, clip_sem0 = c.tally("quant_clip", n)
    down_sem, down_sem0 = c.tally("quant_down", n)
    with nc.Block() as block:
        @block.vector
        def _(dve):
            if peaks == 0:
                nc.vector.memset(peak[:, :], 0.0).then_inc(peak_zero, 1)
                dve.wait_ge(peak_zero, peak_zero0 + 1)
                for i, (src, dst) in enumerate(sources):
                    nc.vector.tensor_reduce(peak[0:src.shape[0], i:i + 1], src, AX.X, ALU.max,
                                            apply_absolute_value=True).then_inc(peak_sem, 1)
                dve.wait_ge(peak_sem, peak_sem0 + n)
            nc.vector.tensor_reduce(top[:, 0:1], peak[:, 0:peaks or n], AX.X, ALU.max).then_inc(peak1_sem, 1)
            dve.wait_ge(top_sem, top_sem0 + 1)
            nc.vector.tensor_scalar(step[:, 0:1], top[:, 1:2], 1e-8, 1.0 / 127.0, ALU.max,
                                    ALU.mult).then_inc(step_sem, 1)
            dve.wait_ge(step_sem, step_sem0 + 1)
            nc.vector.reciprocal(inv[:, 0:1], step[:, 0:1]).then_inc(inv_sem, 1)
            nc.vector.tensor_tensor(out_scale[:, 0:1], step[:, 0:1], scale[:, i_w:i_w + 1],
                                    ALU.mult).then_inc(scale_sem, 1)
            for i, (src, dst) in enumerate(sources):
                dve.wait_ge(up_sem, up_sem0 + i + 1)
                nc.vector.tensor_scalar(src, src, MAGIC - 128.0, MAGIC + 127.0, ALU.max,
                                        ALU.min).then_inc(clip_sem, 1)

        @block.gpsimd
        def _(pool):
            pool.wait_ge(peak1_sem, peak1_sem0 + 1)
            nc.gpsimd.partition_all_reduce(top[:, 1:2], top[:, 0:1], P, RED.max).then_inc(top_sem, 1)
            for i, (src, dst) in enumerate(sources):
                pool.wait_ge(clip_sem, clip_sem0 + i + 1)
                nc.gpsimd.tensor_scalar(dst, src, 1.0, -MAGIC, ALU.mult, ALU.add).then_inc(down_sem, 1)

        @block.sync
        def _(sp):
            if combine is not None:
                combine.load(sp, [e + 2 for e in experts])

        @block.tensor
        def _(pe):
            if combine is not None:
                combine.products(pe, experts)

        @block.scalar
        def _(act):
            act.wait_ge(inv_sem, inv_sem0 + 1)
            for i, (src, dst) in enumerate(sources):
                p = src.shape[0]
                nc.scalar.activation(src, src, ACT.Identity, bias=magic[0:p, 0:1],
                                     scale=inv[0:p, 0:1]).then_inc(up_sem, 1)
            if combine is not None:
                combine.store(act, experts)


def product_block(c, tag, units, out_scale, func=ACT.Identity, peak=None, peak_of=None, sums=None):
    nc = c.nc
    ps, ps0 = c.tally("product_ps", len(units))
    done, done0 = c.tally("product_done", len(units))
    peaked, _peaked = c.tally("product_peak", len(peak_of or units) if peak is not None else 0)
    with nc.Block() as block:
        @block.tensor
        def _(pe):
            for u, (pairs, out, bias) in enumerate(units):
                if u >= 8:
                    pe.wait_ge(done, done0 + u - 7)
                for k, (lhs, rhs) in enumerate(pairs):
                    mm = nc.tensor.matmul(c.bank[:, u % 8, :], lhs, rhs, start=(k == 0),
                                          stop=(k == len(pairs) - 1))
                mm.then_inc(ps, 1)

        @block.scalar
        def _(act):
            for u, (pairs, out, bias) in enumerate(units):
                act.wait_ge(ps, ps0 + u + 1)
                nc.scalar.activation(out, c.bank[:, u % 8, :], func, bias=bias, scale=out_scale[:, 0:1],
                                     accum_out=sums[u] if sums else None).then_inc(done, 1)

        if peak is not None:
            @block.vector
            def _(dve):
                for i, src in enumerate(peak_of or [out for _pairs, out, _bias in units]):
                    if not peak_of:
                        dve.wait_ge(done, done0 + i + 1)
                    nc.vector.tensor_reduce(peak[:, i:i + 1], src, AX.X, ALU.max,
                                            apply_absolute_value=True).then_inc(peaked, 1)


def ternary_cross_blocks(c):
    nc, dram = c.nc, c.dram
    with ExitStack() as ctx:
        n = len(TERNARY)
        tern = [c.sb(ctx, name + "_q", [p, k, w], BF16) for name, p, k, w in TERNARY]
        scale = c.sb(ctx, "t_scale", [P, n])
        loaded = [c.sem(f"t_loaded{i}") for i in range(n)]
        peak = c.sb(ctx, "t_peak", [P, 32])
        top = c.sb(ctx, "t_top", [P, 2])
        step = c.sb(ctx, "t_step", [P, 1])
        inv = c.sb(ctx, "t_inv", [P, 1])
        magic = c.sb(ctx, "t_magic", [P, 1])
        out_scale = c.sb(ctx, "t_out_scale", [P, 1])
        scratch = (peak, top, step, inv, out_scale, magic)
        fused = c.sb(ctx, "t_fused", [P, KD, N])
        mean_img = c.sb(ctx, "t_mean_img", [P, KD, B])
        ctx_in = c.sem("t_ctx_in")
        combine_ctx = ctx.enter_context(ExitStack())
        combine = CombineExperts(c, combine_ctx)
        with ExitStack() as ctx2:
            full = [c.sb(ctx2, name, [p, k, w]) for name, p, k, w in TERNARY]

            def load_ahead(sp):
                for i, (name, p, k, w) in enumerate(TERNARY):
                    sp.dma_start(full[i][:, :, :], dram[name]).then_inc(loaded[i], 16)
                sp.dma_start(fused[0:CK, :, :], dram["ctx_f"]).then_inc(ctx_in, 16)
                combine.load(sp, (0, 1))

            norm_block(c, "n4", load_ahead=load_ahead)
            ternary_weights_block(c, tern, full, loaded, scale, magic, ctx_in, combine, (0,))
        keys_ctx = ExitStack()
        keys_f = c.sb(keys_ctx, "t_keys_f", [P, 2, N])
        keys_t = c.sb(keys_ctx, "t_keys_t", [P, 2, NT, P])

        def cut(ap, b):
            return ap[:, b * T:(b + 1) * T]

        with ExitStack() as ctx2:
            qb = c.sb(ctx2, "t_q", [P, KD, N], BF16)
            img = c.sb(ctx2, "t_img_f", [P, KD, N])
            mean_sem = c.sem("t_mean")
            turned = c.sem("t_keys_turned")
            turned_out = c.sem("t_keys_stored")
            def project(tag, src, rows, i_w, i_b, dst, experts, peaks, **after):
                quantise_block(c, tag + "q", [(cut(src[:, k, :], b), cut(qb[0:rows, k, :], b))
                                              for k in range(2) for b in range(B)], scale, i_w, scratch,
                               combine, experts, peaks)
                product_block(c, tag, [([(tern[i_w][:, k, m * P:(m + 1) * P], cut(qb[0:rows, k, :], b))
                                         for k in range(2)], cut(dst[:, m, :], b), c.col(i_b, m))
                                       for b in range(B) for m in range(KD)], out_scale,
                              **after)

            project("td", fused[0:CK], CK, W_D2V, "b_d2v", fused, (1,), 0, peak=peak)
            project("ti", fused, P, W_IMG, "b_img", img, (2, 3), KD * B, peak=peak,
                    sums=[mean_img[:, m, b:b + 1] for b in range(B) for m in range(KD)])
            quantise_block(c, "tkq", [(cut(img[:, k, :], b), cut(qb[:, k, :], b))
                                      for k in range(2) for b in range(B)], scale, W_ATT0, scratch,
                           combine, (4, 5), KD * B)
            product_block(c, "tk0", [([(tern[W_ATT0][:, k, :], cut(qb[:, k, :], b)) for k in range(2)],
                                      cut(keys_f[:, 0, :], b), c.col("b_att0")) for b in range(B)], out_scale)
            scale1 = c.sem("t_scale1")
            with nc.Block() as block:
                @block.vector
                def _(dve):
                    nc.vector.tensor_tensor(out_scale[:, 0:1], step[:, 0:1], scale[:, W_ATT1:W_ATT1 + 1],
                                            ALU.mult).then_inc(scale1, 1)
                    nc.vector.tensor_scalar(mean_img[:, :, :], mean_img[:, :, :], 1.0 / T, None,
                                            ALU.mult).then_inc(mean_sem, 1)
            product_block(c, "tk1", [([(tern[W_ATT1][:, k, :], cut(qb[:, k, :], b)) for k in range(2)],
                                      cut(keys_f[:, 1, :], b), c.col("b_att1")) for b in range(B)], out_scale,
                          peak=peak, peak_of=[c.xn_f[:, k, :] for k in range(KD)])
            with nc.Block() as block:
                @block.tensor
                def _(pe):
                    for j in range(2 * B):
                        r, b = divmod(j, B)
                        for i in range(TB):
                            tr = nc.tensor.transpose(c.bank[:, j, i * P:(i + 1) * P],
                                                     keys_f[:, r, b * T + i * P:b * T + (i + 1) * P],
                                                     c.ident[:, :])
                        tr.then_inc(turned, 1)

                @block.scalar
                def _(act):
                    for j in range(2 * B):
                        r, b = divmod(j, B)
                        act.wait_ge(turned, j + 1)
                        nc.scalar.activation(keys_t[:, r, TB * b:TB * b + TB, :],
                                             c.bank[:, j, :].rearrange("p (i d) -> p i d", i=TB),
                                             ACT.Copy).then_inc(turned_out, 1)
            project("tt", c.xn_f, P, W_TXT, "b_txt", fused, (6, 7), KD)

        with ExitStack() as ctx2:
            qsum = c.sb(ctx2, "t_qsum", [P, 2, T])
            mx = c.sb(ctx2, "t_mx", [P, 2 * NT])
            neg = c.sb(ctx2, "t_neg", [P, 2 * NT])
            ex = c.sb(ctx2, "t_ex", [P, 4, T])
            rsum = c.sb(ctx2, "t_rsum", [P, 2 * NT])
            rinv = c.sb(ctx2, "t_rinv", [P, 2 * NT])
            probs = c.sb(ctx2, "t_probs", [P, 2, T])
            probs_f = c.sb(ctx2, "t_probs_f", [P, 2, TB, T])
            qsum_sem = c.sem("t_qsum_ready")
            score_ps = c.sem("t_score_ps")
            max_sem = c.sem("t_max")
            neg_sem = c.sem("t_neg_ready")
            exp_sem = c.sem("t_exp")
            inv_sem = c.sem("t_rinv_ready")
            prob_sem = c.sem("t_prob")
            turn_ps = c.sem("t_turn_ps")
            turn_out = c.sem("t_turn_out")
            att_ps = c.sem("t_att_ps")
            add_sem = c.sem("t_add")
            peaked = c.sem("t_peaked")
            inv_sqrt = 1.0 / float(np.sqrt(D))
            AHEAD = 3
            with nc.Block() as block:
                @block.tensor
                def _(pe):
                    def score(u):
                        r, b, i = u // NT, (u // TB) % B, u % TB
                        g = u // TB
                        pe.wait_ge(qsum_sem, g + 1)
                        if u >= 4:
                            pe.wait_ge(exp_sem, u - 3)
                        nc.tensor.matmul(c.bank[:, u % 4, :], qsum[:, g % 2, i * P:(i + 1) * P],
                                         cut(keys_f[:, r, :], b), start=True, stop=True).then_inc(score_ps, 1)

                    def turn(u):
                        pe.wait_ge(prob_sem, u + 1)
                        if u >= 2:
                            pe.wait_ge(turn_out, u - 1)
                        for k in range(TB):
                            tr = nc.tensor.transpose(c.bank[:, 4 + u % 2, k * P:(k + 1) * P],
                                                     probs[:, u % 2, k * P:(k + 1) * P], c.ident[:, :])
                        tr.then_inc(turn_ps, 1)

                    def apply(g, k):
                        r, b = divmod(g, B)
                        if k == 0:
                            pe.wait_ge(turn_out, TB * (g + 1))
                            if g >= 2:
                                pe.wait_ge(add_sem, KD * (g - 1))
                        mm = nc.tensor.matmul(c.bank[:, 6 + g % 2, :], keys_t[:, r, TB * b + k, :],
                                              probs_f[:, g % 2, k, :], start=(k == 0), stop=(k == TB - 1))
                        if k == TB - 1:
                            mm.then_inc(att_ps, 1)

                    for u in range(AHEAD):
                        score(u)
                    for u in range(2 * NT + TB):
                        if u + AHEAD < 2 * NT:
                            score(u + AHEAD)
                        if u < 2 * NT:
                            turn(u)
                        if u >= TB:
                            apply(u // TB - 1, u % TB)

                @block.vector
                def _(dve):
                    def sum_q(g):
                        r, b = divmod(g, B)
                        if g >= 2:
                            dve.wait_ge(score_ps, TB * (g - 1))
                        if r:
                            dve.wait_ge(add_sem, KD * (b + 1))
                        nc.vector.tensor_tensor(qsum[:, g % 2, :], cut(fused[:, 0, :], b), cut(fused[:, 1, :], b),
                                                ALU.add).then_inc(qsum_sem, 1)

                    def top_of(u):
                        dve.wait_ge(score_ps, u + 1)
                        nc.vector.tensor_reduce(mx[:, u:u + 1], c.bank[:, u % 4, :], AX.X,
                                                ALU.max).then_inc(max_sem, 1)
                        dve.wait_ge(max_sem, u + 1)
                        nc.vector.tensor_scalar(neg[:, u:u + 1], mx[:, u:u + 1], -inv_sqrt, None,
                                                ALU.mult).then_inc(neg_sem, 1)

                    def divide(u):
                        dve.wait_ge(exp_sem, u + 1)
                        nc.vector.reciprocal(rinv[:, u:u + 1], rsum[:, u:u + 1]).then_inc(inv_sem, 1)
                        dve.wait_ge(inv_sem, u + 1)
                        if u >= 2:
                            dve.wait_ge(turn_ps, u - 1)
                        nc.vector.tensor_scalar(probs[:, u % 2, :], ex[:, u % 4, :], rinv[:, u:u + 1], 0.1,
                                                ALU.mult, ALU.mult).then_inc(prob_sem, 1)

                    def add(g):
                        r, b = divmod(g, B)
                        dve.wait_ge(att_ps, g + 1)
                        for k in range(KD):
                            nc.vector.tensor_tensor(cut(fused[:, k, :], b), cut(fused[:, k, :], b),
                                                    c.bank[:, 6 + g % 2, :], ALU.add).then_inc(add_sem, 1)
                        if r == 1:
                            for k in range(KD):
                                dve.wait_ge(add_sem, KD * g + k + 1)
                                nc.vector.tensor_reduce(peak[:, KD * b + k:KD * b + k + 1], cut(fused[:, k, :], b),
                                                        AX.X, ALU.max, apply_absolute_value=True
                                                        ).then_inc(peaked, 1)

                    sum_q(0)
                    nc.vector.tensor_reduce(peak[:, KD * B:KD * B + 1], mean_img[:, :, :], AX.XY, ALU.max,
                                            apply_absolute_value=True).then_inc(peaked, 1)
                    for u in range(AHEAD):
                        top_of(u)
                    for u in range(2 * NT):
                        g = u // TB
                        if u % TB == 0 and g + 1 < 2 * B:
                            sum_q(g + 1)
                        divide(u)
                        if u + AHEAD < 2 * NT:
                            top_of(u + AHEAD)
                        if u % TB == 0 and g >= 2:
                            add(g - 2)
                    add(2 * B - 2)
                    add(2 * B - 1)

                @block.scalar
                def _(act):
                    def weigh(u):
                        act.wait_ge(neg_sem, u + 1)
                        if u >= 4:
                            act.wait_ge(prob_sem, u - 3)
                        nc.scalar.activation(ex[:, u % 4, :], c.bank[:, u % 4, :], ACT.Exp, bias=neg[:, u:u + 1],
                                             scale=inv_sqrt, accum_out=rsum[:, u:u + 1]).then_inc(exp_sem, 1)

                    def store(u):
                        g, i = divmod(u, TB)
                        act.wait_ge(turn_ps, u + 1)
                        if g >= 2:
                            act.wait_ge(att_ps, g - 1)
                        nc.scalar.activation(probs_f[:, g % 2, :, i * P:(i + 1) * P],
                                             c.bank[:, 4 + u % 2, :].rearrange("p (k q) -> p k q", k=TB),
                                             ACT.Copy).then_inc(turn_out, 1)

                    for u in range(2 * NT + AHEAD):
                        if u < 2 * NT:
                            weigh(u)
                        if u >= AHEAD:
                            store(u - AHEAD)

        keys_ctx.close()
        combine_ctx.close()
        with ExitStack() as ctx2:
            hid = c.sb(ctx2, "t_hid", [P, FX // P, N])
            qh = c.sb(ctx2, "t_qh", [P, FX // P, N], BF16)
            qf = c.xn[:, :, :].bitcast(BF16).rearrange("p t d -> p (t d)")[:, 0:KD * N].rearrange(
                "p (k n) -> p k n", k=KD)
            qm = c.sb(ctx2, "t_qm", [P, KD * B], BF16)
            mb = c.sb(ctx2, "t_mb", [P, FX // P, B])
            MF = FX // P
            quantise_block(c, "tfq", [(cut(fused[:, k, :], b), cut(qf[:, k, :], b))
                                      for k in range(KD) for b in range(B)]
                           + [(mean_img[:, :, :].rearrange("p k b -> p (k b)"), qm[:, :])], scale, W_F1, scratch,
                           peaks=KD * B + 1)
            mean_ps = c.sem("t_mean_ps")
            mean_bias = c.sem("t_mean_bias")
            with nc.Block() as block:
                @block.tensor
                def _(pe):
                    for m in range(MF):
                        for k in range(KD):
                            mm = nc.tensor.matmul(c.bank[:, m, 0:B], tern[W_F1][:, KD + k, m * P:(m + 1) * P],
                                                  qm[:, k * B:(k + 1) * B], start=(k == 0), stop=(k == KD - 1))
                        mm.then_inc(mean_ps, 1)

                @block.scalar
                def _(act):
                    for m in range(MF):
                        act.wait_ge(mean_ps, m + 1)
                        nc.scalar.activation(mb[:, m, :], c.bank[:, m, 0:B], ACT.Identity, bias=c.col("b_f1", m),
                                             scale=out_scale[:, 0:1]).then_inc(mean_bias, 1)

            product_block(c, "tf1", [([(tern[W_F1][:, k, m * P:(m + 1) * P], cut(qf[:, k, :], b))
                                       for k in range(KD)], cut(hid[:, m, :], b), mb[:, m, b:b + 1])
                                     for b in range(B) for m in range(MF)], out_scale, ACT.Relu, peak=peak)
            quantise_block(c, "thq", [(hid[:, m, :], qh[:, m, :]) for m in range(MF)], scale, W_F2, scratch,
                           peaks=B * MF)
            out_ps = c.sem("t_out_ps")
            off_sem = c.sem("t_offset")
            added = c.sem("t_added")
            with nc.Block() as block:
                @block.tensor
                def _(pe):
                    for t in range(NT):
                        if t >= 8:
                            pe.wait_ge(added, t - 7)
                        for m in range(MF):
                            mm = nc.tensor.matmul(c.bank[:, t % 8, 0:D], qh[:, m, t * P:(t + 1) * P],
                                                  tern[W_F2][:, m, :], start=(m == 0), stop=(m == MF - 1))
                        mm.then_inc(out_ps, 1)

                @block.gpsimd
                def _(pool):
                    for t in range(NT):
                        nc.gpsimd.tensor_tensor(c.X[:, t, :], c.X[:, t, :], c.row("b_f2"),
                                                ALU.add).then_inc(off_sem, 1)

                @block.vector
                def _(dve):
                    for t in range(NT):
                        dve.wait_ge(out_ps, t + 1)
                        dve.wait_ge(off_sem, t + 1)
                        nc.vector.scalar_tensor_tensor(out=c.X[:, t, :], in0=c.bank[:, t % 8, 0:D],
                                                       scalar=out_scale[:, 0:1], in1=c.X[:, t, :],
                                                       op0=ALU.mult, op1=ALU.add).then_inc(added, 1)


def linear_experts_blocks(c):
    nc, dram = c.nc, c.dram
    with ExitStack() as ctx:
        wg = c.sb(ctx, "r1_wg", [P, KD, NE])
        gates = c.sb(ctx, "r1_gates", [P, NT, NE])
        xs = [c.sb(ctx, f"e1_x{i}", [P, KD, N], F32R) for i in range(2)]
        wg_in = c.sem("e1_wg_in")
        comb = [c.sb(ctx, f"e1_comb{i}", [P, KD, NE, D], F32R) for i in range(2)]
        comb_high = c.sem("e1_comb_high")
        comb_low = c.sem("e1_comb_low")
        out_ps = c.sem("e1_out_ps")
        added = c.sem("e1_added")
        NP = NE // 2

        def load_ahead(sp):
            sp.dma_start(wg[:, :, :], dram["e1_gate"]).then_inc(wg_in, 16)

        def round_comb(act):
            for p in range(NP):
                pair = slice(2 * p, 2 * p + 2)
                nc.scalar.activation(comb[0][:, :, pair, :], c.comb[:, :, pair, :], ACT.Copy).then_inc(comb_high, 1)

        def split_comb(pool):
            for p in range(NP):
                pair = slice(2 * p, 2 * p + 2)
                pool.wait_ge(comb_high, p + 1)
                if p:
                    pool.wait_ge(comb_low, p)
                nc.gpsimd.tensor_tensor(comb[1][:, :, pair, :], c.comb[:, :, pair, :],
                                        comb[0][:, :, pair, :].bitcast(F32), ALU.subtract).then_inc(comb_low, 1)

        norm_block(c, "n5", load_ahead=load_ahead)
        route_block(c, "r1", NE, wg, wg_in, False, gates, xs, split_comb, round_comb)
        with nc.Block() as block:
            @block.sync
            def _(sp):
                for t in range(NT):
                    sp.wait_ge(added, NE * (t + 1))
                    sp.dma_start(dram["out"][t * P:(t + 1) * P, :], c.X[:, t, :]).then_inc(c.saved, 16)
                sp.wait_ge(c.saved, 16 * NT)

            @block.tensor
            def _(pe):
                for t in range(NT):
                    for p in range(NP):
                        n = NP * t + p
                        if n >= 8:
                            pe.wait_ge(added, 2 * (n - 7))
                        for k in range(KD):
                            for i, (xi, wi) in enumerate(TERMS):
                                mm = nc.tensor.matmul(c.bank[:, n % 8, :], xs[xi][:, k, t * P:(t + 1) * P],
                                                      comb[wi][:, k, 2 * p:2 * p + 2, :],
                                                      start=(k == 0 and i == 0), stop=(k == KD - 1 and i == 2))
                        mm.then_inc(out_ps, 1)

            @block.vector
            def _(dve):
                for t in range(NT):
                    for e in range(NE):
                        n = NP * t + e // 2
                        dve.wait_ge(out_ps, n + 1)
                        if e:
                            dve.wait_ge(added, NE * t + e)
                        nc.vector.scalar_tensor_tensor(out=c.X[:, t, :],
                                                       in0=c.bank[:, n % 8, (e % 2) * D:(e % 2) * D + D],
                                                       scalar=gates[:, t, e:e + 1], in1=c.X[:, t, :],
                                                       op0=ALU.mult, op1=ALU.add).then_inc(added, 1)


def decoder_kernel(nc, dram):
    with ExitStack() as ctx:
        c = Core(nc, ctx, dram)
        load_block(c)
        attention_blocks(c)
        c.end_section()
        cross_attention_blocks(c)
        c.end_section()
        experts_blocks(c)
        c.end_section()
        gru_blocks(c)
        c.end_section()
        c.comb = c.sb(ctx, "comb", [P, KD, NE, D])
        ternary_cross_blocks(c)
        c.end_section()
        linear_experts_blocks(c)


def _tiles(w, p=P):
    return w.reshape(w.shape[0] // p, p, *w.shape[1:]).swapaxes(0, 1)


def _layout(i):
    a = {k: np.asarray(v) for k, v in i.items()}
    f = np.float32
    cols = np.zeros((P, N_COLS), f)

    def put(name, v):
        lo, hi = COLS[name]
        cols[:v.shape[0], lo:hi] = v

    put("conv_w", a["L0_attn_conv_w"].reshape(KD, P, 4).swapaxes(0, 1).reshape(P, KD * 4))
    for name, key in (("conv_b", "L0_attn_conv_b"), ("g_b", "L0_attn_g_b"), ("bq", "L0_xattn_bq"),
                      ("bk", "L0_xattn_bk"), ("bv", "L0_xattn_bv"), ("b_f", "L1_attn_b_f"),
                      ("b_d2v", "L1_xattn_b_d2v"), ("b_img", "L1_xattn_b_img"), ("b_txt", "L1_xattn_b_txt"),
                      ("b_att0", "L1_xattn_b_att0"), ("b_att1", "L1_xattn_b_att1"), ("b_f1", "L1_xattn_b_f1")):
        put(name, a[key].reshape(-1, P).T)
    put("freqs", a["L0_attn_freqs"].reshape(-1, P).T)
    put("gamma", a["L0_attn_gamma"].reshape(H0, 1))
    rows = np.zeros((P, N_ROWS), f)
    for name, v in (("ln_g", a["L0_attn_ln_g"]), ("ln_b", a["L0_attn_ln_b"]), ("bo", a["L0_xattn_bo"]),
                    ("b_f2", a["L1_xattn_b_f2"]), ("expert_bias", a["L0_ffn_expert_bias"]),
                    ("steps", np.arange(T, dtype=f)), ("expert_index", np.arange(NE_ALL, dtype=f))):
        lo, hi = ROWS[name]
        rows[:, lo:hi] = np.broadcast_to(v, (P, hi - lo))
    head_in = np.zeros((P, ET, 32), f)
    head_out = np.zeros((P, ET, P), f)
    per = E0 // H0
    for e in range(ET):
        for p in range(P):
            h = (e * P + p) // per
            head_in[p, e, h] = 1.0
            for g in range(P // 32):
                head_out[32 * g + h, e, p] = 1.0
    return {
        "x": a["x"].reshape(N, D),
        "columns": cols,
        "rows": rows,
        "ident": np.eye(P, dtype=f),
        "head_in": head_in,
        "head_out": head_out,
        "a0_wq": _tiles(a["L0_attn_qk_w"].T),
        "a0_wv": _tiles(a["L0_attn_v_w"].T),
        "a0_wg": _tiles(a["L0_attn_g_w"].T),
        "a0_wo": _tiles(a["L0_attn_o_w"].T),
        "ctx_f": _tiles(a["ctx_768"].reshape(N, CTX).T, CK),
        "x_wq": _tiles(a["L0_xattn_Wq"]),
        "x_wk": _tiles(a["L0_xattn_Wk"], CK),
        "x_wv": _tiles(a["L0_xattn_Wv"], CK),
        "x_wo": _tiles(a["L0_xattn_Wo"]),
        "e0_gate": _tiles(a["L0_ffn_gate_w"].T),
        "e0_w1": np.stack([_tiles(w.T) for w in a["L0_ffn_w1"]]),
        "e0_w2": np.stack([_tiles(w.T) for w in a["L0_ffn_w2"]]),
        "g_wf": _tiles(a["L1_attn_W_f"].T),
        "g_wd": _tiles(a["L1_attn_W_down"].T),
        "t_d2v": _tiles(a["L1_xattn_W_d2v"].T, CK),
        "t_img": _tiles(a["L1_xattn_W_img"].T),
        "t_txt": _tiles(a["L1_xattn_W_txt"].T),
        "t_att0": _tiles(a["L1_xattn_W_att0"].T),
        "t_att1": _tiles(a["L1_xattn_W_att1"].T),
        "t_f1": _tiles(a["L1_xattn_W_f1"].T),
        "t_f2": _tiles(a["L1_xattn_W_f2"].T),
        "e1_gate": _tiles(a["L1_ffn_w_gate"].T),
        "e1_w_in": np.stack([_tiles(w) for w in a["L1_ffn_w_in"]]),
        "e1_w_out": np.stack([_tiles(w.T) for w in a["L1_ffn_w_out"]]),
    }


def kernel(**inputs):
    import concourse.bacc as _bacc
    from concourse.bass_utils import run_bass_kernel_spmd as _run

    nc = _bacc.Bacc("TRN2", target_bir_lowering=False, num_devices=1)
    arrays, dram = {}, {}
    for name, v in _layout(inputs).items():
        v = np.ascontiguousarray(v)
        arrays[f"in_{name}_dram"] = v
        dram[name] = nc.dram_tensor(f"in_{name}_dram", v.shape, mybir.dt.from_np(v.dtype), kind="ExternalInput").ap()
    dram["out"] = nc.dram_tensor("out_dram", (N, D), F32, kind="ExternalOutput").ap()
    dram["split"] = nc.dram_tensor("split_scratch", (2, 3, D, N), BF16, kind="Internal").ap()
    dram["negmax"] = nc.dram_tensor("negmax_scratch", (B, 3, HX * TB, P), BF16, kind="Internal").ap()
    decoder_kernel(nc, dram)
    r = _run(nc, [arrays], core_ids=[0])
    return r.results[0]["out_dram"].reshape(B, T, D)
```
